# Optimizing a Trainium2 kernel written in Bass

```python
import numpy as np
import jax
import jax.numpy as jnp

def _softmax(x, axis=-1):
    return jax.nn.softmax(x, axis=axis)

def _gelu(x):
    return jax.nn.gelu(x, approximate=True)

def _silu(x):
    return jax.nn.silu(x)

def _sigmoid(x):
    return jax.nn.sigmoid(x)

def _layernorm(x, axis=-1, eps=1e-05):
    m = jnp.mean(x, axis=axis, keepdims=True)
    v = jnp.var(x, axis=axis, keepdims=True)
    return (x - m) / jnp.sqrt(v + eps)

def _scatter_add(tgt, idx, src, axis=0):
    return tgt.at[idx].add(src)

def _segment_sum(src, seg, n):
    return jax.ops.segment_sum(src, seg, n)
kernel_name = 'mk_adj_resnorm_d4_adj_r2_2b3fbe'

def setup_inputs(seed: int=0):
    np.random.seed(seed)
    _w = jnp.asarray

    def _rec_inputs():
        import jax
        import jax.numpy as jnp
        _gk = jax.random.key(seed)
        x = -0.000929 + 1 * jax.random.normal(jax.random.fold_in(_gk, 1), (2048, 128), jnp.float32)
        _a = jax.random.bernoulli(jax.random.fold_in(_gk, 2), 0.000976562, (2048, 2048))
        _a = jnp.logical_or(_a, jnp.eye(2048, dtype=bool))
        _af = _a.astype(jnp.float32)
        _af = _af * jax.random.uniform(jax.random.fold_in(_gk, 3), (2048, 2048), jnp.float32, 0.05, 1)
        adj = _af
        return (x, adj)
    x, adj = _rec_inputs()

    def _L0_gnn_setup():
        import jax, jax.numpy as jnp
        import numpy as np
        N, H, HEADS = (2048, 128, 3)
        ALPHA = 0.2
        NEG_INF = -9000000000000000.0

        def _sign_adj(key, n, density):
            k1, k2 = jax.random.split(key)
            mask = jax.random.uniform(k1, (n, n)) < density
            sign = jnp.where(jax.random.uniform(k2, (n, n)) < 0.5, -1.0, 1.0)
            adj = jnp.where(mask, sign, 0.0).astype(jnp.float32)
            idx = jnp.arange(n)
            return adj.at[idx, idx].set(1.0)

        def _gru_cell(x, hstate, Wih, Whh, bih, bhh):
            gi = x @ Wih.T + bih
            gh = hstate @ Whh.T + bhh
            ir, iz, inn = jnp.split(gi, 3, axis=1)
            hr, hz, hn = jnp.split(gh, 3, axis=1)
            r = jax.nn.sigmoid(ir + hr)
            z = jax.nn.sigmoid(iz + hz)
            n = jnp.tanh(inn + r * hn)
            return (1.0 - z) * n + z * hstate

        def _gat_head(h, node_adj, edge_adj, W, a):
            hW = h @ W
            hp = (node_adj > 0).astype(hW.dtype) @ hW
            hm = (node_adj < 0).astype(hW.dtype) @ hW
            e_plus = jax.nn.leaky_relu(jnp.concatenate([hp, hm], axis=1) @ a, ALPHA)[:, 0]
            e_minus = jax.nn.leaky_relu(jnp.concatenate([hm, hp], axis=1) @ a, ALPHA)[:, 0]
            att = jnp.where(edge_adj > 0, e_plus[None, :], NEG_INF)
            att = jnp.where(edge_adj < 0, e_minus[None, :], att)
            att = jax.nn.softmax(att, axis=1)
            return att * edge_adj @ hW
        key = jax.random.key(seed)
        ks = jax.random.split(key, 16)
        std = 0.01
        gain = 1.414
        return {'h': jax.random.normal(ks[0], (N, H), jnp.float32), 'node_adj': _sign_adj(ks[1], N, 0.005), 'edge_adj': _sign_adj(ks[2], N, 0.005), 'gat_W': jax.random.normal(ks[3], (HEADS, H, H), jnp.float32) * (gain / np.sqrt(H, dtype=np.float32)), 'gat_a': jax.random.normal(ks[4], (HEADS, 2 * H, 1), jnp.float32) * 0.1, 'edge_Wih': jax.random.normal(ks[5], (3 * H, H), jnp.float32) * std, 'edge_Whh': jax.random.normal(ks[6], (3 * H, H), jnp.float32) * std, 'edge_bih': jnp.zeros((3 * H,), jnp.float32), 'edge_bhh': jnp.zeros((3 * H,), jnp.float32), 'node_Wih': jax.random.normal(ks[7], (3 * H, H), jnp.float32) * std, 'node_Whh': jax.random.normal(ks[8], (3 * H, H), jnp.float32) * std, 'node_bih': jnp.zeros((3 * H,), jnp.float32), 'node_bhh': jnp.zeros((3 * H,), jnp.float32)}
    _L0_gnn_all = _L0_gnn_setup()
    _L0_gnn_in = {k: v for k, v in _L0_gnn_all.items() if k in ('gat_W', 'gat_a', 'edge_Wih', 'edge_Whh', 'edge_bih', 'edge_bhh', 'node_Wih', 'node_Whh', 'node_bih', 'node_bhh')}
    del _L0_gnn_all

    def _L1_gnn_setup():
        import jax, jax.numpy as jnp
        import numpy as np
        N, F, OUT = (4096, 128, 128)
        key = jax.random.key(seed)
        k1, k2, k3, k4 = jax.random.split(key, 4)
        features = jax.random.normal(k1, (N, F), dtype=jnp.float32)
        adj = jax.random.uniform(k2, (N, N), dtype=jnp.float32)
        gain = float(np.sqrt(2.0))
        b_n = gain * np.sqrt(6.0 / (F + F))
        neigh_W = jax.random.uniform(k3, (F, F), dtype=jnp.float32, minval=-b_n, maxval=b_n)
        b_l = gain * np.sqrt(6.0 / (2 * F + OUT))
        lin_W = jax.random.uniform(k4, (OUT, 2 * F), dtype=jnp.float32, minval=-b_l, maxval=b_l)
        return {'features': features, 'adj': adj, 'neigh_W': neigh_W, 'lin_W': lin_W}
    _L1_gnn_all = _L1_gnn_setup()
    _L1_gnn_in = {k: v for k, v in _L1_gnn_all.items() if k in ('neigh_W', 'lin_W')}
    del _L1_gnn_all

    def _L2_gnn_setup():
        import jax, jax.numpy as jnp
        import numpy as np
        N = 4096
        DIN = 128
        DOUT = 128
        EDGE_P = 0.004
        key = jax.random.key(seed)
        k1, k2, k3, k4, k5 = jax.random.split(key, 5)
        h = jax.random.normal(k1, (N, DIN), dtype=jnp.float32)
        adj = (jax.random.uniform(k2, (N, N)) < EDGE_P).astype(jnp.float32)
        xav_w = float(np.sqrt(6.0 / (DIN + DOUT)))
        weight = jax.random.uniform(k3, (DIN, DOUT), minval=-xav_w, maxval=xav_w, dtype=jnp.float32)
        xav_a = float(np.sqrt(6.0 / (DOUT + 1)))
        a_l = jax.random.uniform(k4, (DOUT,), minval=-xav_a, maxval=xav_a, dtype=jnp.float32)
        a_r = jax.random.uniform(k5, (DOUT,), minval=-xav_a, maxval=xav_a, dtype=jnp.float32)
        b = jnp.zeros((DOUT,), dtype=jnp.float32)
        return {'h': h, 'adj': adj, 'weight': weight, 'a_l': a_l, 'a_r': a_r, 'b': b}
    _L2_gnn_all = _L2_gnn_setup()
    _L2_gnn_in = {k: v for k, v in _L2_gnn_all.items() if k in ('weight', 'a_l', 'a_r', 'b')}
    del _L2_gnn_all

    def _L3_gnn_setup():
        import jax, jax.numpy as jnp
        import numpy as np
        from jax import lax
        D_MODEL = 128
        D_STATE = 16
        D_CONV = 4
        EXPAND = 2
        D_INNER = EXPAND * D_MODEL
        DT_RANK = (D_MODEL + 15) // 16
        N = 2048
        EPS = 1e-05

        def _mamba(h, w_in, conv_w, conv_b, w_xp, w_dt, b_dt, A_log, D_skip, w_out):
            L = h.shape[0]
            xz = h @ w_in
            xc, z = (xz[:, :D_INNER], xz[:, D_INNER:])
            xpad = jnp.pad(xc, ((D_CONV - 1, 0), (0, 0)))
            xconv = sum((xpad[k:k + L] * conv_w[:, k] for k in range(D_CONV))) + conv_b
            u = jax.nn.silu(xconv)
            dbc = u @ w_xp
            dt = jax.nn.softplus(dbc[:, :DT_RANK] @ w_dt + b_dt)
            B = dbc[:, DT_RANK:DT_RANK + D_STATE]
            C = dbc[:, DT_RANK + D_STATE:]
            A = -jnp.exp(A_log)
            dA = jnp.exp(dt[:, :, None] * A[None])
            dBu = dt[:, :, None] * B[:, None, :] * u[:, :, None]

            def step(hst, inp):
                dAt, dBut, Ct = inp
                hst = dAt * hst + dBut
                return (hst, hst @ Ct)
            _, ys = lax.scan(step, jnp.zeros((D_INNER, D_STATE), h.dtype), (dA, dBu, C))
            y = ys + u * D_skip
            y = y * jax.nn.silu(z)
            return y @ w_out
        key = jax.random.key(seed)
        ks = jax.random.split(key, 16)
        x = jax.random.normal(ks[0], (N, D_MODEL), dtype=jnp.float32)
        a = jax.random.uniform(ks[1], (N, N), dtype=jnp.float32)
        adj = a / a.sum(axis=1, keepdims=True)
        s = lambda fi, fo: 1.0 / np.sqrt(fi)
        gcn_w = jax.random.uniform(ks[2], (D_MODEL, D_MODEL), jnp.float32, -s(D_MODEL, 0), s(D_MODEL, 0))
        gcn_b = jnp.zeros((D_MODEL,), jnp.float32)
        ln_g = jnp.ones((D_MODEL,), jnp.float32)
        ln_b = jnp.zeros((D_MODEL,), jnp.float32)
        w_in = jax.random.normal(ks[3], (D_MODEL, 2 * D_INNER), jnp.float32) * s(D_MODEL, 0)
        conv_w = jax.random.normal(ks[4], (D_INNER, D_CONV), jnp.float32) * s(D_CONV, 0)
        conv_b = jnp.zeros((D_INNER,), jnp.float32)
        w_xp = jax.random.normal(ks[5], (D_INNER, DT_RANK + 2 * D_STATE), jnp.float32) * s(D_INNER, 0)
        w_dt = jax.random.normal(ks[6], (DT_RANK, D_INNER), jnp.float32) * s(DT_RANK, 0)
        b_dt = jnp.log(jnp.expm1(jnp.exp(jax.random.uniform(ks[7], (D_INNER,), jnp.float32, np.log(0.001), np.log(0.1)))))
        A_log = jnp.log(jnp.broadcast_to(jnp.arange(1, D_STATE + 1, dtype=jnp.float32), (D_INNER, D_STATE)))
        D_skip = jnp.ones((D_INNER,), jnp.float32)
        w_out = jax.random.normal(ks[8], (D_INNER, D_MODEL), jnp.float32) * s(D_INNER, 0)
        return dict(x=x, adj=adj, gcn_w=gcn_w, gcn_b=gcn_b, ln_g=ln_g, ln_b=ln_b, w_in=w_in, conv_w=conv_w, conv_b=conv_b, w_xp=w_xp, w_dt=w_dt, b_dt=b_dt, A_log=A_log, D_skip=D_skip, w_out=w_out)
    _L3_gnn_all = _L3_gnn_setup()
    _L3_gnn_in = {k: v for k, v in _L3_gnn_all.items() if k in ('gcn_w', 'gcn_b', 'ln_g', 'ln_b', 'w_in', 'conv_w', 'conv_b', 'w_xp', 'w_dt', 'b_dt', 'A_log', 'D_skip', 'w_out')}
    del _L3_gnn_all
    return {'x': x, 'adj': adj, 'L0_gnn_gat_W': _L0_gnn_in['gat_W'], 'L0_gnn_gat_a': _L0_gnn_in['gat_a'], 'L0_gnn_edge_Wih': _L0_gnn_in['edge_Wih'], 'L0_gnn_edge_Whh': _L0_gnn_in['edge_Whh'], 'L0_gnn_edge_bih': _L0_gnn_in['edge_bih'], 'L0_gnn_edge_bhh': _L0_gnn_in['edge_bhh'], 'L0_gnn_node_Wih': _L0_gnn_in['node_Wih'], 'L0_gnn_node_Whh': _L0_gnn_in['node_Whh'], 'L0_gnn_node_bih': _L0_gnn_in['node_bih'], 'L0_gnn_node_bhh': _L0_gnn_in['node_bhh'], 'L1_gnn_neigh_W': _L1_gnn_in['neigh_W'], 'L1_gnn_lin_W': _L1_gnn_in['lin_W'], 'L2_gnn_weight': _L2_gnn_in['weight'], 'L2_gnn_a_l': _L2_gnn_in['a_l'], 'L2_gnn_a_r': _L2_gnn_in['a_r'], 'L2_gnn_b': _L2_gnn_in['b'], 'L3_gnn_gcn_w': _L3_gnn_in['gcn_w'], 'L3_gnn_gcn_b': _L3_gnn_in['gcn_b'], 'L3_gnn_ln_g': _L3_gnn_in['ln_g'], 'L3_gnn_ln_b': _L3_gnn_in['ln_b'], 'L3_gnn_w_in': _L3_gnn_in['w_in'], 'L3_gnn_conv_w': _L3_gnn_in['conv_w'], 'L3_gnn_conv_b': _L3_gnn_in['conv_b'], 'L3_gnn_w_xp': _L3_gnn_in['w_xp'], 'L3_gnn_w_dt': _L3_gnn_in['w_dt'], 'L3_gnn_b_dt': _L3_gnn_in['b_dt'], 'L3_gnn_A_log': _L3_gnn_in['A_log'], 'L3_gnn_D_skip': _L3_gnn_in['D_skip'], 'L3_gnn_w_out': _L3_gnn_in['w_out']}

def reference(x, adj, L0_gnn_gat_W, L0_gnn_gat_a, L0_gnn_edge_Wih, L0_gnn_edge_Whh, L0_gnn_edge_bih, L0_gnn_edge_bhh, L0_gnn_node_Wih, L0_gnn_node_Whh, L0_gnn_node_bih, L0_gnn_node_bhh, L1_gnn_neigh_W, L1_gnn_lin_W, L2_gnn_weight, L2_gnn_a_l, L2_gnn_a_r, L2_gnn_b, L3_gnn_gcn_w, L3_gnn_gcn_b, L3_gnn_ln_g, L3_gnn_ln_b, L3_gnn_w_in, L3_gnn_conv_w, L3_gnn_conv_b, L3_gnn_w_xp, L3_gnn_w_dt, L3_gnn_b_dt, L3_gnn_A_log, L3_gnn_D_skip, L3_gnn_w_out):
    import jax
    import jax.numpy as jnp

    def _L0_gnn_ref(h, node_adj, edge_adj, gat_W, gat_a, edge_Wih, edge_Whh, edge_bih, edge_bhh, node_Wih, node_Whh, node_bih, node_bhh):
        import jax, jax.numpy as jnp
        import numpy as np
        N, H, HEADS = (2048, 128, 3)
        ALPHA = 0.2
        NEG_INF = -9000000000000000.0

        def _sign_adj(key, n, density):
            k1, k2 = jax.random.split(key)
            mask = jax.random.uniform(k1, (n, n)) < density
            sign = jnp.where(jax.random.uniform(k2, (n, n)) < 0.5, -1.0, 1.0)
            adj = jnp.where(mask, sign, 0.0).astype(jnp.float32)
            idx = jnp.arange(n)
            return adj.at[idx, idx].set(1.0)

        def _gru_cell(x, hstate, Wih, Whh, bih, bhh):
            gi = x @ Wih.T + bih
            gh = hstate @ Whh.T + bhh
            ir, iz, inn = jnp.split(gi, 3, axis=1)
            hr, hz, hn = jnp.split(gh, 3, axis=1)
            r = jax.nn.sigmoid(ir + hr)
            z = jax.nn.sigmoid(iz + hz)
            n = jnp.tanh(inn + r * hn)
            return (1.0 - z) * n + z * hstate

        def _gat_head(h, node_adj, edge_adj, W, a):
            hW = h @ W
            hp = (node_adj > 0).astype(hW.dtype) @ hW
            hm = (node_adj < 0).astype(hW.dtype) @ hW
            e_plus = jax.nn.leaky_relu(jnp.concatenate([hp, hm], axis=1) @ a, ALPHA)[:, 0]
            e_minus = jax.nn.leaky_relu(jnp.concatenate([hm, hp], axis=1) @ a, ALPHA)[:, 0]
            att = jnp.where(edge_adj > 0, e_plus[None, :], NEG_INF)
            att = jnp.where(edge_adj < 0, e_minus[None, :], att)
            att = jax.nn.softmax(att, axis=1)
            return att * edge_adj @ hW
        dn = jnp.diag(node_adj)
        de = jnp.diag(edge_adj)
        idx = jnp.arange(node_adj.shape[0])
        node_adj_norm = node_adj.at[idx, idx].add(-dn)
        edge_adj_norm = edge_adj.at[idx, idx].add(-de)
        node_support = node_adj_norm @ h
        edge_output = _gru_cell(node_support, h, edge_Wih, edge_Whh, edge_bih, edge_bhh)
        edge_support = _gat_head(h, node_adj_norm, edge_adj_norm, gat_W[0], gat_a[0])
        for i in range(1, HEADS):
            edge_support = edge_support + _gat_head(h, node_adj_norm, edge_adj_norm, gat_W[i], gat_a[i])
        edge_support = edge_support / HEADS
        node_output = _gru_cell(edge_support, h, node_Wih, node_Whh, node_bih, node_bhh)
        return de[:, None] * edge_output + dn[:, None] * node_output

    def _L1_gnn_ref(features, adj, neigh_W, lin_W):
        import jax, jax.numpy as jnp
        import numpy as np
        N, F, OUT = (4096, 128, 128)
        h = features @ neigh_W.T
        deg = adj.sum(axis=1, keepdims=True) + 1.0
        h = adj @ h / deg
        z = jnp.concatenate([features, h], axis=-1) @ lin_W.T
        return z

    def _L2_gnn_ref(h, adj, weight, a_l, a_r, b):
        import jax, jax.numpy as jnp
        import numpy as np
        N = 4096
        DIN = 128
        DOUT = 128
        EDGE_P = 0.004
        x = h @ weight
        el = x @ a_l
        er = x @ a_r
        mask = adj != 0
        scores = el[:, None] + er[None, :]
        attn = jnp.exp(jax.nn.leaky_relu(scores, negative_slope=0.2))
        attn = jnp.where(mask, attn, 0.0)
        denom = jnp.maximum(attn.sum(axis=-1, keepdims=True), 1e-12)
        A = attn / denom
        out = A @ x + b
        return out

    def _L3_gnn_ref(x, adj, gcn_w, gcn_b, ln_g, ln_b, w_in, conv_w, conv_b, w_xp, w_dt, b_dt, A_log, D_skip, w_out):
        import jax, jax.numpy as jnp
        import numpy as np
        from jax import lax
        D_MODEL = 128
        D_STATE = 16
        D_CONV = 4
        EXPAND = 2
        D_INNER = EXPAND * D_MODEL
        DT_RANK = (D_MODEL + 15) // 16
        N = 2048
        EPS = 1e-05

        def _mamba(h, w_in, conv_w, conv_b, w_xp, w_dt, b_dt, A_log, D_skip, w_out):
            L = h.shape[0]
            xz = h @ w_in
            xc, z = (xz[:, :D_INNER], xz[:, D_INNER:])
            xpad = jnp.pad(xc, ((D_CONV - 1, 0), (0, 0)))
            xconv = sum((xpad[k:k + L] * conv_w[:, k] for k in range(D_CONV))) + conv_b
            u = jax.nn.silu(xconv)
            dbc = u @ w_xp
            dt = jax.nn.softplus(dbc[:, :DT_RANK] @ w_dt + b_dt)
            B = dbc[:, DT_RANK:DT_RANK + D_STATE]
            C = dbc[:, DT_RANK + D_STATE:]
            A = -jnp.exp(A_log)
            dA = jnp.exp(dt[:, :, None] * A[None])
            dBu = dt[:, :, None] * B[:, None, :] * u[:, :, None]

            def step(hst, inp):
                dAt, dBut, Ct = inp
                hst = dAt * hst + dBut
                return (hst, hst @ Ct)
            _, ys = lax.scan(step, jnp.zeros((D_INNER, D_STATE), h.dtype), (dA, dBu, C))
            y = ys + u * D_skip
            y = y * jax.nn.silu(z)
            return y @ w_out
        h = jax.nn.relu(adj @ x @ gcn_w + gcn_b)
        mu = h.mean(-1, keepdims=True)
        var = h.var(-1, keepdims=True)
        h = (h - mu) * lax.rsqrt(var + EPS) * ln_g + ln_b
        return _mamba(h, w_in, conv_w, conv_b, w_xp, w_dt, b_dt, A_log, D_skip, w_out)
    x = _layernorm(x + _L0_gnn_ref(x, adj, adj, L0_gnn_gat_W, L0_gnn_gat_a, L0_gnn_edge_Wih, L0_gnn_edge_Whh, L0_gnn_edge_bih, L0_gnn_edge_bhh, L0_gnn_node_Wih, L0_gnn_node_Whh, L0_gnn_node_bih, L0_gnn_node_bhh), axis=-1)
    x = _layernorm(x + _L1_gnn_ref(x, adj, L1_gnn_neigh_W, L1_gnn_lin_W), axis=-1)
    x = _layernorm(x + _L2_gnn_ref(x, adj, L2_gnn_weight, L2_gnn_a_l, L2_gnn_a_r, L2_gnn_b), axis=-1)
    x = _layernorm(x + _L3_gnn_ref(x, adj, L3_gnn_gcn_w, L3_gnn_gcn_b, L3_gnn_ln_g, L3_gnn_ln_b, L3_gnn_w_in, L3_gnn_conv_w, L3_gnn_conv_b, L3_gnn_w_xp, L3_gnn_w_dt, L3_gnn_b_dt, L3_gnn_A_log, L3_gnn_D_skip, L3_gnn_w_out), axis=-1)
    return x

_drawn_inputs = setup_inputs


def setup_inputs(seed=0):
    import zlib

    import numpy as np

    out = dict(_drawn_inputs(seed))
    spreads = {'L0_gnn_edge_bih': (0.0, 0.1),
     'L0_gnn_edge_bhh': (0.0, 0.526),
     'L0_gnn_node_bih': (0.0, 0.292),
     'L0_gnn_node_bhh': (0.0, 0.463),
     'L2_gnn_b': (0.0, 0.1),
     'L3_gnn_gcn_b': (0.0, 0.1),
     'L3_gnn_ln_g': (1.0, 0.2),
     'L3_gnn_ln_b': (0.0, 0.1),
     'L3_gnn_conv_b': (0.0, 0.1),
     'L3_gnn_D_skip': (1.0, 0.2)}
    factors = {'L0_gnn_gat_W': 5.901,
     'L0_gnn_gat_a': 8.0,
     'L0_gnn_edge_Wih': 2.722,
     'L0_gnn_edge_Whh': 3.402,
     'L0_gnn_node_Wih': 5.871,
     'L0_gnn_node_Whh': 3.403}
    for name, (base, spread) in spreads.items():
        noise = np.random.default_rng([zlib.crc32(name.encode()), seed]).standard_normal(out[name].shape)
        drawn = base * np.exp(spread * noise) if base else spread * noise
        out[name] = jnp.asarray(drawn.astype(out[name].dtype))
    for name, factor in factors.items():
        out[name] = (out[name] * factor).astype(out[name].dtype)
    return out
```

```python
from contextlib import ExitStack

import numpy as np

import concourse.bass as bass
from concourse import mybir

ALU = mybir.AluOpType
ACT = mybir.ActivationFunctionType
AXL = mybir.AxisListType
F32 = mybir.dt.float32
BF16 = mybir.dt.bfloat16
I32 = mybir.dt.int32

P = 128
N = 2048
NT = N // P
CH = 512
NCH = N // CH
HEADS = 3
ROWS = 1 + 2 * 3 * HEADS
MASKED = 9.0e15
DI = 2
STATES = 16
DTR = 8
TAPS = 4
PAD = 4
LAST = 3

HW0 = 0
EBP0 = HW0 + HEADS * N
EBM0 = EBP0 + HEADS * N
W0 = EBM0 + HEADS * N
A20 = W0 + 6 * N
B20 = A20 + 4 * N
QT0 = B20 + 4 * N // 2
BIGW = QT0 + 4 * CH
ATG0 = EBP0
PM0 = ATG0 + 2 * NT * CH
X0 = NT * N
XT0 = X0 + N
A10 = XT0 + N
SC0 = XT0 + N
assert PM0 + NT * CH <= X0 and A10 + 4 * N <= BIGW and SC0 + 4 * N <= BIGW


def gnn_program(nc, t, out):
    ctx = ExitStack()
    with ctx:
        ctx.enter_context(nc.allow_non_contiguous_dma(reason="small weight vectors, laid out once"))

        def sb(name, shape, dt=F32):
            return ctx.enter_context(nc.sbuf_tensor(name, shape, dt))

        def sem(name):
            return ctx.enter_context(nc.semaphore(name))

        big = sb("big", [P, BIGW])
        PS = ctx.enter_context(nc.psum_tensor("PS", [P, 8, CH], F32))
        at_dram = nc.dram_tensor("at_dram", (N, N), F32, kind="Internal").ap()

        ns = sb("ns", [P, N])
        es = sb("es", [P, N])
        wt = sb("wt", [P, 15, P])
        ident = sb("ident", [P, P])
        smask = sb("smask", [P, 2, NT, 20], BF16)
        wa = sb("wa", [P, 6])
        ga = sb("ga", [P, HEADS, 2])
        war = sb("war", [P, 2])
        a2 = sb("a2", [P, 2])
        gb = sb("gb", [P, 4, 3])
        gbs = sb("gbs", [P, 2, 2])
        dn = sb("dn", [P, NT])
        deg = sb("deg", [P, NT])
        rdeg = sb("rdeg", [P, NT])
        degt = sb("degt", [P, 8])
        dgt = sb("dgt", [P, P])
        mk = sb("mk", [P, 1])
        flag = sb("flag", [1, 1])
        ymin = sb("ymin", [P, 6])
        zsum = sb("zsum", [P, 6])
        rz = sb("rz", [P, 6])
        stats = sb("stats", [P, NT, 6])
        mv = sb("mv", [P, NT, 2])
        rstd = sb("rstd", [P, NT])
        cst = sb("cst", [P, 2])
        elr = sb("elr", [P, NT, 2])
        bj = sb("bj", [P, NT])
        dj = sb("dj", [P, NT])
        ci = sb("ci", [P, NT])
        zi = sb("zi", [P, NT])
        conv_w = sb("conv_w", [P, DI, TAPS])
        conv_b = sb("conv_b", [P, DI])
        b_dt = sb("b_dt", [P, DI])
        dskip = sb("dskip", [P, DI])
        ln_g = sb("ln_g", [P, 1])
        ln_b = sb("ln_b", [P, 1])
        na = sb("na", [P, DI, STATES])
        state = sb("state", [P, STATES, DI])

        def region(at, words):
            return big[:, at:at + words]

        X = region(X0, N).rearrange("p (t f) -> p t f", f=P)
        XT = region(XT0, N)
        AT = region(0, NT * N).rearrange("p (t i) -> p t i", i=N)
        SC = region(SC0, 4 * N)
        raw = region(PM0, 19 * P).rearrange("p (b k) -> p b k", k=P)
        rawt = region(PM0 + 19 * P, 4 * P).rearrange("p (b k) -> p b k", k=P)
        upc = region(PM0 + 24 * P, 96).rearrange("p (t c) -> p t c", c=6)
        upb = region(PM0 + 25 * P, 48).bitcast(BF16).rearrange("p (t c) -> p t c", c=6)
        hw = region(HW0, HEADS * N).rearrange("p (t h f) -> p t h f", h=HEADS, f=P)
        a1 = [region(A10 + 2 * N * s, 2 * N).rearrange("p (t j) -> p t j", t=2) for s in range(2)]
        atg = [region(ATG0 + NT * CH * g, NT * CH).rearrange("p (t i) -> p t i", i=CH) for g in range(2)]
        pm = [region(PM0 + NT * CH // 2 * m, NT * CH // 2).bitcast(BF16).rearrange("p (t i) -> p t i", i=CH)
              for m in range(2)]
        comb = region(PM0, 6 * P).rearrange("p (s h m) -> p s h m", s=2, h=HEADS)
        eb = region(EBP0, 6 * N).rearrange("p (s h j) -> p s h j", s=2, h=HEADS)
        w = [region(W0 + N * k, N) for k in range(6)]
        aw = [region(A20 + 2 * N * s, 2 * N).rearrange("p (t j) -> p t j", t=2) for s in range(2)]
        bm = [region(B20 + N // 2 * k, N // 2).bitcast(BF16) for k in range(4)]
        qt = [region(QT0 + CH * k, CH) for k in range(4)]
        eb_stage = qt

        adj_tiles = t["adj"].rearrange("(t p) j -> p t j", p=P)
        at_tiles = at_dram.rearrange("(t p) i -> p t i", p=P)
        x_tiles = t["x"].rearrange("(t p) f -> p t f", p=P)

        x_in, gat_in, raw_in, vec_in = sem("x_in"), sem("gat_in"), sem("raw_in"), sem("vec_in")
        ident_ready = sem("ident_ready")
        su_mm, su_act, su_dve = sem("su_mm"), sem("su_act"), sem("su_dve")
        dch = sem("dch")
        a1_in = [sem("a1_in0"), sem("a1_in1")]
        diag_out, deg_done = sem("diag_out"), sem("deg_done")
        tr1, ev1a, ev1v = sem("tr1"), sem("ev1a"), sem("ev1v")
        masks_made, ah_done, e1_done, l1_ev = sem("masks_made"), sem("ah_done"), sem("e1_done"), sem("l1_ev")
        at_out = [sem("at_out0"), sem("at_out1")]
        comb_ready, eb_mm, eb_act, eb_dve = sem("comb_ready"), sem("eb_mm"), sem("eb_act"), sem("eb_dve")
        a2_in = [sem("a2_in0"), sem("a2_in1")]
        x_done, exp_done, q_done = sem("x_done"), sem("exp_done"), sem("q_done")
        tr2, qt_ready, qt_used = sem("tr2"), sem("qt_ready"), sem("qt_used")
        es_out, marked = sem("es_out"), sem("marked")
        offd_done, bm_done, rz_done, signed_step = sem("offd_done"), sem("bm_done"), sem("rz_done"), sem("signed_step")
        at_in, diag_back = sem("at_in"), sem("diag_back")
        xt_mm, xt_ev = sem("xt_mm"), sem("xt_ev")
        gru_mm, gate, tanh_in, tanh_out, gru_out = (sem("gru_mm"), sem("gate"), sem("tanh_in"), sem("tanh_out"),
                                                    sem("gru_out"))
        st_mm, res = sem("st_mm"), sem("res")
        var_ready, std_ready, x_ready = sem("var_ready"), sem("std_ready"), sem("x_ready")
        out_sem = sem("out_sem")
        b2_in = sem("b2_in")
        b_mm = sem("b_mm")
        bb_ready = sem("bb_ready")
        c_mm = sem("c_mm")
        conv_done = sem("conv_done")
        da_ready = sem("da_ready")
        dbc_ev = sem("dbc_ev")
        dbc_mm = sem("dbc_mm")
        dbu_ready = sem("dbu_ready")
        dt_mm = sem("dt_mm")
        dt_ready = sem("dt_ready")
        du_ready = sem("du_ready")
        gru_step = sem("gru_step")
        h_ready = sem("h_ready")
        hc_ready = sem("hc_ready")
        ht_ev = sem("ht_ev")
        l1_a = sem("l1_a")
        l1_aev = sem("l1_aev")
        l1_b = sem("l1_b")
        l1_h = sem("l1_h")
        l1_hev = sem("l1_hev")
        l1_mm = sem("l1_mm")
        l2_aev = sem("l2_aev")
        l2_b = sem("l2_b")
        l2_mm = sem("l2_mm")
        l2_rb = sem("l2_rb")
        l2_rbev = sem("l2_rbev")
        l2_vec = sem("l2_vec")
        l2_x = sem("l2_x")
        l2_xev = sem("l2_xev")
        l2_z = sem("l2_z")
        l2_zev = sem("l2_zev")
        l3_aev = sem("l3_aev")
        l3_g = sem("l3_g")
        l3_gev = sem("l3_gev")
        l3_mm = sem("l3_mm")
        na_exp = sem("na_exp")
        na_ready = sem("na_ready")
        o_mm = sem("o_mm")
        ones_ready = sem("ones_ready")
        pad_ready = sem("pad_ready")
        pieces_ready = sem("pieces_ready")
        q2_ready = sem("q2_ready")
        q2_used = sem("q2_used")
        scan_done = sem("scan_done")
        sel_ready = sem("sel_ready")
        sp_act = sem("sp_act")
        sp_exp = sem("sp_exp")
        sp_ln = sem("sp_ln")
        state_saved = sem("state_saved")
        u_ready = sem("u_ready")
        w2_in = sem("w2_in")
        w3_in = sem("w3_in")
        w4_in = sem("w4_in")
        walb_ready = sem("walb_ready")
        x_plus_b = sem("x_plus_b")
        xps_ready = sem("xps_ready")
        xz_ev = sem("xz_ev")
        xz_mm = sem("xz_mm")
        y_done = sem("y_done")
        y_mm = sem("y_mm")
        yg_ready = sem("yg_ready")
        block = ctx.enter_context(nc.Block())


        def transpose_into(bank, col, src):
            return nc.tensor.transpose(PS[:, bank, col:col + P], src, ident[:])

        H1, AHT = SC[:, 0:N], SC[:, N:2 * N]
        q2 = [SC[:, N * k:N * (k + 1)] for k in range(4)]
        gate_r, gate_z, gru_t, gru_n = ([SC[:, CH * (2 * k + g):CH * (2 * k + g + 1)] for g in range(2)] for k in range(4))
        gru_s = SC[:, 8 * CH:9 * CH]
        walb, b2b = wt[:, 0, :], wt[:, 1, :]
        gcn_w, w_in = wt[:, 2, :], wt[:, 3:7, :]
        w_out, gcn_b, ones_row = wt[:, 7:9, :], wt[0:1, 9, :], wt[0:1, 10, :]
        at = 0

        def late(words, dt=F32):
            nonlocal at
            at += words
            v = region(at - words, words)
            return v if dt == F32 else v.bitcast(dt)

        xc = late(DI * (N + PAD)).rearrange("p (b t) -> p b t", b=DI)
        u, zg, dt_, du = (late(DI * N).rearrange("p (b t) -> p b t", b=DI) for _ in range(4))
        dbc, rest = late(N), late(N)
        mid, pieces = late(N // 2, BF16), late(N // 2, BF16)
        sel = late(32 * P // 2, BF16).rearrange("p (n m) -> p n m", m=P)
        xps = late(DI * 104).rearrange("p (b c) -> p b c", b=DI)
        w_xp = late(DI * 40).rearrange("p (b c) -> p b c", b=DI)
        w_dt = late(DI * P)
        assert at <= NT * N
        tmp = xc[:, :, 0:N]
        yg = tmp
        pairs = [SC[:, k * 2 * CH:(k + 1) * 2 * CH].rearrange("p (b t) -> p b t", b=DI) for k in range(7)]
        hs, hc, dbu = pairs[0:2], pairs[2:4], pairs[4:7]
        bb = [SC[:, (14 + s) * CH:(15 + s) * CH] for s in range(2)]
        xtiles = X.rearrange("p t f -> p (t f)")

        def evac4(eng, copy, mm, base, dst, banks, done):
            for c in range(4):
                eng.wait_ge(mm, base + c + 1)
                copy(dst[:, c * CH:(c + 1) * CH], PS[:, banks + c, :]).then_inc(done, 1)

        def act_copy(o, i, **kw):
            return nc.scalar.activation(o, i, ACT.Copy, **kw)

        def later_loads(sp):
            sp.dma_start(dgt[:], t["L2_gnn_weight"]).then_inc(w2_in, 16)
            if LAST >= 1:
                sp.wait_ge(gru_out, 10)
                sp.dma_start(b2b, t["L2_gnn_b"].partition_broadcast(P)).then_inc(b2_in, 16)
                sp.dma_start(gcn_w, t["L3_gnn_gcn_w"]).then_inc(w3_in, 16)
                sp.dma_start(w_in, t["L3_gnn_w_in"].rearrange("k (b m) -> k b m", m=P)).then_inc(w3_in, 16)
                sp.dma_start(w_out, t["L3_gnn_w_out"].rearrange("(b d) m -> d b m", d=P)).then_inc(w3_in, 16)
                sp.dma_start(gcn_b, t["L3_gnn_gcn_b"].rearrange("(o f) -> o f", o=1)).then_inc(w3_in, 16)
                sp.dma_start(ln_g[:], t["L3_gnn_ln_g"].rearrange("(f o) -> f o", o=1)).then_inc(w3_in, 16)
                sp.dma_start(ln_b[:], t["L3_gnn_ln_b"].rearrange("(f o) -> f o", o=1)).then_inc(w3_in, 16)
                sp.dma_start(conv_w[:], t["L3_gnn_conv_w"].rearrange("(b d) k -> d b k", d=P)).then_inc(w3_in, 16)
                sp.dma_start(na[:], t["L3_gnn_A_log"].rearrange("(b d) k -> d b k", d=P)).then_inc(w3_in, 16)
                for name, v in (("conv_b", conv_b), ("b_dt", b_dt), ("D_skip", dskip)):
                    sp.dma_start(v[:], t["L3_gnn_" + name].rearrange("(b d) -> d b", d=P)).then_inc(w3_in, 16)
            if LAST >= 3:
                sp.wait_ge(l3_mm, 4)
                sp.dma_start(w_xp, t["L3_gnn_w_xp"].rearrange("(b d) k -> d b k", d=P)).then_inc(w4_in, 16)
                sp.dma_start(w_dt[96:96 + DTR, :], t["L3_gnn_w_dt"]).then_inc(w4_in, 16)
            out_tiles = out.rearrange("(t p) f -> p t f", p=P)
            sp.wait_ge(x_ready, LAST + 1)
            for q in range(4):
                sp.dma_start(out_tiles[:, 4 * q:4 * q + 4, :], X[:, 4 * q:4 * q + 4, :]).then_inc(out_sem, 16)
            sp.wait_ge(out_sem, 64)

        def later_pool(pool):
            if LAST >= 2:
                pool.wait_ge(b2_in, 16)
                pool.wait_ge(xt_ev, 12)
                nc.gpsimd.tensor_tensor(X, X, b2b.unsqueeze(1).to_broadcast([P, NT, P]), ALU.add).then_inc(x_plus_b, 1)
            if LAST >= 3:
                pool.wait_ge(l3_mm, 4)
                nc.gpsimd.memset(xc[:, :, 0:PAD], 0.0).then_inc(pad_ready, 1)
                nc.gpsimd.memset(sel[0:96], 0.0).then_inc(sel_ready, 1)
                for p in range(3):
                    pool.wait_ge(sel_ready, p + 1)
                    nc.gpsimd.affine_select(out=sel[0:96], in_=sel[0:96], compare_op=ALU.not_equal, fill=1.0,
                                            base=-32 * p, pattern=[[-1, 32], [0, P]],
                                            channel_multiplier=1).then_inc(sel_ready, 1)
                pool.wait_ge(du_ready, DI)
                for k in range(STATES * NCH):
                    c = k // STATES
                    pool.wait_ge(bb_ready, k + 1)
                    if k >= 3:
                        pool.wait_ge(scan_done, k - 2)
                    nc.gpsimd.tensor_tensor(dbu[k % 3], du[:, :, c * CH:(c + 1) * CH],
                                            bb[k % 2].unsqueeze(1).to_broadcast([P, DI, CH]),
                                            ALU.mult).then_inc(dbu_ready, 1)

        def later_act(act):
            def root(k):
                act.wait_ge(var_ready, k + 1)
                nc.scalar.activation(rstd[:], mv[:, :, 1], ACT.Sqrt, bias=cst[:, 0:1]).then_inc(std_ready, 1)

            def xt_copy(r):
                for q in range(2):
                    act.wait_ge(xt_mm, 4 * r + q + 1)
                    act_copy(XT[:, q * CH:(q + 1) * CH], PS[:, q, :]).then_inc(xt_ev, 1)

            xt_copy(0)
            act.sem_inc(tanh_out, 2)
            with act.Fori(0, NCH) as c:
                for g in range(2):
                    act.wait_ge(gru_mm, c * 2 + g + 1)
                    act.wait_ge(gru_out, c * 2 + g + 1)
                    nc.scalar.activation(gate_r[g], PS[:, 4 * g, :], ACT.Sigmoid, bias=gbs[:, g, 0:1])
                    nc.scalar.activation(gate_z[g], PS[:, 4 * g + 1, :], ACT.Sigmoid, bias=gbs[:, g, 1:2]).then_inc(gate, 1)
                    act.wait_ge(tanh_in, c * 2 + g + 1)
                    nc.scalar.activation(gru_n[g], gru_t[g], ACT.Tanh, bias=gb[:, 2 * g, 2:3]).then_inc(tanh_out, 1)
            root(0)
            if LAST < 1:
                return
            xt_copy(1)
            evac4(act, act_copy, l1_h, 0, H1, 4, l1_hev)
            evac4(act, act_copy, l1_mm, 0, AHT, 0, l1_aev)
            root(1)
            if LAST < 2:
                return
            xt_copy(2)
            evac4(act, act_copy, l2_x, 0, ns[:], 0, l2_xev)
            act.wait_ge(l2_x, 5)
            for dst, src, sc in ((bj, 1, 1.0), (dj, 1, 0.2), (ci, 0, 0.2)):
                nc.scalar.activation(dst[:], PS[:, 4, 0:2 * NT].rearrange("p (t s) -> p t s", s=2)[:, :, src], ACT.Exp,
                                     scale=sc).then_inc(l2_vec, 1)
            for c in range(4):
                act.wait_ge(l2_rb, c + 1)
                nc.scalar.activation(es[:, c * CH:(c + 1) * CH], PS[:, (5 + c) if c < 3 else 4, :], ACT.Exp,
                                     scale=0.8).then_inc(l2_rbev, 1)
            for c in range(4):
                act.wait_ge(l2_mm, c + 1)
                act_copy(q2[0][:, c * CH:(c + 1) * CH], PS[:, c, :]).then_inc(l2_aev, 1)
            root(2)
            if LAST < 3:
                return
            evac4(act, act_copy, l3_mm, 0, AHT, 0, l3_aev)
            for q in range(4):
                act.wait_ge(l3_g, q + 1)
                nc.scalar.activation(H1[:, q * CH:(q + 1) * CH], PS[:, 4 + q, :], ACT.Relu).then_inc(l3_gev, 1)
            root(3)
            for c in range(4):
                for m in range(4):
                    k = 4 * c + m
                    act.wait_ge(xz_mm, k + 1)
                    if m < 2:
                        act_copy(xc[:, m, PAD + c * CH:PAD + (c + 1) * CH], PS[:, k % 8, :]).then_inc(xz_ev, 1)
                    else:
                        nc.scalar.activation(zg[:, m - 2, c * CH:(c + 1) * CH], PS[:, k % 8, :], ACT.Silu).then_inc(xz_ev, 1)
            for b in range(DI):
                act.wait_ge(conv_done, b + 1)
                nc.scalar.activation(u[:, b, :], u[:, b, :], ACT.Silu, bias=conv_b[:, b:b + 1]).then_inc(u_ready, 1)
            act.wait_ge(w3_in, 16 * 11)
            nc.scalar.activation(na[:], na[:], ACT.Exp).then_inc(na_exp, 1)
            for b in range(DI):
                src = PS[:, 4 * b:4 * b + 4, :].rearrange("p c t -> p (c t)")
                act.wait_ge(dt_mm, b + 1)
                nc.scalar.activation(tmp[:, b, :], src, ACT.Abs, bias=b_dt[:, b:b + 1]).then_inc(sp_act, 1)
                nc.scalar.activation(dt_[:, b, :], src, ACT.Relu, bias=b_dt[:, b:b + 1]).then_inc(sp_act, 1)
            for b in range(DI):
                act.wait_ge(sp_act, 2 * b + 1)
                nc.scalar.activation(tmp[:, b, :], tmp[:, b, :], ACT.Exp, scale=-1.0).then_inc(sp_exp, 1)
            for b in range(DI):
                act.wait_ge(sp_exp, b + 1)
                nc.scalar.activation(tmp[:, b, :], tmp[:, b, :], ACT.Ln, bias=1.0).then_inc(sp_ln, 1)
            act.wait_ge(na_ready, 1)
            act.wait_ge(dt_ready, DI)

            def copy_b(k):
                act.wait_ge(b_mm, k + 1)
                if k >= 2:
                    act.wait_ge(dbu_ready, k - 1)
                act_copy(bb[k % 2], PS[:, 0, :]).then_inc(bb_ready, 1)

            def decay(k):
                c, n = k // STATES, k % STATES
                if k >= 2:
                    act.wait_ge(scan_done, k - 1)
                for b in range(DI):
                    e = nc.scalar.activation(PS[:, 4 + 2 * (k % 2) + b, :], dt_[:, b, c * CH:(c + 1) * CH], ACT.Exp,
                                             scale=na[:, b, n:n + 1])
                e.then_inc(da_ready, 1)

            copy_b(0)
            decay(0)
            copy_b(1)
            for k in range(STATES * NCH):
                if k + 1 < STATES * NCH:
                    decay(k + 1)
                if k + 2 < STATES * NCH:
                    copy_b(k + 2)
            root(4)

        def later_pe(pe):
            def xt_fill(r, src=None):
                for q in range(4):
                    for b in range(4):
                        m = transpose_into(q, b * P, (X if src is None else src)[:, 4 * q + b, :])
                    m.then_inc(xt_mm, 1)

            def adjacency_product(weights, done, extra=None):
                for jt in range(NT):
                    if jt % 4 == 0:
                        pe.wait_ge(diag_back, jt // 4 + 1)
                    for c in range(NCH):
                        m = nc.tensor.matmul(PS[:, c, :], weights[:, jt, :], AT[:, jt, c * CH:(c + 1) * CH],
                                             start=(jt == 0), stop=(jt == NT - 1))
                        if jt == NT - 1:
                            m.then_inc(done, 1)

            pe.wait_ge(x_in, 32)
            pe.wait_ge(es_out, 2 + NT // 2)
            xt_fill(0)
            pe.wait_ge(xt_ev, 4)
            with pe.Fori(0, NCH) as c:
                for g in range(2):
                    pe.wait_ge(tanh_out, c * 2 + g + 1)
                    xs = (ns, es)[g][:, bass.ds(c * CH, CH)]
                    hx = XT[:, bass.ds(c * CH, CH)]
                    wi, wh = 6 * g, 6 * g + 3
                    for gate_no in range(2):
                        nc.tensor.matmul(PS[:, 4 * g + gate_no, :], wt[:, wi + gate_no, :], xs, start=True, stop=False)
                        nc.tensor.matmul(PS[:, 4 * g + gate_no, :], wt[:, wh + gate_no, :], hx, start=False, stop=True)
                    nc.tensor.matmul(PS[:, 4 * g + 2, :], wt[:, wi + 2, :], xs, start=True, stop=True)
                    nc.tensor.matmul(PS[:, 4 * g + 3, :], wt[:, wh + 2, :], hx, start=True, stop=True).then_inc(gru_mm, 1)
            pe.wait_ge(gru_out, 2 + 8)
            nst = ns[:].rearrange("p (t i) -> p t i", i=P)
            for q in range(4):
                for b in range(4):
                    m = transpose_into(q, b * P, nst[:, 4 * q + b, :])
                m.then_inc(st_mm, 1)
            if LAST < 1:
                return
            pe.wait_ge(x_ready, 1)
            xt_fill(1)
            pe.wait_ge(xt_ev, 8)
            for jt in range(NT):
                m = nc.tensor.matmul(PS[:, 4 + jt // 4, jt % 4 * P:(jt % 4 + 1) * P], XT[:, jt * P:(jt + 1) * P],
                                     wt[:, 12, :], start=True, stop=True)
                if jt % 4 == 3:
                    m.then_inc(l1_h, 1)
            pe.wait_ge(l1_hev, 4)
            adjacency_product(H1.rearrange("p (t f) -> p t f", f=P), l1_mm)
            for it in range(NT):
                m = nc.tensor.matmul(PS[:, 4 + it // 4, it % 4 * P:(it % 4 + 1) * P], XT[:, it * P:(it + 1) * P],
                                     wt[:, 13, :], start=True, stop=True)
                if it % 4 == 3:
                    m.then_inc(l1_a, 1)
            pe.wait_ge(l1_aev, 4)
            for it in range(NT):
                m = nc.tensor.matmul(PS[:, it // 4, it % 4 * P:(it % 4 + 1) * P], AHT[:, it * P:(it + 1) * P],
                                     wt[:, 14, :], start=True, stop=True)
                if it % 4 == 3:
                    m.then_inc(l1_b, 1)
            if LAST < 2:
                return
            pe.wait_ge(x_ready, 2)
            xt_fill(2)
            pe.wait_ge(xt_ev, 12)
            pe.wait_ge(w2_in, 16)
            for jt in range(NT):
                m = nc.tensor.matmul(PS[:, jt // 4, jt % 4 * P:(jt % 4 + 1) * P], XT[:, jt * P:(jt + 1) * P], dgt[:],
                                     start=True, stop=True)
                if jt % 4 == 3:
                    m.then_inc(l2_x, 1)
            for jt in range(NT):
                m = nc.tensor.matmul(PS[:, 4, 2 * jt:2 * jt + 2], XT[:, jt * P:(jt + 1) * P], war[:], start=True, stop=True)
            m.then_inc(l2_x, 1)
            pe.wait_ge(walb_ready, 1)
            for c in range(4):
                if c == 3:
                    pe.wait_ge(l2_vec, 3)
                nc.tensor.matmul(PS[:, (5 + c) if c < 3 else 4, :], walb, XT[:, c * CH:(c + 1) * CH], start=True,
                                 stop=True).then_inc(l2_rb, 1)
            pe.wait_ge(l2_xev, 4)
            pe.wait_ge(l2_rbev, 4)
            x2 = ns[:].rearrange("p (t f) -> p t f", f=P)
            for jt in range(NT):
                pe.wait_ge(q2_ready, jt + 1)
                for c in range(NCH):
                    m = nc.tensor.matmul(PS[:, c, :], x2[:, jt, :], q2[jt % 4][:, c * CH:(c + 1) * CH], start=(jt == 0),
                                         stop=(jt == NT - 1))
                    if jt == NT - 1:
                        m.then_inc(l2_mm, 1)
                for c in range(NCH):
                    m = nc.tensor.matmul(PS[0:1, 4 + c, :], cst[:, 1:2], q2[jt % 4][:, c * CH:(c + 1) * CH],
                                         start=(jt == 0), stop=(jt == NT - 1))
                m.then_inc(q2_used, 1)
            pe.wait_ge(l2_aev, 4)
            nt = q2[0].rearrange("p (t i) -> p t i", i=P)
            for q in range(4):
                for b in range(4):
                    m = transpose_into(q, b * P, nt[:, 4 * q + b, :])
                m.then_inc(l2_b, 1)
            pe.wait_ge(l2_zev, 4)
            for it in range(NT):
                m = nc.tensor.matmul(PS[:, 4, it:it + 1], es[0:1, it * P:(it + 1) * P], cst[0:1, 1:2], start=True, stop=True)
            m.then_inc(l2_z, 1)
            if LAST < 3:
                return
            pe.wait_ge(x_ready, 3)
            adjacency_product(X, l3_mm)
            pe.wait_ge(l3_aev, 4)
            pe.wait_ge(w3_in, 16 * 11)
            pe.wait_ge(ones_ready, 1)
            for it in range(NT):
                o = PS[:, 4 + it // 4, it % 4 * P:(it % 4 + 1) * P]
                nc.tensor.matmul(o, AHT[:, it * P:(it + 1) * P], gcn_w, start=True, stop=False)
                m = nc.tensor.matmul(o, ones_row, gcn_b, start=False, stop=True)
                if it % 4 == 3:
                    m.then_inc(l3_g, 1)
            pe.wait_ge(h_ready, 1)
            xt_fill(3, H1.rearrange("p (t f) -> p t f", f=P))
            for c in range(4):
                pe.wait_ge(ht_ev, c + 1)
                for m_ in range(4):
                    k = 4 * c + m_
                    if k >= 8:
                        pe.wait_ge(xz_ev, k - 7)
                    elif k < 4:
                        pe.wait_ge(ht_ev, 4)
                    nc.tensor.matmul(PS[:, k % 8, :], w_in[:, m_, :], es[:, c * CH:(c + 1) * CH], start=True,
                                     stop=True).then_inc(xz_mm, 1)
            pe.wait_ge(xz_ev, 16)
            pe.wait_ge(u_ready, DI)
            pe.wait_ge(xps_ready, 1)
            for c in range(NCH):
                for b in range(DI):
                    m = nc.tensor.matmul(PS[0:104, c, :], xps[:, b, :], u[:, b, c * CH:(c + 1) * CH], start=(b == 0),
                                         stop=(b == 1))
                m.then_inc(dbc_mm, 1)
            pe.wait_ge(dbc_ev, 4)
            for b in range(DI):
                for c in range(NCH):
                    m = nc.tensor.matmul(PS[:, 4 * b + c, :], w_dt[96:96 + DTR, b * P:(b + 1) * P],
                                         dbc[96:96 + DTR, c * CH:(c + 1) * CH], start=True, stop=True)
                m.then_inc(dt_mm, 1)
            pe.wait_ge(sp_act, 4)
            pe.wait_ge(pieces_ready, 1)
            pe.wait_ge(sel_ready, 4)

            def add_up(k):
                c, n = k // STATES, k % STATES
                pe.wait_ge(hc_ready, k + 1)
                if n == 0 and c:
                    pe.wait_ge(y_done, c)
                for b in range(DI):
                    m = nc.tensor.matmul(PS[:, 2 + b, :], ident[:], hc[k % 2][:, b, :], start=(n == 0),
                                         stop=(n == STATES - 1))
                m.then_inc(y_mm, 1)

            def spread(k, bank, row, done):
                c = k // STATES
                nc.tensor.matmul(PS[:, bank, :], sel[0:96, row + k % STATES, :], pieces[0:96, c * CH:(c + 1) * CH],
                                 start=True, stop=True).then_inc(done, 1)

            spread(0, 0, 0, b_mm)
            pe.wait_ge(bb_ready, 1)
            spread(1, 0, 0, b_mm)
            for k in range(STATES * NCH):
                if k + 2 < STATES * NCH:
                    pe.wait_ge(bb_ready, k + 2)
                    spread(k + 2, 0, 0, b_mm)
                if k:
                    pe.wait_ge(hc_ready, k)
                spread(k, 1, STATES, c_mm)
                if k:
                    add_up(k - 1)
            add_up(STATES * NCH - 1)
            for q in range(4):
                pe.wait_ge(yg_ready, q + 1)
                if q == 0:
                    pe.wait_ge(scan_done, STATES * NCH)
                for s in range(4):
                    it = 4 * q + s
                    for b in range(DI):
                        m = nc.tensor.matmul(PS[:, 4 + q, s * P:(s + 1) * P], yg[:, b, it * P:(it + 1) * P], w_out[:, b, :],
                                             start=(b == 0), stop=(b == 1))
                m.then_inc(o_mm, 1)

        def later_dve(dve, link):
            def norm(k, v, ready):
                for i in range(NT):
                    m = nc.vector.bn_stats(stats[:, i, :], v[:, i, :])
                link(m)
                for i in range(NT):
                    m = nc.vector.bn_aggr(mv[:, i, :], stats[:, i, :])
                m.then_inc(var_ready, 1)
                dve.wait_ge(std_ready, k + 1)
                link(nc.vector.reciprocal(rstd[:], rstd[:]))
                for i in range(NT):
                    m = nc.vector.tensor_scalar(v[:, i, :], v[:, i, :], mv[:, i, 0:1], rstd[:, i:i + 1], ALU.subtract,
                                                ALU.mult)
                m.then_inc(ready, 1)

            def xt_copy(r):
                for q in range(2, 4):
                    dve.wait_ge(xt_mm, 4 * r + q + 1)
                    nc.vector.tensor_copy(XT[:, q * CH:(q + 1) * CH], PS[:, q, :]).then_inc(xt_ev, 1)

            xt_copy(0)
            dve.sem_inc(gru_out, 2)
            with dve.Fori(0, NCH) as c:
                steps = [0]

                def chain(ins):
                    steps[0] += 1
                    ins.then_inc(gru_step, 1)
                    dve.wait_ge(gru_step, c * 7 + steps[0])

                for g in range(2):
                    dve.wait_ge(gate, c * 2 + g + 1)
                    chain(nc.vector.scalar_tensor_tensor(gru_t[g], PS[:, 4 * g + 3, :], gb[:, 2 * g + 1, 2:3], gate_r[g],
                                                         ALU.add, ALU.mult))
                    nc.vector.tensor_tensor(gru_t[g], PS[:, 4 * g + 2, :], gru_t[g], ALU.add).then_inc(tanh_in, 1)
                    dve.wait_ge(tanh_out, c * 2 + g + 3)
                    chain(nc.vector.tensor_tensor(gru_t[g], XT[:, bass.ds(c * CH, CH)], gru_n[g], ALU.subtract))
                    chain(nc.vector.tensor_tensor(gru_t[g], gru_t[g], gate_z[g], ALU.mult))
                    if g == 0:
                        nc.vector.tensor_tensor(gru_s, gru_t[0], gru_n[0], ALU.add).then_inc(gru_out, 1)
                    else:
                        chain(nc.vector.tensor_tensor(gru_t[1], gru_t[1], gru_n[1], ALU.add))
                        nc.vector.tensor_tensor(ns[:, bass.ds(c * CH, CH)], gru_t[1], gru_s, ALU.add).then_inc(gru_out, 1)
                assert steps[0] == 7
            for jt in range(NT):
                blk = AT[:, jt, jt * P:(jt + 1) * P]
                if jt % 4 == 0:
                    dve.wait_ge(at_in, 16 * NCH)
                m = nc.vector.scalar_tensor_tensor(blk, ident[:], dn[:, jt:jt + 1], blk, ALU.mult, ALU.add)
                if jt % 4 == 3:
                    m.then_inc(diag_back, 1)
            nc.vector.tensor_copy(walb, war[:, 0:1].to_broadcast([P, P])).then_inc(walb_ready, 1)
            nc.vector.memset(ones_row, 1.0).then_inc(ones_ready, 1)
            link(nc.vector.scalar_tensor_tensor(rdeg[:], deg[:], 1.0, dn[:], ALU.add, ALU.add))
            link(nc.vector.reciprocal(rdeg[:], rdeg[:]))
            for i in range(NT):
                if i % 4 == 0:
                    dve.wait_ge(st_mm, i // 4 + 1)
                m = nc.vector.scalar_tensor_tensor(X[:, i, :], PS[:, i // 4, i % 4 * P:(i % 4 + 1) * P], dn[:, i:i + 1],
                                                   X[:, i, :], ALU.mult, ALU.add)
            link(m)
            norm(0, X, x_ready)
            if LAST < 1:
                return
            xt_copy(1)
            for q in range(4):
                dve.wait_ge(l1_b, q + 1)
                for i in range(4 * q, 4 * q + 4):
                    m = nc.vector.scalar_tensor_tensor(X[:, i, :], PS[:, q, i % 4 * P:(i % 4 + 1) * P], rdeg[:, i:i + 1],
                                                       X[:, i, :], ALU.mult, ALU.add)
                link(m)
                m = nc.vector.tensor_tensor(xtiles[:, q * CH:(q + 1) * CH], PS[:, 4 + q, :], xtiles[:, q * CH:(q + 1) * CH],
                                            ALU.add)
            link(m)
            norm(1, X, x_ready)
            if LAST < 2:
                return
            xt_copy(2)
            dve.wait_ge(l2_vec, 3)
            dve.wait_ge(l2_rbev, 4)
            for jt in range(NT):
                if jt >= 4:
                    dve.wait_ge(q2_used, jt - 3)
                link(nc.vector.tensor_scalar(q2[jt % 4], es[:], bj[:, jt:jt + 1], dj[:, jt:jt + 1], ALU.mult, ALU.max))
                nc.vector.scalar_tensor_tensor(q2[jt % 4], AT[:, jt, :], 0.0, q2[jt % 4], ALU.not_equal,
                                               ALU.mult).then_inc(q2_ready, 1)
            dve.wait_ge(q2_used, NT)
            for c in range(4):
                nc.vector.tensor_copy(es[0:1, c * CH:(c + 1) * CH], PS[0:1, 4 + c, :]).then_inc(l2_zev, 1)
            dve.wait_ge(l2_z, 1)
            link(nc.vector.tensor_tensor(zi[:], PS[:, 4, 0:NT], ci[:], ALU.mult))
            link(nc.vector.tensor_scalar(zi[:], zi[:], 1e-12, None, ALU.max))
            link(nc.vector.reciprocal(zi[:], zi[:]))
            link(nc.vector.tensor_tensor(zi[:], zi[:], ci[:], ALU.mult))
            dve.wait_ge(x_plus_b, 1)
            for i in range(NT):
                if i % 4 == 0:
                    dve.wait_ge(l2_b, i // 4 + 1)
                m = nc.vector.scalar_tensor_tensor(X[:, i, :], PS[:, i // 4, i % 4 * P:(i % 4 + 1) * P], zi[:, i:i + 1],
                                                   X[:, i, :], ALU.mult, ALU.add)
            link(m)
            norm(2, X, x_ready)
            if LAST < 3:
                return
            dve.wait_ge(l3_gev, 4)
            norm(3, H1.rearrange("p (t f) -> p t f", f=P), h_ready)
            for q in range(4):
                dve.wait_ge(xt_mm, 12 + q + 1)
                nc.vector.tensor_scalar(es[:, q * CH:(q + 1) * CH], PS[:, q, :], ln_g[:], ln_b[:], ALU.mult,
                                        ALU.add).then_inc(ht_ev, 1)
            dve.wait_ge(w4_in, 32)
            for k in range(3):
                nc.vector.tensor_copy(xps[:, :, 32 * k:32 * (k + 1)], w_xp[:, :, DTR:DTR + 32])
            nc.vector.tensor_copy(xps[:, :, 96:104], w_xp[:, :, 0:DTR]).then_inc(xps_ready, 1)
            dve.wait_ge(pad_ready, 1)
            dve.wait_ge(xz_ev, 16)
            for k in range(TAPS):
                for b in range(DI):
                    src = xc[:, b, PAD - 3 + k:PAD - 3 + k + N]
                    if k == 0:
                        m = nc.vector.tensor_scalar(u[:, b, :], src, conv_w[:, b, 0:1], None, ALU.mult)
                    else:
                        m = nc.vector.scalar_tensor_tensor(u[:, b, :], src, conv_w[:, b, k:k + 1], u[:, b, :], ALU.mult,
                                                           ALU.add)
                    if k == TAPS - 1:
                        m.then_inc(conv_done, 1)
                    elif b == 1:
                        link(m)
            dve.wait_ge(na_exp, 1)
            nc.vector.tensor_scalar(na[:], na[:], -1.0, None, ALU.mult).then_inc(na_ready, 1)
            nc.vector.memset(state[:], 0.0).then_inc(state_saved, 1)
            for c in range(4):
                dve.wait_ge(dbc_mm, c + 1)
                nc.vector.tensor_copy(dbc[0:104, c * CH:(c + 1) * CH], PS[0:104, c, :]).then_inc(dbc_ev, 1)
            dve.wait_ge(dbc_ev, 4)
            link(nc.vector.tensor_copy(pieces[0:96], dbc[0:96]))
            link(nc.vector.tensor_tensor(rest[0:96], dbc[0:96], pieces[0:96], ALU.subtract))
            link(nc.vector.tensor_copy(mid[0:96], rest[0:96]))
            link(nc.vector.tensor_copy(pieces[32:64], mid[32:64]))
            link(nc.vector.tensor_tensor(rest[64:96], rest[64:96], mid[64:96], ALU.subtract))
            nc.vector.tensor_copy(pieces[64:96], rest[64:96]).then_inc(pieces_ready, 1)
            for b in range(DI):
                dve.wait_ge(sp_ln, b + 1)
                nc.vector.tensor_tensor(dt_[:, b, :], dt_[:, b, :], tmp[:, b, :], ALU.add).then_inc(dt_ready, 1)
            for b in range(DI):
                dve.wait_ge(dt_ready, b + 1)
                nc.vector.tensor_tensor(du[:, b, :], dt_[:, b, :], u[:, b, :], ALU.mult).then_inc(du_ready, 1)
            for c in range(NCH):
                cols = slice(c * CH, (c + 1) * CH)
                for n in range(STATES):
                    k = STATES * c + n
                    dve.wait_ge(da_ready, k + 1)
                    dve.wait_ge(dbu_ready, k + 1)
                    dve.wait_ge(state_saved, k - STATES + 2 if k >= STATES else 1)
                    for b in range(DI):
                        m = nc.vector.tensor_tensor_scan(hs[k % 2][:, b, :], PS[:, 4 + 2 * (k % 2) + b, :], dbu[k % 3][:, b, :],
                                                         state[:, n, b:b + 1], ALU.mult, ALU.add)
                    m.then_inc(scan_done, 1)
                    dve.wait_ge(scan_done, k + 1)
                    dve.wait_ge(c_mm, k + 1)
                    if k >= 2:
                        dve.wait_ge(y_mm, k - 1)
                    nc.vector.tensor_tensor(hc[k % 2], PS[:, 1, :].unsqueeze(1).to_broadcast([P, DI, CH]), hs[k % 2],
                                            ALU.mult).then_inc(hc_ready, 1)
                    nc.vector.tensor_copy(state[:, n, :], hs[k % 2][:, :, CH - 1]).then_inc(state_saved, 1)
                dve.wait_ge(y_mm, STATES * (c + 1))
                for b in range(DI):
                    m = nc.vector.scalar_tensor_tensor(yg[:, b, cols], u[:, b, cols], dskip[:, b:b + 1], PS[:, 2 + b, :],
                                                       ALU.mult, ALU.add)
                m.then_inc(y_done, 1)
                dve.wait_ge(y_done, c + 1)
                nc.vector.tensor_tensor(yg[:, :, cols], yg[:, :, cols], zg[:, :, cols], ALU.mult).then_inc(yg_ready, 1)
            for q in range(4):
                dve.wait_ge(o_mm, q + 1)
                m = nc.vector.tensor_tensor(xtiles[:, q * CH:(q + 1) * CH], PS[:, 4 + q, :], xtiles[:, q * CH:(q + 1) * CH],
                                            ALU.add)
            link(m)
            norm(4, X, x_ready)

        @block.sync
        def _(sp):
            for s in range(2):
                sp.dma_start(a1[s], adj_tiles[:, 2 * s:2 * s + 2, :]).then_inc(a1_in[s], 16)
            for g in range(NCH):
                for s in range(2):
                    k = 2 * g + s
                    if k + 2 < NT // 2:
                        sp.wait_ge(tr1, 8 * (k + 1))
                        sp.wait_ge(deg_done, 2 * (k + 1))
                        sp.dma_start(a1[s], adj_tiles[:, 2 * k + 4:2 * k + 6, :]).then_inc(a1_in[s], 16)
                sp.wait_ge(ev1a, 8 * (g + 1))
                sp.wait_ge(ev1v, 8 * (g + 1))
                sp.dma_start(at_tiles[:, :, g * CH:(g + 1) * CH], atg[g % 2]).then_inc(at_out[g % 2], 16)
            sp.wait_ge(ah_done, NCH)
            sp.wait_ge(deg_done, NT)
            for s in range(2):
                sp.dma_start(aw[s], adj_tiles[:, 2 * s:2 * s + 2, :]).then_inc(a2_in[s], 16)
            with sp.Fori(0, NT // 4 - 1) as it:
                for s in range(2):
                    sp.wait_ge(q_done, it * 6 + 3 * (s + 1))
                    sp.dma_start(aw[s], adj_tiles[:, bass.ds(it * 4 + 4 + 2 * s, 2), :]).then_inc(a2_in[s], 16)
            sp.wait_ge(qt_used, 4 + 4 * 48)
            sp.wait_ge(q_done, 3 * NT // 2)
            for s in range(2):
                sp.wait_ge(at_out[s], 32)
            sp.dma_start(X, x_tiles).then_inc(x_in, 16)
            for b in range(NT // 4):
                sp.dma_start(AT[:, 4 * b:4 * b + 4, :], at_tiles[:, 4 * b:4 * b + 4, :]).then_inc(at_in, 16)
            later_loads(sp)

        @block.gpsimd
        def _(pool):
            nc.gpsimd.memset(ident[:], 0.0).then_inc(ident_ready, 1)
            nc.gpsimd.memset(cst[:, 0:1], 1e-5).then_inc(ident_ready, 1)
            nc.gpsimd.memset(cst[:, 1:2], 1.0).then_inc(ident_ready, 1)
            nc.gpsimd.memset(smask[:, 0], 0.0).then_inc(ident_ready, 1)
            nc.gpsimd.memset(smask[:, 1], 1.0).then_inc(ident_ready, 1)
            pool.wait_ge(ident_ready, 5)
            nc.gpsimd.affine_select(out=ident[:], in_=ident[:], compare_op=ALU.not_equal, fill=1.0, base=0,
                                    pattern=[[-1, P]], channel_multiplier=1).then_inc(ident_ready, 1)
            pool.wait_ge(e1_done, NCH)
            nc.gpsimd.memset(comb[0:ROWS], 0.0).then_inc(comb_ready, 1)
            for p in range(3):
                pool.wait_ge(comb_ready, p + 1)
                nc.gpsimd.affine_select(out=comb[0:ROWS], in_=comb[0:ROWS], compare_op=ALU.not_equal, fill=-1.0,
                                        base=-(1 + 3 * p), pattern=[[-9, 2], [-1, 3], [0, P]],
                                        channel_multiplier=1).then_inc(comb_ready, 1)
            later_pool(pool)

        @block.scalar
        def _(act):
            act.dma_start(X, x_tiles).then_inc(x_in, 16)
            act.dma_start(raw[:, 16:19, :], t["L0_gnn_gat_W"].rearrange("h k f -> k h f")).then_inc(gat_in, 16)
            act.dma_start(raw[:, 15, :], t["L2_gnn_weight"]).then_inc(gat_in, 16)
            for h in range(HEADS):
                act.dma_start(ga[:, h, :], t["L0_gnn_gat_a"][h].rearrange("(s f) o -> f (s o)", f=P)).then_inc(vec_in, 16)
            act.dma_start(a2[:, 0:1], t["L2_gnn_a_l"].rearrange("(f o) -> f o", o=1)).then_inc(vec_in, 16)
            act.dma_start(a2[:, 1:2], t["L2_gnn_a_r"].rearrange("(f o) -> f o", o=1)).then_inc(vec_in, 16)
            gru = ["edge_Wih", "edge_Whh", "node_Wih", "node_Whh"]
            for k, name in enumerate(gru):
                act.dma_start(raw[:, 3 * k:3 * k + 3, :],
                              t["L0_gnn_" + name].rearrange("(g p) k -> p g k", p=P)).then_inc(raw_in, 16)
            act.dma_start(raw[:, 12, :], t["L1_gnn_neigh_W"]).then_inc(raw_in, 16)
            act.dma_start(raw[:, 13:15, :], t["L1_gnn_lin_W"].rearrange("o (b c) -> o b c", c=P)).then_inc(raw_in, 16)
            for k, name in enumerate(["edge_bih", "edge_bhh", "node_bih", "node_bhh"]):
                act.dma_start(gb[:, k, :], t["L0_gnn_" + name].rearrange("(g p) -> p g", p=P)).then_inc(vec_in, 16)

            act.wait_ge(su_mm, 1)
            nc.scalar.activation(rawt[:], PS[:, 0, :].rearrange("p (b k) -> p b k", k=P), ACT.Copy).then_inc(su_act, 1)
            for q in range(4):
                n = 4 if q < 3 else 3
                act.wait_ge(su_mm, 6 + q)
                nc.scalar.activation(wt[:, 4 * q:4 * q + n, :],
                                     PS[:, (5 + q) % 8, 0:n * P].rearrange("p (b k) -> p b k", k=P),
                                     ACT.Copy).then_inc(su_act, 1)
            act.wait_ge(su_mm, 10)
            nc.scalar.activation(wa[:], PS[:, 1, 0:6], ACT.Copy).then_inc(su_act, 1)
            nc.scalar.activation(war[:], PS[:, 1, 6:8], ACT.Copy).then_inc(su_act, 1)
            for jt in range(NT):
                act.wait_ge(su_mm, 11 + jt)
                nc.scalar.activation(hw[:, jt].rearrange("p h f -> p (h f)"), PS[:, 4 + jt % 4, 0:HEADS * P],
                                     ACT.Copy).then_inc(su_act, 1)

            for g in range(NCH):
                for k in range(4):
                    tile = 4 * g + k
                    act.wait_ge(diag_out, tile + 1)
                    if tile:
                        act.wait_ge(deg_done, tile)
                    nc.scalar.activation(XT, a1[tile // 2 % 2][:, tile % 2, :], ACT.Copy,
                                         accum_out=deg[:, tile:tile + 1]).then_inc(deg_done, 1)
                    for b in range(2):
                        act.wait_ge(tr1, 4 * tile + b + 1)
                        if k == 0 and b == 0 and g >= 2:
                            act.wait_ge(at_out[g % 2], 16)
                            act.wait_ge(ah_done, g - 1)
                            act.wait_ge(masks_made, 4 * (g - 1))
                        nc.scalar.activation(atg[g % 2][:, 4 * b:4 * b + 4, k * P:(k + 1) * P],
                                             PS[:, b, :].rearrange("p (t i) -> p t i", i=P),
                                             ACT.Copy).then_inc(ev1a, 1)

            for q in range(24):
                act.wait_ge(eb_mm, q + 1)
                if q >= 2:
                    act.wait_ge(eb_dve, q - 1)
                nc.scalar.activation(eb_stage[q % 2], PS[:, q % 8, :], ACT.Copy, scale=0.2).then_inc(eb_act, 1)

            act.sem_inc(qt_ready, 4)
            act.sem_inc(es_out, 2)
            with act.Fori(0, NT // 4) as it:
                def evacuate(k):
                    for v in range(8):
                        act.wait_ge(tr2, it * 48 + 8 * k + v + 25)
                        act.wait_ge(qt_used, it * 48 + 8 * k + v + 1)
                        nc.scalar.activation(qt[v % 4], PS[:, v % 4, :], ACT.Copy).then_inc(qt_ready, 1)

                def support(pair):
                    act.wait_ge(qt_used, it * 48 + 24 * pair + 28)
                    act.wait_ge(eb_dve, 24)
                    nc.scalar.activation(es[:, bass.ds(it * CH + 256 * pair, 256)], PS[:, 4 + pair, 0:256], ACT.Copy,
                                         scale=1.0 / HEADS).then_inc(es_out, 1)

                for k in range(6):
                    act.wait_ge(x_done, it * 6 + k + 1)
                    for j in range(2):
                        s = 2 * (k % 3) + j
                        e = nc.scalar.activation(w[s], w[s], ACT.Exp, bias=ymin[:, s:s + 1], scale=-1.0,
                                                 accum_out=zsum[:, s:s + 1])
                    e.then_inc(exp_done, 1)
                    if k >= 1:
                        evacuate(k - 1)
                    if k == 5:
                        support(0)
                evacuate(5)
                support(1)
            later_act(act)

        @block.tensor
        def _(pe):
            pe.wait_ge(ident_ready, 6)
            pe.wait_ge(gat_in, 16 * 2)
            for b in range(4):
                m = transpose_into(0, b * P, raw[:, 15 + b, :])
            m.then_inc(su_mm, 1)
            pe.wait_ge(x_in, 16)
            for q in range(4):
                for b in range(4):
                    m = transpose_into(1 + q, b * P, X[:, 4 * q + b, :])
                m.then_inc(su_mm, 1)
            pe.wait_ge(raw_in, 16 * 6)
            for q in range(4):
                if q == 3:
                    pe.wait_ge(su_act, 1)
                for b in range(4 if q < 3 else 3):
                    m = transpose_into((5 + q) % 8, b * P, raw[:, 4 * q + b, :])
                m.then_inc(su_mm, 1)
            pe.wait_ge(su_dve, 4)
            pe.wait_ge(vec_in, 16 * 9)
            for h in range(HEADS):
                nc.tensor.matmul(PS[:, 1, 2 * h:2 * h + 2], rawt[:, 1 + h, :], ga[:, h, :], start=True, stop=True)
            nc.tensor.matmul(PS[:, 1, 6:8], rawt[:, 0, :], a2[:], start=True, stop=True).then_inc(su_mm, 1)
            for jt in range(NT):
                if jt < 4:
                    pe.wait_ge(su_act, 2 + min(jt, 3) if jt else 2)
                else:
                    pe.wait_ge(su_act, 7 + jt - 3)
                nc.tensor.matmul(PS[:, 4 + jt % 4, 0:HEADS * P], XT[:, jt * P:(jt + 1) * P],
                                 raw[:, 16:19, :].rearrange("p h f -> p (h f)"), start=True,
                                 stop=True).then_inc(su_mm, 1)
            pe.wait_ge(su_act, 7)
            for jt in range(NT):
                m = nc.tensor.matmul(PS[:, 2, 6 * jt:6 * jt + 6], XT[:, jt * P:(jt + 1) * P], wa[:], start=True,
                                     stop=True)
            m.then_inc(su_mm, 1)

            def products(g, q):
                pe.wait_ge(ev1a, 8 * (g + 1))
                pe.wait_ge(ev1v, 8 * (g + 1))
                if q == 0 and g >= 2:
                    pe.wait_ge(l1_ev, 2 * (g - 1))
                for jt in range(4 * q, 4 * q + 4):
                    m = nc.tensor.matmul(PS[:, 4 + g % 2, :], X[:, jt, :], atg[g % 2][:, jt, :],
                                         start=(jt == 0), stop=(jt == NT - 1))
                if q == 3:
                    m.then_inc(ah_done, 1)
                pe.wait_ge(masks_made, 4 * g + q + 1)
                for jt in range(4 * q, 4 * q + 4):
                    for s in range(2):
                        m = nc.tensor.matmul(PS[0:ROWS, 6 + g % 2, :], smask[:, s, jt, 0:ROWS], pm[s][:, jt, :],
                                             start=(jt == 0 and s == 0), stop=(jt == NT - 1 and s == 1))
                if q == 3:
                    m.then_inc(e1_done, 1)

            pe.wait_ge(su_act, 7 + NT)
            pe.wait_ge(su_dve, 5)
            for g in range(NCH):
                for k in range(4):
                    tile = 4 * g + k
                    pe.wait_ge(diag_out, tile + 1)
                    for b in range(4):
                        if tile:
                            pe.wait_ge(ev1a if b < 2 else ev1v, 2 * (tile - 1) + b % 2 + 1)
                        for c in range(4):
                            m = transpose_into(b, c * P, a1[tile // 2 % 2][:, tile % 2, (4 * b + c) * P:(4 * b + c + 1) * P])
                        m.then_inc(tr1, 1)
                    if g >= 1:
                        products(g - 1, k)
            for k in range(4):
                products(NCH - 1, k)

            pe.wait_ge(comb_ready, 4)
            pe.wait_ge(l1_ev, 2 * NCH)
            for q in range(24):
                if q >= 8:
                    pe.wait_ge(eb_dve, q - 7)
                nc.tensor.matmul(PS[:, q % 8, :], comb[0:ROWS, q // 12, q // 4 % 3, :],
                                 es[0:ROWS, q % 4 * CH:(q % 4 + 1) * CH], start=True, stop=True).then_inc(eb_mm, 1)
            pe.wait_ge(eb_dve, 24)

            pe.sem_inc(tr2, 24)
            pe.sem_inc(qt_used, 4)
            with pe.Fori(0, NT // 4) as it:
                for k in range(6):
                    h = k % 3
                    pe.wait_ge(q_done, it * 6 + k + 1)

                    def fill(v):
                        pe.wait_ge(qt_ready, it * 48 + 8 * k + v + 1)
                        for c in range(2):
                            for j in range(2):
                                m = transpose_into(v % 4, 256 * c + j * P, w[2 * (k % 3) + j][:, (2 * v + c) * P:(2 * v + c + 1) * P])
                        m.then_inc(tr2, 1)

                    def multiply(v):
                        pe.wait_ge(qt_ready, it * 48 + 8 * k + v + 5)
                        if h == 0 and v == 0:
                            pe.wait_ge(es_out, it * 2 + k // 3 + 1)
                        for c in range(2):
                            jt = 2 * v + c
                            m = nc.tensor.matmul(PS[:, 4 + k // 3, 0:256], hw[:, jt, h, :], qt[v % 4][:, 256 * c:256 * c + 256],
                                                 start=(h == 0 and jt == 0), stop=(h == 2 and jt == NT - 1))
                        m.then_inc(qt_used, 1)

                    fill(0)
                    fill(1)
                    for v in range(8):
                        if v + 2 < 8:
                            fill(v + 2)
                        multiply(v)
            later_pe(pe)

        @block.vector
        def _(dve):
            count = [0]

            def link(ins):
                count[0] += 1
                ins.then_inc(dch, 1)
                dve.wait_ge(dch, count[0])

            for q in range(4):
                dve.wait_ge(su_mm, 2 + q)
                nc.vector.tensor_copy(XT[:, q * CH:(q + 1) * CH], PS[:, 1 + q, :]).then_inc(su_dve, 1)
            nc.vector.memset(mk[:], 0.0).then_inc(marked, 1)
            dve.wait_ge(vec_in, 16 * 9)
            for g in range(2):
                nc.vector.tensor_tensor(gbs[:, g, :], gb[:, 2 * g, 0:2], gb[:, 2 * g + 1, 0:2], ALU.add)
            dve.wait_ge(su_mm, 11 + NT)
            link(nc.vector.tensor_copy(upc[:], PS[:, 2, 0:96].rearrange("p (t c) -> p t c", c=6)))
            dve.wait_ge(ident_ready, 6)
            for p in range(3):
                link(nc.vector.tensor_copy(upb[:], upc[:]))
                for s in range(2):
                    part = upb[:].rearrange("p t (h s) -> p t h s", s=2)[:, :, :, s]
                    nc.vector.tensor_copy(smask[:, 0, :, 1 + 9 * s + 3 * p:4 + 9 * s + 3 * p], part)
                    last = nc.vector.tensor_copy(smask[:, 1, :, 10 - 9 * s + 3 * p:13 - 9 * s + 3 * p], part)
                if p < 2:
                    link(last)
                    link(nc.vector.tensor_tensor(upc[:], upc[:], upb[:], ALU.subtract))
            last.then_inc(su_dve, 1)

            def masks(g, q):
                if q == 0:
                    dve.wait_ge(ev1a, 8 * (g + 1))
                    dve.wait_ge(ev1v, 8 * (g + 1))
                    if g:
                        dve.wait_ge(e1_done, g)
                src = atg[g % 2][:, 4 * q:4 * q + 4, :]
                nc.vector.tensor_scalar(pm[0][:, 4 * q:4 * q + 4, :], src, 0.0, None, ALU.is_gt)
                nc.vector.tensor_scalar(pm[1][:, 4 * q:4 * q + 4, :], src, 0.0, None, ALU.is_lt).then_inc(masks_made, 1)

            def rows_out(g):
                dve.wait_ge(ah_done, g + 1)
                nc.vector.tensor_copy(ns[:, g * CH:(g + 1) * CH], PS[:, 4 + g % 2, :]).then_inc(l1_ev, 1)
                dve.wait_ge(e1_done, g + 1)
                nc.vector.tensor_copy(es[0:ROWS, g * CH:(g + 1) * CH], PS[0:ROWS, 6 + g % 2, :]).then_inc(l1_ev, 1)

            for g in range(NCH):
                for k in range(4):
                    tile = 4 * g + k
                    blk = a1[tile // 2 % 2][:, tile % 2, tile * P:(tile + 1) * P]
                    dve.wait_ge(a1_in[tile // 2 % 2], 16 * (tile // 4 + 1))
                    if tile:
                        dve.wait_ge(diag_out, tile)
                    link(nc.vector.tensor_tensor(dgt[:], blk, ident[:], ALU.mult))
                    nc.vector.reduce_sum(dn[:, tile:tile + 1], dgt[:], AXL.X)
                    nc.vector.tensor_tensor(blk, blk, dgt[:], ALU.subtract).then_inc(diag_out, 1)
                    if g >= 1:
                        masks(g - 1, k)
                    for b in range(2, 4):
                        dve.wait_ge(tr1, 4 * tile + b + 1)
                        if k == 0 and b == 2 and g >= 2:
                            dve.wait_ge(at_out[g % 2], 16)
                            dve.wait_ge(ah_done, g - 1)
                        nc.vector.tensor_copy(atg[g % 2][:, 4 * b:4 * b + 4, k * P:(k + 1) * P],
                                              PS[:, b, :].rearrange("p (t i) -> p t i", i=P)).then_inc(ev1v, 1)
                if g >= 1:
                    rows_out(g - 1)
            for k in range(4):
                masks(NCH - 1, k)
            rows_out(NCH - 1)

            dve.wait_ge(l1_ev, 2 * NCH)
            link(nc.vector.tensor_reduce(flag[:], es[0:1, :], AXL.X, ALU.max))
            negative = dve.value_load(flag[:].bitcast(I32), min_val=0, max_val=0x7fffffff)
            for s in range(2):
                dve.wait_ge(at_out[s], 32)
            for q in range(24):
                dve.wait_ge(eb_act, q + 1)
                nc.vector.tensor_tensor(eb[:, q // 12, q // 4 % 3, q % 4 * CH:(q % 4 + 1) * CH], PS[:, q % 8, :],
                                        eb_stage[q % 2], ALU.min).then_inc(eb_dve, 1)
            dve.wait_ge(eb_dve, 24)

            def attention(signed):
                with dve.Fori(0, NT // 4) as it:
                    steps = [0]

                    def chain(ins):
                        steps[0] += 1
                        ins.then_inc(signed_step, 1)
                        dve.wait_ge(signed_step, it * 84 + steps[0])

                    def logits(k):
                        pair, h = k // 3, k % 3
                        if h == 0:
                            dve.wait_ge(a2_in[pair], it * 16 + 16)
                            for j in range(2):
                                blk = aw[pair][:, j, bass.ds((it * 4 + 2 * pair + j) * P, P)]
                                m = nc.vector.tensor_tensor(blk, blk, dgt[:], ALU.mult)
                            m.then_inc(offd_done, 1)
                            dve.wait_ge(offd_done, it * 2 + pair + 1)
                            for j in range(2):
                                m = nc.vector.tensor_scalar(bm[2 * pair + j], aw[pair][:, j, :], 0.0, MASKED, ALU.is_le,
                                                            ALU.mult)
                            m.then_inc(bm_done, 1)
                            dve.wait_ge(bm_done, it * 2 + pair + 1)
                        dve.wait_ge(tr2, it * 48 + 8 * k + 8)
                        dve.wait_ge(marked, it * 6 + k + 1)
                        nc.vector.memset(mk[:], 0.0).then_inc(marked, 1)
                        for j in range(2):
                            s = 2 * h + j
                            if not signed:
                                m = nc.vector.tensor_tensor_reduce(
                                    out=w[s], in0=bm[2 * pair + j], in1=eb[:, 0, h, :], scale=1.0, scalar=3.0e38,
                                    op0=ALU.add, op1=ALU.min, accum_out=ymin[:, s:s + 1])
                            else:
                                a = aw[pair][:, j, :]
                                chain(nc.vector.tensor_tensor(w[s], bm[2 * pair + j], eb[:, 0, h, :], ALU.add))
                                for half in range(2):
                                    cols = slice(half * N // 2, (half + 1) * N // 2)
                                    spare = PS[:, 6:8, :].rearrange("p b c -> p (b c)")
                                    chain(nc.vector.tensor_scalar(spare, a[:, cols], 0.0, MASKED, ALU.is_ge, ALU.mult))
                                    chain(nc.vector.tensor_tensor(spare, spare, eb[:, 1, h, cols], ALU.add))
                                    chain(nc.vector.tensor_tensor(w[s][:, cols], spare, w[s][:, cols], ALU.min))
                                m = nc.vector.tensor_reduce(ymin[:, s:s + 1], w[s], AXL.X, ALU.min)
                        m.then_inc(x_done, 1)

                    def weights(k):
                        pair, h = k // 3, k % 3
                        dve.wait_ge(exp_done, it * 6 + k + 1)
                        nc.vector.reciprocal(rz[:, 2 * h:2 * h + 2], zsum[:, 2 * h:2 * h + 2]).then_inc(rz_done, 1)
                        dve.wait_ge(rz_done, it * 6 + k + 1)
                        for j in range(2):
                            s = 2 * h + j
                            m = nc.vector.scalar_tensor_tensor(w[s], w[s], rz[:, s:s + 1], aw[pair][:, j, :], ALU.mult,
                                                               ALU.mult)
                        m.then_inc(q_done, 1)

                    logits(0)
                    for k in range(6):
                        if k < 5:
                            logits(k + 1)
                        weights(k)
                    assert steps[0] in (0, 84)

            link(nc.vector.tensor_scalar(dgt[:], ident[:], -1.0, 1.0, ALU.mult, ALU.add))
            with dve.If(negative != 0):
                attention(True)
            with dve.Else():
                attention(False)
            later_dve(dve, link)


_INS = ["x", "adj", "L0_gnn_gat_W", "L0_gnn_gat_a", "L0_gnn_edge_Wih", "L0_gnn_edge_Whh", "L0_gnn_edge_bih",
        "L0_gnn_edge_bhh", "L0_gnn_node_Wih", "L0_gnn_node_Whh", "L0_gnn_node_bih", "L0_gnn_node_bhh",
        "L1_gnn_neigh_W", "L1_gnn_lin_W", "L2_gnn_weight", "L2_gnn_a_l", "L2_gnn_a_r", "L2_gnn_b", "L3_gnn_gcn_w",
        "L3_gnn_gcn_b", "L3_gnn_ln_g", "L3_gnn_ln_b", "L3_gnn_w_in", "L3_gnn_conv_w", "L3_gnn_conv_b", "L3_gnn_w_xp",
        "L3_gnn_w_dt", "L3_gnn_b_dt", "L3_gnn_A_log", "L3_gnn_D_skip", "L3_gnn_w_out"]


def kernel(**inputs):
    import numpy as _np
    import concourse.bacc as _bacc
    from concourse import mybir as _mybir
    from concourse.bass_utils import run_bass_kernel_spmd as _run

    nc = _bacc.Bacc("TRN2", target_bir_lowering=False, num_devices=1)
    arrays, aps = {}, {}
    for name in _INS:
        a = _np.ascontiguousarray(inputs[name])
        arrays[f"in_{name}"] = a
        aps[name] = nc.dram_tensor(f"in_{name}", a.shape, _mybir.dt.from_np(a.dtype), kind="ExternalInput").ap()
    out = nc.dram_tensor("out_x", (N, P), F32, kind="ExternalOutput").ap()
    gnn_program(nc, aps, out)
    r = _run(nc, [arrays], core_ids=[0])
    return r.results[0]["out_x"]
```

```python
from contextlib import ExitStack

import numpy as np

import concourse.bass as bass
from concourse import mybir

ALU = mybir.AluOpType
ACT = mybir.ActivationFunctionType
AXL = mybir.AxisListType
F32 = mybir.dt.float32
BF16 = mybir.dt.bfloat16
I32 = mybir.dt.int32

P = 128
N = 2048
NT = N // P
CH = 512
NCH = N // CH
HEADS = 3
ROWS = 1 + 2 * 3 * HEADS
MASKED = 9.0e15
DI = 2
STATES = 16
DTR = 8
TAPS = 4
PAD = 4
LAST = 3

HW0 = 0
EBP0 = HW0 + HEADS * N
EBM0 = EBP0 + HEADS * N
W0 = EBM0 + HEADS * N
A20 = W0 + 6 * N
B20 = A20 + 4 * N
QT0 = B20 + 4 * N // 2
BIGW = QT0 + 4 * CH
ATG0 = EBP0
PM0 = ATG0 + 2 * NT * CH
X0 = NT * N
XT0 = X0 + N
A10 = XT0 + N
SC0 = XT0 + N
assert PM0 + NT * CH <= X0 and A10 + 4 * N <= BIGW and SC0 + 4 * N <= BIGW


def gnn_program(nc, t, out):
    ctx = ExitStack()
    with ctx:
        ctx.enter_context(nc.allow_non_contiguous_dma(reason="small weight vectors, laid out once"))

        def sb(name, shape, dt=F32):
            return ctx.enter_context(nc.sbuf_tensor(name, shape, dt))

        def sem(name):
            return ctx.enter_context(nc.semaphore(name))

        big = sb("big", [P, BIGW])
        PS = ctx.enter_context(nc.psum_tensor("PS", [P, 8, CH], F32))
        at_dram = nc.dram_tensor("at_dram", (N, N), F32, kind="Internal").ap()
        e_dram = nc.dram_tensor("e_dram", (6, N), F32, kind="Internal").ap()

        ns = sb("ns", [P, N])
        es = sb("es", [P, N])
        wt = sb("wt", [P, 15, P])
        ident = sb("ident", [P, P])
        smask = sb("smask", [P, 2, NT, 20], BF16)
        wa = sb("wa", [P, 6])
        ga = sb("ga", [P, HEADS, 2])
        war = sb("war", [P, 2])
        a2 = sb("a2", [P, 2])
        gb = sb("gb", [P, 4, 3])
        gbs = sb("gbs", [P, 2, 2])
        comb = sb("comb", [P, 2, HEADS])
        dn = sb("dn", [P, NT])
        deg = sb("deg", [P, NT])
        rdeg = sb("rdeg", [P, NT])
        degt = sb("degt", [P, 8])
        dgt = sb("dgt", [P, P])
        mk = sb("mk", [P, 1])
        flag = sb("flag", [1, 1])
        ymin = sb("ymin", [P, 6])
        zsum = sb("zsum", [P, 6])
        rz = sb("rz", [P, 6])
        stats = sb("stats", [P, NT, 6])
        mv = sb("mv", [P, NT, 2])
        rstd = sb("rstd", [P, NT])
        cst = sb("cst", [P, 2])
        elr = sb("elr", [P, NT, 2])
        bj = sb("bj", [P, NT])
        dj = sb("dj", [P, NT])
        ci = sb("ci", [P, NT])
        zi = sb("zi", [P, NT])
        conv_w = sb("conv_w", [P, DI, TAPS])
        conv_b = sb("conv_b", [P, DI])
        b_dt = sb("b_dt", [P, DI])
        dskip = sb("dskip", [P, DI])
        ln_g = sb("ln_g", [P, 1])
        ln_b = sb("ln_b", [P, 1])
        na = sb("na", [P, DI, STATES])
        state = sb("state", [P, STATES, DI])

        def region(at, words):
            return big[:, at:at + words]

        X = region(X0, N).rearrange("p (t f) -> p t f", f=P)
        XT = region(XT0, N)
        AT = region(0, NT * N).rearrange("p (t i) -> p t i", i=N)
        SC = region(SC0, 4 * N)
        raw = region(PM0, 19 * P).rearrange("p (b k) -> p b k", k=P)
        rawt = region(PM0 + 19 * P, 4 * P).rearrange("p (b k) -> p b k", k=P)
        upc = region(PM0 + 24 * P, 96).rearrange("p (t c) -> p t c", c=6)
        upb = region(PM0 + 25 * P, 48).bitcast(BF16).rearrange("p (t c) -> p t c", c=6)
        hw = region(HW0, HEADS * N).rearrange("p (t h f) -> p t h f", h=HEADS, f=P)
        a1 = [region(A10 + 2 * N * s, 2 * N).rearrange("p (t j) -> p t j", t=2) for s in range(2)]
        atg = [region(ATG0 + NT * CH * g, NT * CH).rearrange("p (t i) -> p t i", i=CH) for g in range(2)]
        pm = [region(PM0 + NT * CH // 2 * m, NT * CH // 2).bitcast(BF16).rearrange("p (t i) -> p t i", i=CH)
              for m in range(2)]
        e_rows = region(XT0, N)[0:6]
        eb = region(EBP0, 6 * N).rearrange("p (s h j) -> p s h j", s=2, h=HEADS)
        w = [region(W0 + N * k, N) for k in range(6)]
        aw = [region(A20 + 2 * N * s, 2 * N).rearrange("p (t j) -> p t j", t=2) for s in range(2)]
        bm = [region(B20 + N // 2 * k, N // 2).bitcast(BF16) for k in range(4)]
        qt = [region(QT0 + CH * k, CH) for k in range(4)]

        adj_tiles = t["adj"].rearrange("(t p) j -> p t j", p=P)
        at_tiles = at_dram.rearrange("(t p) i -> p t i", p=P)
        x_tiles = t["x"].rearrange("(t p) f -> p t f", p=P)

        x_in, gat_in, ga_in, raw_in, vec_in = sem("x_in"), sem("gat_in"), sem("ga_in"), sem("raw_in"), sem("vec_in")
        ident_ready = sem("ident_ready")
        su_mm, su_act, su_dve = sem("su_mm"), sem("su_act"), sem("su_dve")
        dch = sem("dch")
        a1_in = [sem("a1_in0"), sem("a1_in1")]
        diag_out, deg_done = sem("diag_out"), sem("deg_done")
        tr1, ev1a, ev1v = sem("tr1"), sem("ev1a"), sem("ev1v")
        masks_made, ah_done, e1_done, l1_ev = sem("masks_made"), sem("ah_done"), sem("e1_done"), sem("l1_ev")
        at_out = [sem("at_out0"), sem("at_out1")]
        comb_ready, eb_mm, eb_act, er_ready = sem("comb_ready"), sem("eb_mm"), sem("eb_act"), sem("er_ready")
        e_out, em_in, ep_in = sem("e_out"), sem("em_in"), [sem("ep_in%d" % h) for h in range(HEADS)]
        a2_in = [sem("a2_in0"), sem("a2_in1")]
        x_done, exp_done, q_done = sem("x_done"), sem("exp_done"), sem("q_done")
        tr2, qt_ready, qt_used = sem("tr2"), sem("qt_ready"), sem("qt_used")
        es_out, marked = sem("es_out"), sem("marked")
        offd_done, bm_done, rz_done, signed_step = sem("offd_done"), sem("bm_done"), sem("rz_done"), sem("signed_step")
        at_in, diag_back = sem("at_in"), sem("diag_back")
        xt_mm, xt_ev = sem("xt_mm"), sem("xt_ev")
        gru_mm, gate, tanh_in, tanh_out, gru_out = (sem("gru_mm"), sem("gate"), sem("tanh_in"), sem("tanh_out"),
                                                    sem("gru_out"))
        st_mm, res = sem("st_mm"), sem("res")
        var_ready, std_ready, x_ready = sem("var_ready"), sem("std_ready"), sem("x_ready")
        out_sem = sem("out_sem")
        b2_in = sem("b2_in")
        b_mm = sem("b_mm")
        bb_ready = sem("bb_ready")
        c_mm = sem("c_mm")
        conv_done = sem("conv_done")
        da_ready = sem("da_ready")
        dbc_ev = sem("dbc_ev")
        dbc_mm = sem("dbc_mm")
        dbu_ready = sem("dbu_ready")
        dt_mm = sem("dt_mm")
        dt_ready = sem("dt_ready")
        du_ready = sem("du_ready")
        gru_step = sem("gru_step")
        h_ready = sem("h_ready")
        hc_ready = sem("hc_ready")
        ht_ev = sem("ht_ev")
        l1_a = sem("l1_a")
        l1_add = sem("l1_add")
        l1_aev = sem("l1_aev")
        l1_b = sem("l1_b")
        l1_h = sem("l1_h")
        l1_hev = sem("l1_hev")
        l1_mm = sem("l1_mm")
        l2_aev = sem("l2_aev")
        l2_b = sem("l2_b")
        l2_mm = sem("l2_mm")
        l2_rb = sem("l2_rb")
        l2_rbev = sem("l2_rbev")
        l2_v = sem("l2_v")
        l2_vec = sem("l2_vec")
        l2_x = sem("l2_x")
        l2_xev = sem("l2_xev")
        l3_aev = sem("l3_aev")
        l3_g = sem("l3_g")
        l3_gev = sem("l3_gev")
        l3_mm = sem("l3_mm")
        na_exp = sem("na_exp")
        na_ready = sem("na_ready")
        o_mm = sem("o_mm")
        ones_ready = sem("ones_ready")
        pad_ready = sem("pad_ready")
        pieces_ready = sem("pieces_ready")
        q2_added = sem("q2_added")
        q2_ready = sem("q2_ready")
        q2_used = sem("q2_used")
        scan_done = sem("scan_done")
        sel_ready = sem("sel_ready")
        sp_act = sem("sp_act")
        sp_exp = sem("sp_exp")
        sp_ln = sem("sp_ln")
        state_saved = sem("state_saved")
        sums_read = sem("sums_read")
        u_ready = sem("u_ready")
        w2_in = sem("w2_in")
        w3_in = sem("w3_in")
        w4_in = sem("w4_in")
        walb_ready = sem("walb_ready")
        x_plus_b = sem("x_plus_b")
        xps_ready = sem("xps_ready")
        xz_ev = sem("xz_ev")
        xz_mm = sem("xz_mm")
        y_done = sem("y_done")
        y_mm = sem("y_mm")
        yg_ready = sem("yg_ready")
        block = ctx.enter_context(nc.Block())


        def transpose_into(bank, col, src):
            return nc.tensor.transpose(PS[:, bank, col:col + P], src, ident[:])

        H1, AHT = SC[:, 0:N], SC[:, N:2 * N]
        q2 = [SC[:, N * k:N * (k + 1)] for k in range(4)]
        gate_r, gate_z, gru_t, gru_n = ([SC[:, CH * (2 * k + g):CH * (2 * k + g + 1)] for g in range(2)] for k in range(4))
        gru_s = SC[:, 8 * CH:9 * CH]
        walb, b2b = wt[:, 0, :], wt[:, 1, :]
        gcn_w, w_in = wt[:, 2, :], wt[:, 3:7, :]
        w_out, gcn_b, ones_row = wt[:, 7:9, :], wt[0:1, 9, :], wt[0:1, 10, :]
        at = 0

        def late(words, dt=F32):
            nonlocal at
            at += words
            v = region(at - words, words)
            return v if dt == F32 else v.bitcast(dt)

        xc = late(DI * (N + PAD)).rearrange("p (b t) -> p b t", b=DI)
        u, zg, dt_, du = (late(DI * N).rearrange("p (b t) -> p b t", b=DI) for _ in range(4))
        dbc, rest = late(N), late(N)
        mid, pieces = late(N // 2, BF16), late(N // 2, BF16)
        sel = late(32 * P // 2, BF16).rearrange("p (n m) -> p n m", m=P)
        xps = late(DI * 104).rearrange("p (b c) -> p b c", b=DI)
        w_xp = late(DI * 40).rearrange("p (b c) -> p b c", b=DI)
        w_dt = late(DI * P)
        assert at <= NT * N
        tmp = xc[:, :, 0:N]
        yg = tmp
        pairs = [SC[:, k * 2 * CH:(k + 1) * 2 * CH].rearrange("p (b t) -> p b t", b=DI) for k in range(7)]
        hs, hc, dbu = pairs[0:2], pairs[2:4], pairs[4:7]
        bb = [SC[:, (14 + s) * CH:(15 + s) * CH] for s in range(2)]
        xtiles = X.rearrange("p t f -> p (t f)")

        POOL_TILES = [jt for jt in range(NT) if jt % 4 < 3 and jt < NT - 2]

        def act_copy(o, i, **kw):
            return nc.scalar.activation(o, i, ACT.Copy, **kw)

        def later_loads(sp):
            sp.dma_start(dgt[:], t["L2_gnn_weight"]).then_inc(w2_in, 16)
            if True:
                sp.wait_ge(gru_out, 10)
                sp.dma_start(b2b, t["L2_gnn_b"].partition_broadcast(P)).then_inc(b2_in, 16)
                sp.dma_start(gcn_w, t["L3_gnn_gcn_w"]).then_inc(w3_in, 16)
                sp.dma_start(w_in, t["L3_gnn_w_in"].rearrange("k (b m) -> k b m", m=P)).then_inc(w3_in, 16)
                sp.dma_start(w_out, t["L3_gnn_w_out"].rearrange("(b d) m -> d b m", d=P)).then_inc(w3_in, 16)
                sp.dma_start(gcn_b, t["L3_gnn_gcn_b"].rearrange("(o f) -> o f", o=1)).then_inc(w3_in, 16)
                sp.dma_start(ln_g[:], t["L3_gnn_ln_g"].rearrange("(f o) -> f o", o=1)).then_inc(w3_in, 16)
                sp.dma_start(ln_b[:], t["L3_gnn_ln_b"].rearrange("(f o) -> f o", o=1)).then_inc(w3_in, 16)
                sp.dma_start(conv_w[:], t["L3_gnn_conv_w"].rearrange("(b d) k -> d b k", d=P)).then_inc(w3_in, 16)
                sp.dma_start(na[:], t["L3_gnn_A_log"].rearrange("(b d) k -> d b k", d=P)).then_inc(w3_in, 16)
                for name, v in (("conv_b", conv_b), ("b_dt", b_dt), ("D_skip", dskip)):
                    sp.dma_start(v[:], t["L3_gnn_" + name].rearrange("(b d) -> d b", d=P)).then_inc(w3_in, 16)
            if LAST >= 3:
                sp.wait_ge(l3_mm, 4)
                sp.dma_start(w_xp, t["L3_gnn_w_xp"].rearrange("(b d) k -> d b k", d=P)).then_inc(w4_in, 16)
                sp.dma_start(w_dt[96:96 + DTR, :], t["L3_gnn_w_dt"]).then_inc(w4_in, 16)
            out_tiles = out.rearrange("(t p) f -> p t f", p=P)
            for q in range(4):
                sp.wait_ge(x_ready, 12 + q + 1)
                sp.dma_start(out_tiles[:, 4 * q:4 * q + 4, :], X[:, 4 * q:4 * q + 4, :]).then_inc(out_sem, 16)
            sp.wait_ge(out_sem, 64)

        def later_pool(pool):
            if True:
                pool.wait_ge(b2_in, 16)
                pool.wait_ge(xt_ev, 12)
                nc.gpsimd.tensor_tensor(X, X, b2b.unsqueeze(1).to_broadcast([P, NT, P]), ALU.add).then_inc(x_plus_b, 1)
                pool.wait_ge(l2_x, 4)
                pool.wait_ge(l2_v, 1)
                for m, jt in enumerate(POOL_TILES):
                    if m:
                        pool.wait_ge(q2_ready, jt + 1)
                        if m > 1:
                            pool.wait_ge(q2_added, m - 1)
                        nc.gpsimd.tensor_tensor(XT, q2[0] if m == 1 else XT, q2[jt % 4], ALU.add).then_inc(q2_added, 1)
            if LAST >= 3:
                pool.wait_ge(l3_mm, 4)
                nc.gpsimd.memset(xc[:, :, 0:PAD], 0.0).then_inc(pad_ready, 1)
                nc.gpsimd.memset(sel[0:96], 0.0).then_inc(sel_ready, 1)
                for p in range(3):
                    pool.wait_ge(sel_ready, p + 1)
                    nc.gpsimd.affine_select(out=sel[0:96], in_=sel[0:96], compare_op=ALU.not_equal, fill=1.0,
                                            base=-32 * p, pattern=[[-1, 32], [0, P]],
                                            channel_multiplier=1).then_inc(sel_ready, 1)
                pool.wait_ge(du_ready, DI)
                for k in range(STATES * NCH):
                    c = k // STATES
                    pool.wait_ge(bb_ready, k + 1)
                    if k >= 3:
                        pool.wait_ge(scan_done, k - 2)
                    nc.gpsimd.tensor_tensor(dbu[k % 3], du[:, :, c * CH:(c + 1) * CH],
                                            bb[k % 2].unsqueeze(1).to_broadcast([P, DI, CH]),
                                            ALU.mult).then_inc(dbu_ready, 1)

        def later_act(act):
            def root(k, q):
                act.wait_ge(var_ready, 4 * k + q + 1)
                nc.scalar.activation(rstd[:, 4 * q:4 * q + 4], mv[:, 4 * q:4 * q + 4, 1], ACT.Sqrt,
                                     bias=cst[:, 0:1]).then_inc(std_ready, 1)

            def xt_copy(r, q, bank):
                act.wait_ge(xt_mm, 4 * r + q + 1)
                act_copy(XT[:, q * CH:(q + 1) * CH], PS[:, bank, :]).then_inc(xt_ev, 1)

            def evac(mm, count, dst, q, bank, done):
                act.wait_ge(mm, count)
                act_copy(dst[:, q * CH:(q + 1) * CH], PS[:, bank, :]).then_inc(done, 1)

            for q in range(2):
                xt_copy(0, q, q)
            act.sem_inc(tanh_out, 2)
            with act.Fori(0, NCH) as c:
                for g in range(2):
                    act.wait_ge(gru_mm, c * 2 + g + 1)
                    act.wait_ge(gru_out, c * 2 + g + 1)
                    nc.scalar.activation(gate_r[g], PS[:, 4 * g, :], ACT.Sigmoid, bias=gbs[:, g, 0:1])
                    nc.scalar.activation(gate_z[g], PS[:, 4 * g + 1, :], ACT.Sigmoid, bias=gbs[:, g, 1:2]).then_inc(gate, 1)
                    act.wait_ge(tanh_in, c * 2 + g + 1)
                    nc.scalar.activation(gru_n[g], gru_t[g], ACT.Tanh, bias=gb[:, 2 * g, 2:3]).then_inc(tanh_out, 1)
            root(0, 0)
            xt_copy(1, 0, 4)
            root(0, 1)
            evac(l1_h, 1, H1, 0, 4, l1_hev)
            xt_copy(1, 1, 5)
            root(0, 2)
            evac(l1_h, 2, H1, 1, 5, l1_hev)
            root(0, 3)
            for q in range(2, 4):
                xt_copy(1, q, 4 + q)
                evac(l1_h, q + 1, H1, q, 4 + q, l1_hev)
            for q in range(4):
                evac(l1_mm, q + 1, AHT, q, q, l1_aev)
            def right_factor(q):
                act.wait_ge(l2_rb, q + 1)
                nc.scalar.activation(es[:, q * CH:(q + 1) * CH], PS[:, (5 + q) if q < 3 else 0, :], ACT.Exp,
                                     scale=0.8).then_inc(l2_rbev, 1)

            root(1, 0)
            for q in range(3):
                xt_copy(2, q, q)
                root(1, q + 1)
                if q:
                    evac(l2_x, q, ns, q - 1, q - 1, l2_xev)
            right_factor(0)
            xt_copy(2, 3, 3)
            evac(l2_x, 3, ns, 2, 2, l2_xev)
            right_factor(1)
            right_factor(2)
            right_factor(3)
            act.wait_ge(l2_v, 1)
            for dst, src, sc in ((bj, 1, 1.0), (dj, 1, 0.2), (ci, 0, 0.2)):
                nc.scalar.activation(dst[:], PS[:, 4, 0:2 * NT].rearrange("p (t s) -> p t s", s=2)[:, :, src], ACT.Exp,
                                     scale=sc).then_inc(l2_vec, 1)
            evac(l2_x, 4, ns, 3, 3, l2_xev)
            act.wait_ge(q2_added, POOL_TILES.index(NT - 4))
            for q in range(4):
                evac(l2_mm, q + 1, q2[0], q, q, l2_aev)
            for q in range(4):
                root(2, q)
            def relu(q):
                act.wait_ge(l3_g, q + 1)
                nc.scalar.activation(H1[:, q * CH:(q + 1) * CH], PS[:, 4 + q, :], ACT.Relu).then_inc(l3_gev, 1)

            def ht_copy(q):
                act.wait_ge(xt_mm, 12 + q + 1)
                nc.scalar.activation(es[:, q * CH:(q + 1) * CH], PS[:, q, :], ACT.Identity, scale=ln_g[:],
                                     bias=ln_b[:]).then_inc(ht_ev, 1)

            for q in range(4):
                evac(l3_mm, q + 1, AHT, q, q, l3_aev)
            relu(0)
            root(3, 0)
            relu(1)
            relu(2)
            root(3, 1)
            ht_copy(0)
            relu(3)
            root(3, 2)
            ht_copy(1)
            root(3, 3)
            ht_copy(2)
            ht_copy(3)
            for c in range(4):
                for m in range(4):
                    k = 4 * c + m
                    act.wait_ge(xz_mm, k + 1)
                    if m < 2:
                        act_copy(xc[:, m, PAD + c * CH:PAD + (c + 1) * CH], PS[:, k % 8, :]).then_inc(xz_ev, 1)
                    else:
                        nc.scalar.activation(zg[:, m - 2, c * CH:(c + 1) * CH], PS[:, k % 8, :], ACT.Silu).then_inc(xz_ev, 1)
            for b in range(DI):
                act.wait_ge(conv_done, b + 1)
                nc.scalar.activation(u[:, b, :], u[:, b, :], ACT.Silu, bias=conv_b[:, b:b + 1]).then_inc(u_ready, 1)
            act.wait_ge(w3_in, 16 * 11)
            nc.scalar.activation(na[:], na[:], ACT.Exp).then_inc(na_exp, 1)
            for b in range(DI):
                src = PS[:, 4 * b:4 * b + 4, :].rearrange("p c t -> p (c t)")
                act.wait_ge(dt_mm, b + 1)
                nc.scalar.activation(tmp[:, b, :], src, ACT.Abs, bias=b_dt[:, b:b + 1]).then_inc(sp_act, 1)
                nc.scalar.activation(dt_[:, b, :], src, ACT.Relu, bias=b_dt[:, b:b + 1]).then_inc(sp_act, 1)
            for b in range(DI):
                act.wait_ge(sp_act, 2 * b + 1)
                nc.scalar.activation(tmp[:, b, :], tmp[:, b, :], ACT.Exp, scale=-1.0).then_inc(sp_exp, 1)
            for b in range(DI):
                act.wait_ge(sp_exp, b + 1)
                nc.scalar.activation(tmp[:, b, :], tmp[:, b, :], ACT.Ln, bias=1.0).then_inc(sp_ln, 1)
            act.wait_ge(na_ready, 1)
            act.wait_ge(dt_ready, DI)

            def copy_b(k):
                act.wait_ge(b_mm, k + 1)
                if k >= 2:
                    act.wait_ge(dbu_ready, k - 1)
                act_copy(bb[k % 2], PS[:, 0, :]).then_inc(bb_ready, 1)

            def decay(k):
                c, n = k // STATES, k % STATES
                if k >= 2:
                    act.wait_ge(scan_done, k - 1)
                for b in range(DI):
                    e = nc.scalar.activation(PS[:, 4 + 2 * (k % 2) + b, :], dt_[:, b, c * CH:(c + 1) * CH], ACT.Exp,
                                             scale=na[:, b, n:n + 1])
                e.then_inc(da_ready, 1)

            copy_b(0)
            decay(0)
            copy_b(1)
            for k in range(STATES * NCH):
                if k + 1 < STATES * NCH:
                    decay(k + 1)
                if k + 2 < STATES * NCH:
                    copy_b(k + 2)
            for q in range(4):
                root(4, q)

        def later_pe(pe):
            def xt_fill(r, q, bank, src):
                for b in range(4):
                    m = transpose_into(bank, b * P, src[:, 4 * q + b, :])
                m.then_inc(xt_mm, 1)

            def adjacency_product(weights, q, done):
                pe.wait_ge(diag_back, q + 1)
                for jt in range(4 * q, 4 * q + 4):
                    for c in range(NCH):
                        m = nc.tensor.matmul(PS[:, c, :], weights[:, jt, :], AT[:, jt, c * CH:(c + 1) * CH],
                                             start=(jt == 0), stop=(jt == NT - 1))
                        if jt == NT - 1:
                            m.then_inc(done, 1)

            def tiles_product(q, bank, left, right, done):
                for jt in range(4 * q, 4 * q + 4):
                    m = nc.tensor.matmul(PS[:, bank, jt % 4 * P:(jt % 4 + 1) * P], left[:, jt * P:(jt + 1) * P], right,
                                         start=True, stop=True)
                m.then_inc(done, 1)

            pe.wait_ge(x_in, 32)
            pe.wait_ge(es_out, 2 + NT // 2)
            for q in range(4):
                xt_fill(0, q, q, X)
            pe.wait_ge(xt_ev, 4)
            with pe.Fori(0, NCH) as c:
                for g in range(2):
                    pe.wait_ge(tanh_out, c * 2 + g + 1)
                    xs = (ns, es)[g][:, bass.ds(c * CH, CH)]
                    hx = XT[:, bass.ds(c * CH, CH)]
                    wi, wh = 6 * g, 6 * g + 3
                    for gate_no in range(2):
                        nc.tensor.matmul(PS[:, 4 * g + gate_no, :], wt[:, wi + gate_no, :], xs, start=True, stop=False)
                        nc.tensor.matmul(PS[:, 4 * g + gate_no, :], wt[:, wh + gate_no, :], hx, start=False, stop=True)
                    nc.tensor.matmul(PS[:, 4 * g + 2, :], wt[:, wi + 2, :], xs, start=True, stop=True)
                    nc.tensor.matmul(PS[:, 4 * g + 3, :], wt[:, wh + 2, :], hx, start=True, stop=True).then_inc(gru_mm, 1)
            pe.wait_ge(gru_out, 2 + 8)
            nst = ns[:].rearrange("p (t i) -> p t i", i=P)
            for q in range(4):
                for b in range(4):
                    m = transpose_into(4 + q, b * P, nst[:, 4 * q + b, :])
                m.then_inc(st_mm, 1)
            hj = H1.rearrange("p (t f) -> p t f", f=P)

            def features(q):
                pe.wait_ge(x_ready, q + 1)
                xt_fill(1, q, 4 + q, X)
                pe.wait_ge(xt_ev, 4 + q + 1)
                tiles_product(q, 4 + q, XT, wt[:, 12, :], l1_h)

            features(0)
            features(1)
            pe.wait_ge(l1_hev, 1)
            adjacency_product(hj, 0, l1_mm)
            features(2)
            features(3)
            pe.wait_ge(l1_hev, 4)
            adjacency_product(hj, 1, l1_mm)
            for q in range(4):
                tiles_product(q, 4 + q, XT, wt[:, 13, :], l1_a)
            adjacency_product(hj, 2, l1_mm)
            adjacency_product(hj, 3, l1_mm)
            for q in range(4):
                pe.wait_ge(l1_aev, q + 1)
                tiles_product(q, q, AHT, wt[:, 14, :], l1_b)
            pe.wait_ge(w2_in, 16)
            pe.wait_ge(walb_ready, 1)
            pe.wait_ge(l1_add, 4)
            for q in range(4):
                pe.wait_ge(x_ready, 4 + q + 1)
                xt_fill(2, q, q, X)
                pe.wait_ge(xt_ev, 8 + q + 1)
                if q == 3:
                    pe.wait_ge(l2_xev, 1)
                nc.tensor.matmul(PS[:, (5 + q) if q < 3 else 0, :], walb, XT[:, q * CH:(q + 1) * CH], start=True,
                                 stop=True).then_inc(l2_rb, 1)
                for jt in range(4 * q, 4 * q + 4):
                    m = nc.tensor.matmul(PS[:, 4, 2 * jt:2 * jt + 2], XT[:, jt * P:(jt + 1) * P], war[:], start=True,
                                         stop=True)
                if q == 3:
                    m.then_inc(l2_v, 1)
                tiles_product(q, q, XT, dgt[:], l2_x)
            pe.wait_ge(l2_xev, 4)
            pe.wait_ge(l2_rbev, 4)
            pe.wait_ge(l2_vec, 3)
            x2 = ns[:].rearrange("p (t f) -> p t f", f=P)

            def add_rows(tile, last):
                for it in range(NT):
                    m = nc.tensor.matmul(PS[:, 4, it:it + 1], tile[:, it * P:(it + 1) * P], cst[:, 1:2], start=False,
                                         stop=(last and it == NT - 1))
                return m

            nc.tensor.matmul(PS[:, 4, 0:NT], ident[:], zi[:], start=True, stop=False)
            for jt in range(NT):
                if jt == NT - 1:
                    pe.wait_ge(q2_added, len(POOL_TILES) - 1)
                    add_rows(XT, False)
                pe.wait_ge(q2_ready, jt + 1)
                for c in range(NCH):
                    m = nc.tensor.matmul(PS[:, c, :], x2[:, jt, :], q2[jt % 4][:, c * CH:(c + 1) * CH], start=(jt == 0),
                                         stop=(jt == NT - 1))
                    if jt == NT - 1:
                        m.then_inc(l2_mm, 1)
                if jt not in POOL_TILES:
                    m = add_rows(q2[jt % 4], jt == NT - 1)
                m.then_inc(q2_used, 1)
            nt = q2[0].rearrange("p (t i) -> p t i", i=P)
            for q in range(4):
                pe.wait_ge(l2_aev, q + 1)
                if q == 3:
                    pe.wait_ge(sums_read, 1)
                for b in range(4):
                    m = transpose_into(4 + (q + 1) % 4, b * P, nt[:, 4 * q + b, :])
                m.then_inc(l2_b, 1)
            for q in range(4):
                pe.wait_ge(x_ready, 8 + q + 1)
                adjacency_product(X, q, l3_mm)
            pe.wait_ge(w3_in, 16 * 11)
            pe.wait_ge(ones_ready, 1)
            for q in range(4):
                pe.wait_ge(l3_aev, q + 1)
                for it in range(4 * q, 4 * q + 4):
                    o = PS[:, 4 + q, it % 4 * P:(it % 4 + 1) * P]
                    nc.tensor.matmul(o, AHT[:, it * P:(it + 1) * P], gcn_w, start=True, stop=False)
                    m = nc.tensor.matmul(o, ones_row, gcn_b, start=False, stop=True)
                m.then_inc(l3_g, 1)
            for q in range(4):
                pe.wait_ge(h_ready, q + 1)
                xt_fill(3, q, q, hj)
            for c in range(4):
                pe.wait_ge(ht_ev, c + 1)
                for m_ in range(4):
                    k = 4 * c + m_
                    if k >= 8:
                        pe.wait_ge(xz_ev, k - 7)
                    elif k < 4:
                        pe.wait_ge(ht_ev, 4)
                    nc.tensor.matmul(PS[:, k % 8, :], w_in[:, m_, :], es[:, c * CH:(c + 1) * CH], start=True,
                                     stop=True).then_inc(xz_mm, 1)
            pe.wait_ge(xz_ev, 16)
            pe.wait_ge(u_ready, DI)
            pe.wait_ge(xps_ready, 1)
            for c in range(NCH):
                for b in range(DI):
                    m = nc.tensor.matmul(PS[0:104, c, :], xps[:, b, :], u[:, b, c * CH:(c + 1) * CH], start=(b == 0),
                                         stop=(b == 1))
                m.then_inc(dbc_mm, 1)
            pe.wait_ge(dbc_ev, 4)
            for b in range(DI):
                for c in range(NCH):
                    m = nc.tensor.matmul(PS[:, 4 * b + c, :], w_dt[96:96 + DTR, b * P:(b + 1) * P],
                                         dbc[96:96 + DTR, c * CH:(c + 1) * CH], start=True, stop=True)
                m.then_inc(dt_mm, 1)
            pe.wait_ge(sp_act, 4)
            pe.wait_ge(pieces_ready, 1)
            pe.wait_ge(sel_ready, 4)

            def add_up(k):
                c, n = k // STATES, k % STATES
                pe.wait_ge(hc_ready, k + 1)
                if n == 0 and c:
                    pe.wait_ge(y_done, c)
                for b in range(DI):
                    m = nc.tensor.matmul(PS[:, 2 + b, :], ident[:], hc[k % 2][:, b, :], start=(n == 0),
                                         stop=(n == STATES - 1))
                m.then_inc(y_mm, 1)

            def spread(k, bank, row, done):
                c = k // STATES
                nc.tensor.matmul(PS[:, bank, :], sel[0:96, row + k % STATES, :], pieces[0:96, c * CH:(c + 1) * CH],
                                 start=True, stop=True).then_inc(done, 1)

            spread(0, 0, 0, b_mm)
            pe.wait_ge(bb_ready, 1)
            spread(1, 0, 0, b_mm)
            for k in range(STATES * NCH):
                if k + 2 < STATES * NCH:
                    pe.wait_ge(bb_ready, k + 2)
                    spread(k + 2, 0, 0, b_mm)
                if k:
                    pe.wait_ge(hc_ready, k)
                spread(k, 1, STATES, c_mm)
                if k:
                    add_up(k - 1)
            add_up(STATES * NCH - 1)
            for q in range(4):
                pe.wait_ge(yg_ready, q + 1)
                if q == 0:
                    pe.wait_ge(scan_done, STATES * NCH)
                for s in range(4):
                    it = 4 * q + s
                    for b in range(DI):
                        m = nc.tensor.matmul(PS[:, 4 + q, s * P:(s + 1) * P], yg[:, b, it * P:(it + 1) * P], w_out[:, b, :],
                                             start=(b == 0), stop=(b == 1))
                m.then_inc(o_mm, 1)

        def later_dve(dve, link):
            def norm(k, v, ready, residual):
                def scale(q):
                    dve.wait_ge(std_ready, 4 * k + q + 1)
                    link(nc.vector.reciprocal(rstd[:, 4 * q:4 * q + 4], rstd[:, 4 * q:4 * q + 4]))
                    for i in range(4 * q, 4 * q + 4):
                        m = nc.vector.tensor_scalar(v[:, i, :], v[:, i, :], mv[:, i, 0:1], rstd[:, i:i + 1],
                                                    ALU.subtract, ALU.mult)
                    m.then_inc(ready, 1)

                for q in range(4):
                    residual(q)
                    if q:
                        scale(q - 1)
                    for i in range(4 * q, 4 * q + 4):
                        m = nc.vector.bn_stats(stats[:, i, :], v[:, i, :])
                    link(m)
                    for i in range(4 * q, 4 * q + 4):
                        m = nc.vector.bn_aggr(mv[:, i, :], stats[:, i, :])
                    m.then_inc(var_ready, 1)
                scale(3)

            def add_scaled(q, bank, factors):
                for i in range(4 * q, 4 * q + 4):
                    m = nc.vector.scalar_tensor_tensor(X[:, i, :], PS[:, bank, i % 4 * P:(i % 4 + 1) * P],
                                                       factors[:, i:i + 1], X[:, i, :], ALU.mult, ALU.add)
                link(m)

            def add_bank(q):
                return nc.vector.tensor_tensor(xtiles[:, q * CH:(q + 1) * CH], PS[:, 4 + q, :],
                                               xtiles[:, q * CH:(q + 1) * CH], ALU.add)

            for q in range(2, 4):
                dve.wait_ge(xt_mm, q + 1)
                nc.vector.tensor_copy(XT[:, q * CH:(q + 1) * CH], PS[:, q, :]).then_inc(xt_ev, 1)
            dve.sem_inc(gru_out, 2)
            with dve.Fori(0, NCH) as c:
                steps = [0]

                def chain(ins):
                    steps[0] += 1
                    ins.then_inc(gru_step, 1)
                    dve.wait_ge(gru_step, c * 7 + steps[0])

                for g in range(2):
                    dve.wait_ge(gate, c * 2 + g + 1)
                    chain(nc.vector.scalar_tensor_tensor(gru_t[g], PS[:, 4 * g + 3, :], gb[:, 2 * g + 1, 2:3], gate_r[g],
                                                         ALU.add, ALU.mult))
                    nc.vector.tensor_tensor(gru_t[g], PS[:, 4 * g + 2, :], gru_t[g], ALU.add).then_inc(tanh_in, 1)
                    dve.wait_ge(tanh_out, c * 2 + g + 3)
                    chain(nc.vector.tensor_tensor(gru_t[g], XT[:, bass.ds(c * CH, CH)], gru_n[g], ALU.subtract))
                    chain(nc.vector.tensor_tensor(gru_t[g], gru_t[g], gate_z[g], ALU.mult))
                    if g == 0:
                        nc.vector.tensor_tensor(gru_s, gru_t[0], gru_n[0], ALU.add).then_inc(gru_out, 1)
                    else:
                        chain(nc.vector.tensor_tensor(gru_t[1], gru_t[1], gru_n[1], ALU.add))
                        nc.vector.tensor_tensor(ns[:, bass.ds(c * CH, CH)], gru_t[1], gru_s, ALU.add).then_inc(gru_out, 1)
                assert steps[0] == 7
            for jt in range(NT):
                blk = AT[:, jt, jt * P:(jt + 1) * P]
                if jt % 4 == 0:
                    dve.wait_ge(at_in, 16 * NCH)
                m = nc.vector.scalar_tensor_tensor(blk, ident[:], dn[:, jt:jt + 1], blk, ALU.mult, ALU.add)
                if jt % 4 == 3:
                    m.then_inc(diag_back, 1)
            nc.vector.tensor_copy(walb, war[:, 0:1].to_broadcast([P, P])).then_inc(walb_ready, 1)
            nc.vector.memset(zi[:], 0.0)
            nc.vector.memset(ones_row, 1.0).then_inc(ones_ready, 1)
            link(nc.vector.scalar_tensor_tensor(rdeg[:], deg[:], 1.0, dn[:], ALU.add, ALU.add))
            link(nc.vector.reciprocal(rdeg[:], rdeg[:]))

            def after_gru(q):
                dve.wait_ge(st_mm, q + 1)
                add_scaled(q, 4 + q, dn)

            norm(0, X, x_ready, after_gru)
            for q in range(4):
                dve.wait_ge(l1_a, q + 1)
                m = add_bank(q)
                m.then_inc(l1_add, 1)
            dve.wait_ge(l1_add, 4)

            def after_layer1(q):
                dve.wait_ge(l1_b, q + 1)
                add_scaled(q, q, rdeg)

            norm(1, X, x_ready, after_layer1)
            dve.wait_ge(l2_vec, 3)
            dve.wait_ge(l2_rbev, 4)
            for jt in range(NT):
                if jt >= 4:
                    dve.wait_ge(q2_used, jt - 3)
                    if jt - 4 in POOL_TILES:
                        dve.wait_ge(q2_added, max(POOL_TILES.index(jt - 4), 1))
                link(nc.vector.tensor_scalar(q2[jt % 4], es[:], bj[:, jt:jt + 1], dj[:, jt:jt + 1], ALU.mult, ALU.max))
                nc.vector.scalar_tensor_tensor(q2[jt % 4], AT[:, jt, :], 0.0, q2[jt % 4], ALU.not_equal,
                                               ALU.mult).then_inc(q2_ready, 1)
            dve.wait_ge(q2_used, NT)
            nc.vector.tensor_tensor(zi[:], PS[:, 4, 0:NT], ci[:], ALU.mult).then_inc(sums_read, 1)
            dve.wait_ge(sums_read, 1)
            link(nc.vector.tensor_scalar(zi[:], zi[:], 1e-12, None, ALU.max))
            link(nc.vector.reciprocal(zi[:], zi[:]))
            link(nc.vector.tensor_tensor(zi[:], zi[:], ci[:], ALU.mult))
            dve.wait_ge(x_plus_b, 1)

            def after_layer2(q):
                dve.wait_ge(l2_b, q + 1)
                add_scaled(q, 4 + (q + 1) % 4, zi)

            norm(2, X, x_ready, after_layer2)
            norm(3, H1.rearrange("p (t f) -> p t f", f=P), h_ready, lambda q: dve.wait_ge(l3_gev, q + 1))
            dve.wait_ge(w4_in, 32)
            for k in range(3):
                nc.vector.tensor_copy(xps[:, :, 32 * k:32 * (k + 1)], w_xp[:, :, DTR:DTR + 32])
            nc.vector.tensor_copy(xps[:, :, 96:104], w_xp[:, :, 0:DTR]).then_inc(xps_ready, 1)
            dve.wait_ge(pad_ready, 1)
            dve.wait_ge(xz_ev, 16)
            for k in range(TAPS):
                for b in range(DI):
                    src = xc[:, b, PAD - 3 + k:PAD - 3 + k + N]
                    if k == 0:
                        m = nc.vector.tensor_scalar(u[:, b, :], src, conv_w[:, b, 0:1], None, ALU.mult)
                    else:
                        m = nc.vector.scalar_tensor_tensor(u[:, b, :], src, conv_w[:, b, k:k + 1], u[:, b, :], ALU.mult,
                                                           ALU.add)
                    if k == TAPS - 1:
                        m.then_inc(conv_done, 1)
                    elif b == 1:
                        link(m)
            dve.wait_ge(na_exp, 1)
            nc.vector.tensor_scalar(na[:], na[:], -1.0, None, ALU.mult).then_inc(na_ready, 1)
            nc.vector.memset(state[:], 0.0).then_inc(state_saved, 1)
            for c in range(4):
                dve.wait_ge(dbc_mm, c + 1)
                nc.vector.tensor_copy(dbc[0:104, c * CH:(c + 1) * CH], PS[0:104, c, :]).then_inc(dbc_ev, 1)
            dve.wait_ge(dbc_ev, 4)
            link(nc.vector.tensor_copy(pieces[0:96], dbc[0:96]))
            link(nc.vector.tensor_tensor(rest[0:96], dbc[0:96], pieces[0:96], ALU.subtract))
            link(nc.vector.tensor_copy(mid[0:96], rest[0:96]))
            link(nc.vector.tensor_copy(pieces[32:64], mid[32:64]))
            link(nc.vector.tensor_tensor(rest[64:96], rest[64:96], mid[64:96], ALU.subtract))
            nc.vector.tensor_copy(pieces[64:96], rest[64:96]).then_inc(pieces_ready, 1)
            for b in range(DI):
                dve.wait_ge(sp_ln, b + 1)
                nc.vector.tensor_tensor(dt_[:, b, :], dt_[:, b, :], tmp[:, b, :], ALU.add).then_inc(dt_ready, 1)
            for b in range(DI):
                dve.wait_ge(dt_ready, b + 1)
                nc.vector.tensor_tensor(du[:, b, :], dt_[:, b, :], u[:, b, :], ALU.mult).then_inc(du_ready, 1)
            for c in range(NCH):
                cols = slice(c * CH, (c + 1) * CH)
                for n in range(STATES):
                    k = STATES * c + n
                    dve.wait_ge(da_ready, k + 1)
                    dve.wait_ge(dbu_ready, k + 1)
                    dve.wait_ge(state_saved, k - STATES + 2 if k >= STATES else 1)
                    for b in range(DI):
                        m = nc.vector.tensor_tensor_scan(hs[k % 2][:, b, :], PS[:, 4 + 2 * (k % 2) + b, :], dbu[k % 3][:, b, :],
                                                         state[:, n, b:b + 1], ALU.mult, ALU.add)
                    m.then_inc(scan_done, 1)
                    dve.wait_ge(scan_done, k + 1)
                    dve.wait_ge(c_mm, k + 1)
                    if k >= 2:
                        dve.wait_ge(y_mm, k - 1)
                    nc.vector.tensor_tensor(hc[k % 2], PS[:, 1, :].unsqueeze(1).to_broadcast([P, DI, CH]), hs[k % 2],
                                            ALU.mult).then_inc(hc_ready, 1)
                    nc.vector.tensor_copy(state[:, n, :], hs[k % 2][:, :, CH - 1]).then_inc(state_saved, 1)
                dve.wait_ge(y_mm, STATES * (c + 1))
                for b in range(DI):
                    m = nc.vector.scalar_tensor_tensor(yg[:, b, cols], u[:, b, cols], dskip[:, b:b + 1], PS[:, 2 + b, :],
                                                       ALU.mult, ALU.add)
                m.then_inc(y_done, 1)
                dve.wait_ge(y_done, c + 1)
                nc.vector.tensor_tensor(yg[:, :, cols], yg[:, :, cols], zg[:, :, cols], ALU.mult).then_inc(yg_ready, 1)

            def after_layer3(q):
                dve.wait_ge(o_mm, q + 1)
                link(add_bank(q))

            norm(4, X, x_ready, after_layer3)

        @block.sync
        def _(sp):
            sp.dma_start(X, x_tiles).then_inc(x_in, 16)
            for s in range(2):
                sp.dma_start(a1[s], adj_tiles[:, 2 * s:2 * s + 2, :]).then_inc(a1_in[s], 16)
            for g in range(NCH):
                for s in range(2):
                    k = 2 * g + s
                    if k + 2 < NT // 2:
                        sp.wait_ge(tr1, 8 * (k + 1))
                        sp.wait_ge(deg_done, 2 * (k + 1))
                        sp.dma_start(a1[s], adj_tiles[:, 2 * k + 4:2 * k + 6, :]).then_inc(a1_in[s], 16)
                sp.wait_ge(ev1a, 8 * (g + 1))
                sp.wait_ge(ev1v, 8 * (g + 1))
                sp.dma_start(at_tiles[:, :, g * CH:(g + 1) * CH], atg[g % 2]).then_inc(at_out[g % 2], 16)
            sp.wait_ge(ah_done, NCH)
            sp.wait_ge(deg_done, NT)
            sp.dma_start(aw[0], adj_tiles[:, 0:2, :]).then_inc(a2_in[0], 16)
            sp.wait_ge(er_ready, 4)
            sp.dma_start(e_dram, e_rows).then_inc(e_out, 16)
            sp.wait_ge(e_out, 16)
            sp.wait_ge(e1_done, NCH)
            for s in range(2):
                sp.wait_ge(at_out[s], 32)
            for h in range(HEADS):
                sp.dma_start(eb[:, 0, h, :], e_dram[h].partition_broadcast(P)).then_inc(ep_in[h], 16)
            sp.dma_start(aw[1], adj_tiles[:, 2:4, :]).then_inc(a2_in[1], 16)
            for h in range(HEADS):
                sp.dma_start(eb[:, 1, h, :], e_dram[HEADS + h].partition_broadcast(P)).then_inc(em_in, 16)
            with sp.Fori(0, NT // 4 - 1) as it:
                for s in range(2):
                    sp.wait_ge(q_done, it * 6 + 3 * (s + 1))
                    sp.dma_start(aw[s], adj_tiles[:, bass.ds(it * 4 + 4 + 2 * s, 2), :]).then_inc(a2_in[s], 16)
            sp.wait_ge(em_in, 16 * HEADS)
            sp.wait_ge(qt_used, 4 + 4 * 48)
            sp.wait_ge(q_done, 3 * NT // 2)
            for s in range(2):
                sp.wait_ge(at_out[s], 32)
            sp.dma_start(X, x_tiles).then_inc(x_in, 16)
            for b in range(NT // 4):
                sp.dma_start(AT[:, 4 * b:4 * b + 4, :], at_tiles[:, 4 * b:4 * b + 4, :]).then_inc(at_in, 16)
            later_loads(sp)

        @block.gpsimd
        def _(pool):
            nc.gpsimd.memset(ident[:], 0.0).then_inc(ident_ready, 1)
            nc.gpsimd.memset(cst[:, 0:1], 1e-5).then_inc(ident_ready, 1)
            nc.gpsimd.memset(cst[:, 1:2], 1.0).then_inc(ident_ready, 1)
            nc.gpsimd.memset(smask[:, 0], 0.0).then_inc(ident_ready, 1)
            nc.gpsimd.memset(smask[:, 1], 1.0).then_inc(ident_ready, 1)
            pool.wait_ge(ident_ready, 5)
            nc.gpsimd.affine_select(out=ident[:], in_=ident[:], compare_op=ALU.not_equal, fill=1.0, base=0,
                                    pattern=[[-1, P]], channel_multiplier=1).then_inc(ident_ready, 1)
            nc.gpsimd.memset(comb[0:ROWS], 0.0).then_inc(comb_ready, 1)
            for p in range(3):
                pool.wait_ge(comb_ready, p + 1)
                nc.gpsimd.affine_select(out=comb[0:ROWS], in_=comb[0:ROWS], compare_op=ALU.not_equal, fill=-1.0,
                                        base=-(1 + 3 * p), pattern=[[-9, 2], [-1, 3]],
                                        channel_multiplier=1).then_inc(comb_ready, 1)
            later_pool(pool)

        @block.scalar
        def _(act):
            act.dma_start(raw[:, 16:19, :], t["L0_gnn_gat_W"].rearrange("h k f -> k h f")).then_inc(gat_in, 16)
            act.dma_start(raw[:, 15, :], t["L2_gnn_weight"]).then_inc(gat_in, 16)
            for h in range(HEADS):
                act.dma_start(ga[:, h, :], t["L0_gnn_gat_a"][h].rearrange("(s f) o -> f (s o)", f=P)).then_inc(ga_in, 16)
            act.dma_start(a2[:, 0:1], t["L2_gnn_a_l"].rearrange("(f o) -> f o", o=1)).then_inc(ga_in, 16)
            act.dma_start(a2[:, 1:2], t["L2_gnn_a_r"].rearrange("(f o) -> f o", o=1)).then_inc(ga_in, 16)
            gru = ["edge_Wih", "edge_Whh", "node_Wih", "node_Whh"]
            for k, name in enumerate(gru):
                act.dma_start(raw[:, 3 * k:3 * k + 3, :],
                              t["L0_gnn_" + name].rearrange("(g p) k -> p g k", p=P)).then_inc(raw_in, 16)
            act.dma_start(raw[:, 12, :], t["L1_gnn_neigh_W"]).then_inc(raw_in, 16)
            act.dma_start(raw[:, 13:15, :], t["L1_gnn_lin_W"].rearrange("o (b c) -> o b c", c=P)).then_inc(raw_in, 16)
            for k, name in enumerate(["edge_bih", "edge_bhh", "node_bih", "node_bhh"]):
                act.dma_start(gb[:, k, :], t["L0_gnn_" + name].rearrange("(g p) -> p g", p=P)).then_inc(vec_in, 16)

            act.wait_ge(su_mm, 1)
            nc.scalar.activation(rawt[:], PS[:, 0, :].rearrange("p (b k) -> p b k", k=P), ACT.Copy).then_inc(su_act, 1)
            act.wait_ge(su_mm, 6)
            nc.scalar.activation(wa[:], PS[:, 5, 0:6], ACT.Copy).then_inc(su_act, 1)
            nc.scalar.activation(war[:], PS[:, 5, 6:8], ACT.Copy).then_inc(su_act, 1)

            for g in range(NCH):
                for k in range(4):
                    tile = 4 * g + k
                    act.wait_ge(diag_out, tile + 1)
                    if tile:
                        act.wait_ge(deg_done, tile)
                    if tile == 4:
                        act.wait_ge(su_mm, 23)
                    nc.scalar.activation(XT if g else es[:], a1[tile // 2 % 2][:, tile % 2, :], ACT.Copy,
                                         accum_out=deg[:, tile:tile + 1]).then_inc(deg_done, 1)
                    for b in range(2):
                        act.wait_ge(tr1, 4 * tile + b + 1)
                        if k == 0 and b == 0 and g >= 2:
                            act.wait_ge(at_out[g % 2], 16)
                            act.wait_ge(ah_done, g - 1)
                            act.wait_ge(masks_made, 4 * (g - 1))
                        nc.scalar.activation(atg[g % 2][:, 4 * b:4 * b + 4, k * P:(k + 1) * P],
                                             PS[:, b, :].rearrange("p (t i) -> p t i", i=P),
                                             ACT.Copy).then_inc(ev1a, 1)
                    if g == 0:
                        for jt in range(4 * k, 4 * k + 2):
                            act.wait_ge(su_mm, 7 + jt)
                            nc.scalar.activation(hw[:, jt].rearrange("p h f -> p (h f)"), PS[:, 4 + jt % 4, 0:HEADS * P],
                                                 ACT.Copy).then_inc(su_act, 1)
                if g == 0:
                    for q in range(4):
                        n = 4 if q < 3 else 3
                        act.wait_ge(su_mm, 24 + q)
                        nc.scalar.activation(wt[:, 4 * q:4 * q + n, :],
                                             PS[:, 5 + q % 3, 0:n * P].rearrange("p (b k) -> p b k", k=P),
                                             ACT.Copy).then_inc(su_act, 1)

            for q in range(NCH):
                act.wait_ge(eb_mm, q + 1)
                nc.scalar.activation(qt[q][0:6], PS[0:6, q, :], ACT.Copy, scale=0.2).then_inc(eb_act, 1)

            act.sem_inc(qt_ready, 4)
            act.sem_inc(es_out, 2)

            def softmax(it, k, tiles):
                for j in tiles:
                    s = 2 * (k % 3) + j
                    act.wait_ge(x_done, it * 12 + 2 * k + j + 1)
                    e = nc.scalar.activation(w[s], w[s], ACT.Exp, bias=ymin[:, s:s + 1], scale=-1.0,
                                             accum_out=zsum[:, s:s + 1])
                    if j == 1:
                        e.then_inc(exp_done, 1)

            def evacuate(it, k, parts):
                for v in parts:
                    act.wait_ge(tr2, it * 48 + 8 * k + v + 25)
                    act.wait_ge(qt_used, it * 48 + 8 * k + v + 1)
                    nc.scalar.activation(qt[v % 4], PS[:, v % 4, :], ACT.Copy).then_inc(qt_ready, 1)

            def support(it, pair):
                act.wait_ge(qt_used, it * 48 + 24 * pair + 28)
                act.wait_ge(er_ready, 4)
                nc.scalar.activation(es[:, bass.ds(it * CH + 256 * pair, 256)], PS[:, 4 + pair, 0:256], ACT.Copy,
                                     scale=1.0 / HEADS).then_inc(es_out, 1)

            def four_tiles(it, last):
                for k in range(6):
                    ahead = k < 4 or not last
                    evacuate(it, k, range(0, 3))
                    if k == 3:
                        support(it, 0)
                    if ahead:
                        softmax(it, k + 2, [0])
                    evacuate(it, k, range(3, 6))
                    if ahead:
                        softmax(it, k + 2, [1])
                    evacuate(it, k, range(6, 8))
                support(it, 1)

            for k in range(2):
                softmax(0, k, [0, 1])
            with act.Fori(0, NT // 4 - 1) as it:
                four_tiles(it, False)
            four_tiles(NT // 4 - 1, True)
            later_act(act)

        @block.tensor
        def _(pe):
            pe.wait_ge(ident_ready, 6)
            pe.wait_ge(gat_in, 16 * 2)
            for b in range(4):
                m = transpose_into(0, b * P, raw[:, 15 + b, :])
            m.then_inc(su_mm, 1)
            pe.wait_ge(x_in, 16)
            for q in range(4):
                for b in range(4):
                    m = transpose_into(1 + q, b * P, X[:, 4 * q + b, :])
                m.then_inc(su_mm, 1)
            pe.wait_ge(su_act, 1)
            pe.wait_ge(ga_in, 16 * 5)
            for h in range(HEADS):
                nc.tensor.matmul(PS[:, 5, 2 * h:2 * h + 2], rawt[:, 1 + h, :], ga[:, h, :], start=True, stop=True)
            nc.tensor.matmul(PS[:, 5, 6:8], rawt[:, 0, :], a2[:], start=True, stop=True).then_inc(su_mm, 1)

            def head_features(k):
                for jt in range(4 * k, 4 * k + 4):
                    b = jt % 4
                    if b < 2:
                        pe.wait_ge(su_act, 3 + (2 * k - 1 + b if k else 0))
                    elif k:
                        pe.wait_ge(su_dve, 4 + 2 * k - 3 + b)
                    nc.tensor.matmul(PS[:, 4 + b, 0:HEADS * P], XT[:, jt * P:(jt + 1) * P],
                                     raw[:, 16:19, :].rearrange("p h f -> p (h f)"), start=True,
                                     stop=True).then_inc(su_mm, 1)

            def rest_of_setup():
                pe.wait_ge(su_act, 3 + 7)
                for jt in range(NT):
                    m = nc.tensor.matmul(PS[:, 4, 6 * jt:6 * jt + 6], XT[:, jt * P:(jt + 1) * P], wa[:], start=True,
                                         stop=True)
                m.then_inc(su_mm, 1)
                pe.wait_ge(raw_in, 16 * 6)
                pe.wait_ge(su_act, 3 + 8)
                pe.wait_ge(su_dve, 4 + 8)
                for q in range(4):
                    if q == 3:
                        pe.wait_ge(su_act, 3 + 8 + 1)
                    for b in range(4 if q < 3 else 3):
                        m = transpose_into(5 + q % 3, b * P, raw[:, 4 * q + b, :])
                    m.then_inc(su_mm, 1)

            def products(g, q):
                pe.wait_ge(ev1a, 8 * (g + 1))
                pe.wait_ge(ev1v, 8 * (g + 1))
                if q == 0 and g >= 2:
                    pe.wait_ge(l1_ev, 2 * (g - 1))
                if q == 0 and g == 0:
                    pe.wait_ge(su_act, 15)
                    pe.wait_ge(su_dve, 13)
                for jt in range(4 * q, 4 * q + 4):
                    m = nc.tensor.matmul(PS[:, 4 + g % 2, :], X[:, jt, :], atg[g % 2][:, jt, :],
                                         start=(jt == 0), stop=(jt == NT - 1))
                if q == 3:
                    m.then_inc(ah_done, 1)
                pe.wait_ge(masks_made, 4 * g + q + 1)
                for jt in range(4 * q, 4 * q + 4):
                    for s in range(2):
                        m = nc.tensor.matmul(PS[0:ROWS, 6 + g % 2, :], smask[:, s, jt, 0:ROWS], pm[s][:, jt, :],
                                             start=(jt == 0 and s == 0), stop=(jt == NT - 1 and s == 1))
                if q == 3:
                    m.then_inc(e1_done, 1)

            pe.wait_ge(su_dve, 4)
            for g in range(NCH):
                for k in range(4):
                    tile = 4 * g + k
                    pe.wait_ge(diag_out, tile + 1)
                    for b in range(4):
                        if tile:
                            pe.wait_ge(ev1a if b < 2 else ev1v, 2 * (tile - 1) + b % 2 + 1)
                        for c in range(4):
                            m = transpose_into(b, c * P, a1[tile // 2 % 2][:, tile % 2, (4 * b + c) * P:(4 * b + c + 1) * P])
                        m.then_inc(tr1, 1)
                    if g == 0:
                        head_features(k)
                    else:
                        products(g - 1, k)
                if g == 0:
                    rest_of_setup()
            for k in range(4):
                products(NCH - 1, k)

            pe.wait_ge(comb_ready, 4)
            for q in range(NCH):
                pe.wait_ge(l1_ev, 2 * (q + 1))
                nc.tensor.matmul(PS[0:6, q, :], comb[0:ROWS].rearrange("p s h -> p (s h)"),
                                 es[0:ROWS, q * CH:(q + 1) * CH], start=True, stop=True).then_inc(eb_mm, 1)
            pe.wait_ge(er_ready, 4)

            pe.sem_inc(tr2, 24)
            pe.sem_inc(qt_used, 4)
            with pe.Fori(0, NT // 4) as it:
                for k in range(6):
                    h = k % 3
                    pe.wait_ge(q_done, it * 6 + k + 1)

                    def fill(v):
                        pe.wait_ge(qt_ready, it * 48 + 8 * k + v + 1)
                        for c in range(2):
                            for j in range(2):
                                m = transpose_into(v % 4, 256 * c + j * P, w[2 * (k % 3) + j][:, (2 * v + c) * P:(2 * v + c + 1) * P])
                        m.then_inc(tr2, 1)

                    def multiply(v):
                        pe.wait_ge(qt_ready, it * 48 + 8 * k + v + 5)
                        if h == 0 and v == 0:
                            pe.wait_ge(es_out, it * 2 + k // 3 + 1)
                        for c in range(2):
                            jt = 2 * v + c
                            m = nc.tensor.matmul(PS[:, 4 + k // 3, 0:256], hw[:, jt, h, :], qt[v % 4][:, 256 * c:256 * c + 256],
                                                 start=(h == 0 and jt == 0), stop=(h == 2 and jt == NT - 1))
                        m.then_inc(qt_used, 1)

                    fill(0)
                    fill(1)
                    for v in range(8):
                        if v + 2 < 8:
                            fill(v + 2)
                        multiply(v)
            later_pe(pe)

        @block.vector
        def _(dve):
            count = [0]

            def link(ins):
                count[0] += 1
                ins.then_inc(dch, 1)
                dve.wait_ge(dch, count[0])

            for q in range(4):
                dve.wait_ge(su_mm, 2 + q)
                nc.vector.tensor_copy(XT[:, q * CH:(q + 1) * CH], PS[:, 1 + q, :]).then_inc(su_dve, 1)
            nc.vector.memset(mk[:], 0.0).then_inc(marked, 1)

            def stationary_pieces():
                dve.wait_ge(su_mm, 23)
                link(nc.vector.tensor_copy(upc[:], PS[:, 4, 0:96].rearrange("p (t c) -> p t c", c=6)))
                dve.wait_ge(ident_ready, 6)
                for p in range(3):
                    link(nc.vector.tensor_copy(upb[:], upc[:]))
                    for s in range(2):
                        part = upb[:].rearrange("p t (h s) -> p t h s", s=2)[:, :, :, s]
                        nc.vector.tensor_copy(smask[:, 0, :, 1 + 9 * s + 3 * p:4 + 9 * s + 3 * p], part)
                        last = nc.vector.tensor_copy(smask[:, 1, :, 10 - 9 * s + 3 * p:13 - 9 * s + 3 * p], part)
                    if p < 2:
                        link(last)
                        link(nc.vector.tensor_tensor(upc[:], upc[:], upb[:], ALU.subtract))
                last.then_inc(su_dve, 1)
                dve.wait_ge(vec_in, 16 * 4)
                for g in range(2):
                    nc.vector.tensor_tensor(gbs[:, g, :], gb[:, 2 * g, 0:2], gb[:, 2 * g + 1, 0:2], ALU.add)

            def masks(g, q):
                if q == 0:
                    if g == 0:
                        dve.wait_ge(su_mm, 27)
                        dve.wait_ge(su_dve, 13)
                    dve.wait_ge(ev1a, 8 * (g + 1))
                    dve.wait_ge(ev1v, 8 * (g + 1))
                    if g:
                        dve.wait_ge(e1_done, g)
                src = atg[g % 2][:, 4 * q:4 * q + 4, :]
                nc.vector.tensor_scalar(pm[0][:, 4 * q:4 * q + 4, :], src, 0.0, None, ALU.is_gt)
                nc.vector.tensor_scalar(pm[1][:, 4 * q:4 * q + 4, :], src, 0.0, None, ALU.is_lt).then_inc(masks_made, 1)

            def rows_out(g):
                dve.wait_ge(ah_done, g + 1)
                nc.vector.tensor_copy(ns[:, g * CH:(g + 1) * CH], PS[:, 4 + g % 2, :]).then_inc(l1_ev, 1)
                dve.wait_ge(e1_done, g + 1)
                dve.wait_ge(deg_done, 4)
                nc.vector.tensor_copy(es[0:ROWS, g * CH:(g + 1) * CH], PS[0:ROWS, 6 + g % 2, :]).then_inc(l1_ev, 1)

            for g in range(NCH):
                for k in range(4):
                    tile = 4 * g + k
                    blk = a1[tile // 2 % 2][:, tile % 2, tile * P:(tile + 1) * P]
                    dve.wait_ge(a1_in[tile // 2 % 2], 16 * (tile // 4 + 1))
                    if tile:
                        dve.wait_ge(diag_out, tile)
                    link(nc.vector.tensor_tensor(dgt[:], blk, ident[:], ALU.mult))
                    nc.vector.reduce_sum(dn[:, tile:tile + 1], dgt[:], AXL.X)
                    nc.vector.tensor_tensor(blk, blk, dgt[:], ALU.subtract).then_inc(diag_out, 1)
                    if g >= 1:
                        masks(g - 1, k)
                    for b in range(2, 4):
                        dve.wait_ge(tr1, 4 * tile + b + 1)
                        if k == 0 and b == 2 and g >= 2:
                            dve.wait_ge(at_out[g % 2], 16)
                            dve.wait_ge(ah_done, g - 1)
                        nc.vector.tensor_copy(atg[g % 2][:, 4 * b:4 * b + 4, k * P:(k + 1) * P],
                                              PS[:, b, :].rearrange("p (t i) -> p t i", i=P)).then_inc(ev1v, 1)
                    if g == 0:
                        for jt in range(4 * k + 2, 4 * k + 4):
                            dve.wait_ge(su_mm, 7 + jt)
                            nc.vector.tensor_copy(hw[:, jt].rearrange("p h f -> p (h f)"),
                                                  PS[:, 4 + jt % 4, 0:HEADS * P]).then_inc(su_dve, 1)
                if g == 0:
                    stationary_pieces()
                if g >= 1:
                    rows_out(g - 1)
            for k in range(4):
                masks(NCH - 1, k)
            rows_out(NCH - 1)

            dve.wait_ge(deg_done, NT)
            for q in range(NCH):
                dve.wait_ge(eb_act, q + 1)
                nc.vector.tensor_tensor(e_rows[:, q * CH:(q + 1) * CH], PS[0:6, q, :], qt[q][0:6],
                                        ALU.min).then_inc(er_ready, 1)
            dve.wait_ge(l1_ev, 2 * NCH)
            link(nc.vector.tensor_reduce(flag[:], es[0:1, :], AXL.X, ALU.max))
            negative = dve.value_load(flag[:].bitcast(I32), min_val=0, max_val=0x7fffffff)

            def attention(signed):
                steps = [0]

                def chain(it, ins):
                    steps[0] += 1
                    ins.then_inc(signed_step, 1)
                    dve.wait_ge(signed_step, it * 84 + steps[0])

                def logits(it, k, j):
                    pair, h = k // 3 % 2, k % 3
                    s = 2 * h + j
                    if h == 0:
                        tile = it * 4 + 2 * (k // 3) + j
                        if j == 0:
                            dve.wait_ge(a2_in[pair], it * 16 + 16 * (k // 6) + 16)
                        blk = aw[pair][:, j, bass.ds(tile * P, P)]
                        nc.vector.tensor_tensor(blk, blk, dgt[:], ALU.mult).then_inc(offd_done, 1)
                        dve.wait_ge(offd_done, tile + 1)
                        nc.vector.tensor_scalar(bm[2 * pair + j], aw[pair][:, j, :], 0.0, MASKED, ALU.is_le,
                                                ALU.mult).then_inc(bm_done, 1)
                        dve.wait_ge(bm_done, tile + 1)
                    dve.wait_ge(ep_in[h], 16)
                    if signed:
                        dve.wait_ge(em_in, 16 * HEADS)
                    dve.wait_ge(tr2, it * 48 + 8 * k + 8)
                    dve.wait_ge(marked, it * 12 + 2 * k + j + 1)
                    nc.vector.memset(mk[:], 0.0).then_inc(marked, 1)
                    if not signed:
                        m = nc.vector.tensor_tensor_reduce(
                            out=w[s], in0=bm[2 * pair + j], in1=eb[:, 0, h, :], scale=1.0, scalar=3.0e38,
                            op0=ALU.add, op1=ALU.min, accum_out=ymin[:, s:s + 1])
                    else:
                        a = aw[pair][:, j, :]
                        chain(it, nc.vector.tensor_tensor(w[s], bm[2 * pair + j], eb[:, 0, h, :], ALU.add))
                        for half in range(2):
                            cols = slice(half * N // 2, (half + 1) * N // 2)
                            spare = PS[:, 6:8, :].rearrange("p b c -> p (b c)")
                            chain(it, nc.vector.tensor_scalar(spare, a[:, cols], 0.0, MASKED, ALU.is_ge, ALU.mult))
                            chain(it, nc.vector.tensor_tensor(spare, spare, eb[:, 1, h, cols], ALU.add))
                            chain(it, nc.vector.tensor_tensor(w[s][:, cols], spare, w[s][:, cols], ALU.min))
                        m = nc.vector.tensor_reduce(ymin[:, s:s + 1], w[s], AXL.X, ALU.min)
                    m.then_inc(x_done, 1)

                def weights(it, k, j):
                    pair, h = k // 3, k % 3
                    if j == 0:
                        dve.wait_ge(exp_done, it * 6 + k + 1)
                        nc.vector.reciprocal(rz[:, 2 * h:2 * h + 2], zsum[:, 2 * h:2 * h + 2]).then_inc(rz_done, 1)
                        dve.wait_ge(rz_done, it * 6 + k + 1)
                    s = 2 * h + j
                    m = nc.vector.scalar_tensor_tensor(w[s], w[s], rz[:, s:s + 1], aw[pair][:, j, :], ALU.mult, ALU.mult)
                    if j == 1:
                        m.then_inc(q_done, 1)

                def four_tiles(it, last):
                    for k in range(6):
                        for j in range(2):
                            if k < 5 or not last:
                                logits(it, k + 1, j)
                            weights(it, k, j)

                for j in range(2):
                    logits(0, 0, j)
                with dve.Fori(0, NT // 4 - 1) as it:
                    four_tiles(it, False)
                steps[0] -= 84
                four_tiles(NT // 4 - 1, True)

            link(nc.vector.tensor_scalar(dgt[:], ident[:], -1.0, 1.0, ALU.mult, ALU.add))
            with dve.If(negative != 0):
                attention(True)
            with dve.Else():
                attention(False)
            later_dve(dve, link)


_INS = ["x", "adj", "L0_gnn_gat_W", "L0_gnn_gat_a", "L0_gnn_edge_Wih", "L0_gnn_edge_Whh", "L0_gnn_edge_bih",
        "L0_gnn_edge_bhh", "L0_gnn_node_Wih", "L0_gnn_node_Whh", "L0_gnn_node_bih", "L0_gnn_node_bhh",
        "L1_gnn_neigh_W", "L1_gnn_lin_W", "L2_gnn_weight", "L2_gnn_a_l", "L2_gnn_a_r", "L2_gnn_b", "L3_gnn_gcn_w",
        "L3_gnn_gcn_b", "L3_gnn_ln_g", "L3_gnn_ln_b", "L3_gnn_w_in", "L3_gnn_conv_w", "L3_gnn_conv_b", "L3_gnn_w_xp",
        "L3_gnn_w_dt", "L3_gnn_b_dt", "L3_gnn_A_log", "L3_gnn_D_skip", "L3_gnn_w_out"]


def kernel(**inputs):
    import numpy as _np
    import concourse.bacc as _bacc
    from concourse import mybir as _mybir
    from concourse.bass_utils import run_bass_kernel_spmd as _run

    nc = _bacc.Bacc("TRN2", target_bir_lowering=False, num_devices=1)
    arrays, aps = {}, {}
    for name in _INS:
        a = _np.ascontiguousarray(inputs[name])
        arrays[f"in_{name}"] = a
        aps[name] = nc.dram_tensor(f"in_{name}", a.shape, _mybir.dt.from_np(a.dtype), kind="ExternalInput").ap()
    out = nc.dram_tensor("out_x", (N, P), F32, kind="ExternalOutput").ap()
    gnn_program(nc, aps, out)
    r = _run(nc, [arrays], core_ids=[0])
    return r.results[0]["out_x"]
```

```python
from contextlib import ExitStack

import numpy as np

import concourse.bass as bass
from concourse import mybir

ALU = mybir.AluOpType
ACT = mybir.ActivationFunctionType
AXL = mybir.AxisListType
F32 = mybir.dt.float32
BF16 = mybir.dt.bfloat16
I32 = mybir.dt.int32

P = 128
N = 2048
NT = N // P
CH = 512
NCH = N // CH
HEADS = 3
ROWS = 1 + 2 * 3 * HEADS
MASKED = 9.0e15
DI = 2
STATES = 16
DTR = 8
TAPS = 4
PAD = 4

HW0 = 0
EBP0 = HW0 + HEADS * N
EBM0 = EBP0 + HEADS * N
W0 = EBM0 + HEADS * N
A20 = W0 + 6 * N
B20 = A20 + 4 * N
QT0 = B20 + 4 * N // 2
BIGW = QT0 + 4 * CH
ATG0 = EBP0
PM0 = ATG0 + 2 * NT * CH
X0 = NT * N
XT0 = X0 + N
A10 = XT0 + N
SC0 = XT0 + N
assert PM0 + NT * CH <= X0 and A10 + 4 * N <= BIGW and SC0 + 4 * N <= BIGW


def gnn_program(nc, t, out):
    ctx = ExitStack()
    with ctx:
        ctx.enter_context(nc.allow_non_contiguous_dma(reason="small weight vectors, laid out once"))

        def sb(name, shape, dt=F32):
            return ctx.enter_context(nc.sbuf_tensor(name, shape, dt))

        def sem(name):
            return ctx.enter_context(nc.semaphore(name))

        big = sb("big", [P, BIGW])
        PS = ctx.enter_context(nc.psum_tensor("PS", [P, 8, CH], F32))
        at_dram = nc.dram_tensor("at_dram", (N, N), F32, kind="Internal").ap()
        e_dram = nc.dram_tensor("e_dram", (6, N), F32, kind="Internal").ap()

        ns = sb("ns", [P, N])
        es = sb("es", [P, N])
        wt = sb("wt", [P, 15, P])
        ident = sb("ident", [P, P])
        smask = sb("smask", [P, 2, NT, 20], BF16)
        wa = sb("wa", [P, 6])
        ga = sb("ga", [P, HEADS, 2])
        war = sb("war", [P, 2])
        a2 = sb("a2", [P, 2])
        gb = sb("gb", [P, 4, 3])
        gbs = sb("gbs", [P, 2, 2])
        comb = sb("comb", [P, 2, HEADS])
        dn = sb("dn", [P, NT])
        deg = sb("deg", [P, NT])
        rdeg = sb("rdeg", [P, NT])
        degt = sb("degt", [P, 8])
        dgt = sb("dgt", [P, P])
        mk = sb("mk", [P, 1])
        flag = sb("flag", [1, 1])
        ymin = sb("ymin", [P, 6])
        zsum = sb("zsum", [P, 6])
        rz = sb("rz", [P, 6])
        stats = sb("stats", [P, NT, 6])
        mv = sb("mv", [P, NT, 2])
        rstd = sb("rstd", [P, NT])
        cst = sb("cst", [P, 2])
        elr = sb("elr", [P, NT, 2])
        bj = sb("bj", [P, NT])
        dj = sb("dj", [P, NT])
        ci = sb("ci", [P, NT])
        zi = sb("zi", [P, NT])
        conv_w = sb("conv_w", [P, DI, TAPS])
        conv_b = sb("conv_b", [P, DI])
        dskip = sb("dskip", [P, DI])
        ln_g = sb("ln_g", [P, 1])
        ln_b = sb("ln_b", [P, 1])
        na = sb("na", [P, DI, STATES])
        state = sb("state", [P, STATES, DI])

        def region(at, words):
            return big[:, at:at + words]

        X = region(X0, N).rearrange("p (t f) -> p t f", f=P)
        XT = region(XT0, N)
        AT = region(0, NT * N).rearrange("p (t i) -> p t i", i=N)
        SC = region(SC0, 4 * N)
        raw = region(PM0, 19 * P).rearrange("p (b k) -> p b k", k=P)
        rawt = region(PM0 + 19 * P, 4 * P).rearrange("p (b k) -> p b k", k=P)
        upc = region(PM0 + 24 * P, 96).rearrange("p (t c) -> p t c", c=6)
        upb = region(PM0 + 25 * P, 48).bitcast(BF16).rearrange("p (t c) -> p t c", c=6)
        hw = region(HW0, HEADS * N).rearrange("p (t h f) -> p t h f", h=HEADS, f=P)
        a1 = [region(A10 + 2 * N * s, 2 * N).rearrange("p (t j) -> p t j", t=2) for s in range(2)]
        atg = [region(ATG0 + NT * CH * g, NT * CH).rearrange("p (t i) -> p t i", i=CH) for g in range(2)]
        pm = [region(PM0 + NT * CH // 2 * m, NT * CH // 2).bitcast(BF16).rearrange("p (t i) -> p t i", i=CH)
              for m in range(2)]
        e_rows = region(XT0, N)[0:6]
        eb = region(EBP0, 6 * N).rearrange("p (s h j) -> p s h j", s=2, h=HEADS)
        w = [region(W0 + N * k, N) for k in range(6)]
        aw = [region(A20 + 2 * N * s, 2 * N).rearrange("p (t j) -> p t j", t=2) for s in range(2)]
        bm = [region(B20 + N // 2 * k, N // 2).bitcast(BF16) for k in range(4)]
        qt = [region(QT0 + CH * k, CH) for k in range(4)]

        adj_tiles = t["adj"].rearrange("(t p) j -> p t j", p=P)
        at_tiles = at_dram.rearrange("(t p) i -> p t i", p=P)
        x_tiles = t["x"].rearrange("(t p) f -> p t f", p=P)

        x_in, gat_in, ga_in, raw_in, vec_in = sem("x_in"), sem("gat_in"), sem("ga_in"), sem("raw_in"), sem("vec_in")
        ident_ready = sem("ident_ready")
        su_mm, su_act, su_dve = sem("su_mm"), sem("su_act"), sem("su_dve")
        dch = sem("dch")
        a1_in = [sem("a1_in0"), sem("a1_in1")]
        diag_out, deg_done = sem("diag_out"), sem("deg_done")
        tr1, ev1a, ev1v = sem("tr1"), sem("ev1a"), sem("ev1v")
        masks_made, ah_done, e1_done, l1_ev = sem("masks_made"), sem("ah_done"), sem("e1_done"), sem("l1_ev")
        at_out = [sem("at_out0"), sem("at_out1")]
        comb_ready, eb_mm, eb_act, er_ready = sem("comb_ready"), sem("eb_mm"), sem("eb_act"), sem("er_ready")
        e_out, em_in, ep_in = sem("e_out"), sem("em_in"), [sem("ep_in%d" % h) for h in range(HEADS)]
        a2_in = [sem("a2_in0"), sem("a2_in1")]
        x_done, exp_done, q_done = sem("x_done"), sem("exp_done"), sem("q_done")
        tr2, qt_ready, qt_used = sem("tr2"), sem("qt_ready"), sem("qt_used")
        es_out, marked = sem("es_out"), sem("marked")
        offd_done, bm_done, rz_done, signed_step = sem("offd_done"), sem("bm_done"), sem("rz_done"), sem("signed_step")
        at_in, diag_back = [sem("at_in%d" % b) for b in range(4)], sem("diag_back")
        xt_mm, xt_ev = sem("xt_mm"), sem("xt_ev")
        gru_mm, gate, tanh_in, tanh_out, gru_out = (sem("gru_mm"), sem("gate"), sem("tanh_in"), sem("tanh_out"),
                                                    sem("gru_out"))
        st_mm = sem("st_mm")
        var_ready, std_ready, x_ready = sem("var_ready"), sem("std_ready"), sem("x_ready")
        out_sem = sem("out_sem")
        b2_in = sem("b2_in")
        b_mm = sem("b_mm")
        bb_ready = sem("bb_ready")
        c_mm = sem("c_mm")
        conv_done = sem("conv_done")
        conv_step = sem("conv_step")
        da_ready = sem("da_ready")
        dbc_ev = sem("dbc_ev")
        dbc_mm = sem("dbc_mm")
        dbu_ready = sem("dbu_ready")
        dt_mm = sem("dt_mm")
        dt_ready = sem("dt_ready")
        du_ready = sem("du_ready")
        gru_step = sem("gru_step")
        h_ready = sem("h_ready")
        hc_ready = sem("hc_ready")
        ht_ev = sem("ht_ev")
        l1_a = sem("l1_a")
        l1_add = sem("l1_add")
        l1_aev = sem("l1_aev")
        l1_b = sem("l1_b")
        l1_h = sem("l1_h")
        l1_hev = sem("l1_hev")
        l1_mm = sem("l1_mm")
        l2_aev = sem("l2_aev")
        l2_b = sem("l2_b")
        l2_mm = sem("l2_mm")
        l2_rb = sem("l2_rb")
        l2_rbev = sem("l2_rbev")
        l2_v = sem("l2_v")
        l2_vec = sem("l2_vec")
        l2_x = sem("l2_x")
        l2_xev = sem("l2_xev")
        l3_aev = sem("l3_aev")
        l3_g = sem("l3_g")
        l3_gev = sem("l3_gev")
        l3_mm = sem("l3_mm")
        na_exp = sem("na_exp")
        na_ready = sem("na_ready")
        o_mm = sem("o_mm")
        ones_in_dbc = sem("ones_in_dbc")
        ones_ready = sem("ones_ready")
        pad_ready = sem("pad_ready")
        pieces_ready = sem("pieces_ready")
        q2_act = sem("q2_act")
        q2_added = sem("q2_added")
        q2_ready = sem("q2_ready")
        q2_used = sem("q2_used")
        res0_added = sem("res0_added")
        rest_added = sem("rest_added")
        scan_done = sem("scan_done")
        sel_ready = sem("sel_ready")
        sp_exp = sem("sp_exp")
        sp_ln = sem("sp_ln")
        sp_neg = sem("sp_neg")
        sp_relu = sem("sp_relu")
        state_saved = sem("state_saved")
        state_zero = sem("state_zero")
        sums_read = sem("sums_read")
        u_ready = sem("u_ready")
        w2_in = sem("w2_in")
        w3_in = sem("w3_in")
        w4_in = sem("w4_in")
        walb_ready = sem("walb_ready")
        x_plus_b = sem("x_plus_b")
        xps_ready = sem("xps_ready")
        xz_ev = sem("xz_ev")
        xz_mm = sem("xz_mm")
        y_done = sem("y_done")
        y_mm = sem("y_mm")
        yg_ready = sem("yg_ready")
        z_mm = sem("z_mm")
        block = ctx.enter_context(nc.Block())


        def transpose_into(bank, col, src):
            return nc.tensor.transpose(PS[:, bank, col:col + P], src, ident[:])

        H1, AHT = SC[:, 0:N], SC[:, N:2 * N]
        q2 = [SC[:, N * k:N * (k + 1)] for k in range(4)]
        gate_r, gate_z, gru_t, gru_n = ([SC[:, CH * (2 * k + g):CH * (2 * k + g + 1)] for g in range(2)] for k in range(4))
        gru_s = SC[:, 8 * CH:9 * CH]
        walb, b2b = wt[:, 0, :], wt[:, 1, :]
        gcn_w, w_in = wt[:, 2, :], wt[:, 3:7, :]
        w_out, gcn_b, ones_row = wt[:, 7:9, :], wt[0:1, 9, :], wt[0:1, 10, :]
        at = 0

        def late(words, dt=F32):
            nonlocal at
            at += words
            v = region(at - words, words)
            return v if dt == F32 else v.bitcast(dt)

        xc = late(DI * (N + PAD)).rearrange("p (b t) -> p b t", b=DI)
        u, zg, dt_, du = (late(DI * N).rearrange("p (b t) -> p b t", b=DI) for _ in range(4))
        dbc, rest = late(N), late(N)
        mid, pieces = late(N // 2, BF16), late(N // 2, BF16)
        sel = late(32 * P // 2, BF16).rearrange("p (n m) -> p n m", m=P)
        xps = late(DI * 104).rearrange("p (b c) -> p b c", b=DI)
        w_xp = late(DI * 40).rearrange("p (b c) -> p b c", b=DI)
        w_dt = late(DI * P)
        hs_third = late(2 * CH).rearrange("p (b t) -> p b t", b=DI)
        bb_third = late(CH)
        assert at <= NT * N
        tmp = xc[:, :, 0:N]
        yg = tmp

        def pair(v, c):
            return v[:, :, c * CH:(c + 1) * CH]

        def banks(c):
            b = (4 + 2 * c) % 8
            return PS[:, b:b + 2, :]

        pairs = [SC[:, k * 2 * CH:(k + 1) * 2 * CH].rearrange("p (b t) -> p b t", b=DI) for k in range(7)]
        hs, hc, dbu = pairs[0:2] + [hs_third], pairs[2:4], pairs[4:7]
        bb = [SC[:, (14 + s) * CH:(15 + s) * CH] for s in range(2)] + [bb_third]
        xtiles = X.rearrange("p t f -> p (t f)")

        SPLIT = 1536

        def act_copy(o, i, **kw):
            return nc.scalar.activation(o, i, ACT.Copy, **kw)

        def later_loads(sp):
            sp.dma_start(dgt[:], t["L2_gnn_weight"]).then_inc(w2_in, 16)
            sp.wait_ge(gru_out, 10)
            sp.dma_start(b2b, t["L2_gnn_b"].partition_broadcast(P)).then_inc(b2_in, 16)
            sp.dma_start(gcn_w, t["L3_gnn_gcn_w"]).then_inc(w3_in, 16)
            sp.dma_start(w_in, t["L3_gnn_w_in"].rearrange("k (b m) -> k b m", m=P)).then_inc(w3_in, 16)
            sp.dma_start(w_out, t["L3_gnn_w_out"].rearrange("(b d) m -> d b m", d=P)).then_inc(w3_in, 16)
            sp.dma_start(gcn_b, t["L3_gnn_gcn_b"].rearrange("(o f) -> o f", o=1)).then_inc(w3_in, 16)
            sp.dma_start(ln_g[:], t["L3_gnn_ln_g"].rearrange("(f o) -> f o", o=1)).then_inc(w3_in, 16)
            sp.dma_start(ln_b[:], t["L3_gnn_ln_b"].rearrange("(f o) -> f o", o=1)).then_inc(w3_in, 16)
            sp.dma_start(conv_w[:], t["L3_gnn_conv_w"].rearrange("(b d) k -> d b k", d=P)).then_inc(w3_in, 16)
            sp.dma_start(na[:], t["L3_gnn_A_log"].rearrange("(b d) k -> d b k", d=P)).then_inc(w3_in, 16)
            for name, v in (("conv_b", conv_b), ("D_skip", dskip)):
                sp.dma_start(v[:], t["L3_gnn_" + name].rearrange("(b d) -> d b", d=P)).then_inc(w3_in, 16)
            sp.wait_ge(l3_mm, 4)
            sp.dma_start(w_xp, t["L3_gnn_w_xp"].rearrange("(b d) k -> d b k", d=P)).then_inc(w4_in, 16)
            sp.dma_start(w_dt[96:96 + DTR, :], t["L3_gnn_w_dt"]).then_inc(w4_in, 16)
            sp.dma_start(w_dt[96 + DTR:97 + DTR, :], t["L3_gnn_b_dt"].rearrange("(o f) -> o f", o=1)).then_inc(w4_in, 16)
            out_tiles = out.rearrange("(t p) f -> p t f", p=P)
            for q in range(4):
                sp.wait_ge(x_ready, 12 + q + 1)
                sp.dma_start(out_tiles[:, 4 * q:4 * q + 4, :], X[:, 4 * q:4 * q + 4, :]).then_inc(out_sem, 16)
            sp.wait_ge(out_sem, 64)

        def later_pool(pool):
            pool.wait_ge(b2_in, 16)
            pool.wait_ge(xt_ev, 12)
            nc.gpsimd.tensor_tensor(X, X, b2b.unsqueeze(1).to_broadcast([P, NT, P]), ALU.add).then_inc(x_plus_b, 1)
            pool.wait_ge(l2_x, 4)
            pool.wait_ge(l2_v, 1)
            for jt in range(1, NT):
                pool.wait_ge(q2_ready, jt + 1)
                if jt > 1:
                    pool.wait_ge(q2_added, jt - 1)
                nc.gpsimd.tensor_tensor(XT[:, 0:SPLIT], (q2[0] if jt == 1 else XT)[:, 0:SPLIT], q2[jt % 4][:, 0:SPLIT],
                                        ALU.add).then_inc(q2_added, 1)
            pool.wait_ge(l3_mm, 4)
            nc.gpsimd.memset(xc[:, :, 0:PAD], 0.0).then_inc(pad_ready, 1)
            nc.gpsimd.memset(sel[0:96], 0.0).then_inc(sel_ready, 1)
            for p in range(3):
                pool.wait_ge(sel_ready, p + 1)
                nc.gpsimd.affine_select(out=sel[0:96], in_=sel[0:96], compare_op=ALU.not_equal, fill=1.0,
                                        base=-32 * p, pattern=[[-1, 32], [0, P]],
                                        channel_multiplier=1).then_inc(sel_ready, 1)
            for k in range(STATES * NCH):
                c = k // STATES
                if k % STATES == 0:
                    pool.wait_ge(du_ready, c + 1)
                pool.wait_ge(bb_ready, k + 1)
                if k >= 3:
                    pool.wait_ge(scan_done, k - 2)
                nc.gpsimd.tensor_tensor(dbu[k % 3], du[:, :, c * CH:(c + 1) * CH],
                                        bb[k % 3].unsqueeze(1).to_broadcast([P, DI, CH]),
                                        ALU.mult).then_inc(dbu_ready, 1)
                if k % STATES == 3 and c < NCH - 1:
                    pool.wait_ge(dt_ready, c + 2)
                    pool.wait_ge(dbu_ready, k + 1)
                    nc.gpsimd.tensor_tensor(pair(du, c + 1), pair(dt_, c + 1), pair(u, c + 1),
                                            ALU.mult).then_inc(du_ready, 1)

        def later_act(act):
            def root(k, q):
                act.wait_ge(var_ready, 4 * k + q + 1)
                nc.scalar.activation(rstd[:, 4 * q:4 * q + 4], mv[:, 4 * q:4 * q + 4, 1], ACT.Sqrt,
                                     bias=cst[:, 0:1]).then_inc(std_ready, 1)

            def xt_copy(r, q, bank):
                act.wait_ge(xt_mm, 4 * r + q + 1)
                act_copy(XT[:, q * CH:(q + 1) * CH], PS[:, bank, :]).then_inc(xt_ev, 1)

            def evac(mm, count, dst, q, bank, done):
                act.wait_ge(mm, count)
                act_copy(dst[:, q * CH:(q + 1) * CH], PS[:, bank, :]).then_inc(done, 1)

            for q in range(2):
                xt_copy(0, q, q)
            act.sem_inc(tanh_out, 2)
            with act.Fori(0, NCH) as c:
                for g in range(2):
                    act.wait_ge(gru_mm, c * 2 + g + 1)
                    act.wait_ge(gru_out, c * 2 + g + 1)
                    nc.scalar.activation(gate_r[g], PS[:, 4 * g, :], ACT.Sigmoid, bias=gbs[:, g, 0:1])
                    nc.scalar.activation(gate_z[g], PS[:, 4 * g + 1, :], ACT.Sigmoid, bias=gbs[:, g, 1:2]).then_inc(gate, 1)
                    act.wait_ge(tanh_in, c * 2 + g + 1)
                    nc.scalar.activation(gru_n[g], gru_t[g], ACT.Tanh, bias=gb[:, 2 * g, 2:3]).then_inc(tanh_out, 1)
            root(0, 0)
            xt_copy(1, 0, 4)
            root(0, 1)
            evac(l1_h, 1, H1, 0, 4, l1_hev)
            root(0, 2)
            root(0, 3)
            for q in range(1, 4):
                xt_copy(1, q, 4 + q)
            for q in range(1, 4):
                evac(l1_h, q + 1, H1, q, 4 + q, l1_hev)
            for q in range(4):
                evac(l1_mm, q + 1, AHT, q, q, l1_aev)
            def right_factor(q):
                act.wait_ge(l2_rb, q + 1)
                nc.scalar.activation(es[:, q * CH:(q + 1) * CH], PS[:, (5 + q) if q < 3 else 0, :], ACT.Exp,
                                     scale=0.8).then_inc(l2_rbev, 1)

            root(1, 0)
            for q in range(3):
                xt_copy(2, q, q)
                root(1, q + 1)
            right_factor(0)
            xt_copy(2, 3, 3)
            right_factor(1)
            right_factor(2)
            right_factor(3)
            act.wait_ge(l2_v, 1)
            for dst, src, sc in ((bj, 1, 1.0), (dj, 1, 0.2), (ci, 0, 0.2)):
                nc.scalar.activation(dst[:], PS[:, 4, 0:2 * NT].rearrange("p (t s) -> p t s", s=2)[:, :, src], ACT.Exp,
                                     scale=sc).then_inc(l2_vec, 1)
            act.wait_ge(l2_vec, 3)
            nc.scalar.activation(deg[:], dj[:], ACT.Copy, scale=-1.0).then_inc(l2_vec, 1)
            act.wait_ge(l2_vec, 4)
            act.wait_ge(l2_rbev, 4)
            evac(l2_x, 1, ns, 0, 5, l2_xev)
            for jt in range(1, NT, 2):
                if jt >= 4:
                    act.wait_ge(q2_used, jt - 3)
                    act.wait_ge(q2_added, jt - 4)
                    act.wait_ge(rest_added, jt - 4)
                q = q2[jt % 4]
                nc.scalar.activation(q, es[:], ACT.Relu, scale=bj[:, jt:jt + 1], bias=deg[:, jt:jt + 1]).then_inc(q2_act, 1)
                act.wait_ge(q2_act, jt)
                nc.scalar.activation(q, q, ACT.Identity, bias=dj[:, jt:jt + 1]).then_inc(q2_act, 1)
                if jt == 1:
                    for b in range(1, 4):
                        evac(l2_x, b + 1, ns, b, 5 + b % 3, l2_xev)
            act.wait_ge(q2_added, NT - 4)
            act.wait_ge(rest_added, NT - 4)
            for q in range(4):
                evac(l2_mm, q + 1, q2[0], q, q, l2_aev)
            for q in range(4):
                root(2, q)
            def relu(q):
                act.wait_ge(l3_g, q + 1)
                nc.scalar.activation(H1[:, q * CH:(q + 1) * CH], PS[:, 4 + q, :], ACT.Relu).then_inc(l3_gev, 1)

            def ht_copy(q):
                act.wait_ge(xt_mm, 12 + q + 1)
                nc.scalar.activation(es[:, q * CH:(q + 1) * CH], PS[:, q, :], ACT.Identity, scale=ln_g[:],
                                     bias=ln_b[:]).then_inc(ht_ev, 1)

            def x_branch(c):
                act.wait_ge(xz_mm, c + 1)
                if c == 0:
                    act.wait_ge(pad_ready, 1)
                act_copy(xc[:, :, PAD + c * CH:PAD + (c + 1) * CH], banks(c)).then_inc(xz_ev, 1)

            def z_branch(c):
                act.wait_ge(xz_mm, 4 + c + 1)
                nc.scalar.activation(pair(zg, c), banks(c), ACT.Silu).then_inc(xz_ev, 1)

            def conv_out(c):
                act.wait_ge(conv_done, 2 * (c + 1))
                for b in range(DI):
                    m = nc.scalar.activation(u[:, b, c * CH:(c + 1) * CH], u[:, b, c * CH:(c + 1) * CH], ACT.Silu,
                                             bias=conv_b[:, b:b + 1])
                m.then_inc(u_ready, 1)

            def dbc_copy(c):
                act.wait_ge(dbc_mm, c + 1)
                act.wait_ge(ones_in_dbc, 1)
                act_copy(dbc[0:104, c * CH:(c + 1) * CH], banks(c)[0:104, 0, :]).then_inc(dbc_ev, 1)

            def dt_relu(c):
                act.wait_ge(dt_mm, c + 1)
                nc.scalar.activation(pair(dt_, c), banks(c), ACT.Relu).then_inc(sp_relu, 1)

            for q in range(4):
                evac(l3_mm, q + 1, AHT, q, q, l3_aev)
            relu(0)
            root(3, 0)
            relu(1)
            relu(2)
            root(3, 1)
            ht_copy(0)
            relu(3)
            root(3, 2)
            ht_copy(1)
            root(3, 3)
            ht_copy(2)
            x_branch(0)
            ht_copy(3)
            for c in range(1, 4):
                x_branch(c)
            z_branch(0)
            conv_out(0)
            z_branch(1)
            dbc_copy(0)
            z_branch(2)
            conv_out(1)
            dt_relu(0)
            dbc_copy(1)
            z_branch(3)
            conv_out(2)
            dt_relu(1)
            dbc_copy(2)
            conv_out(3)
            dt_relu(2)
            dbc_copy(3)
            act.wait_ge(w3_in, 16 * 10)
            nc.scalar.activation(na[:], na[:], ACT.Exp).then_inc(na_exp, 1)
            for c in range(NCH):
                if c == 1:
                    dt_relu(NCH - 1)
                act.wait_ge(sp_neg, c + 1)
                nc.scalar.activation(pair(tmp, c), pair(tmp, c), ACT.Exp).then_inc(sp_exp, 1)
            for c in range(NCH):
                act.wait_ge(sp_exp, c + 1)
                nc.scalar.activation(pair(tmp, c), pair(tmp, c), ACT.Ln, bias=1.0).then_inc(sp_ln, 1)
            act.wait_ge(na_ready, 1)

            def copy_b(k):
                act.wait_ge(b_mm, k + 1)
                if k >= 3:
                    act.wait_ge(dbu_ready, k - 2)
                act_copy(bb[k % 3], PS[:, 0, :]).then_inc(bb_ready, 1)

            def decay(k):
                c, n = k // STATES, k % STATES
                if n == 0:
                    act.wait_ge(dt_ready, c + 1)
                if k >= 2:
                    act.wait_ge(scan_done, k - 1)
                for b in range(DI):
                    e = nc.scalar.activation(PS[:, 4 + 2 * (k % 2) + b, :], dt_[:, b, c * CH:(c + 1) * CH], ACT.Exp,
                                             scale=na[:, b, n:n + 1])
                e.then_inc(da_ready, 1)

            def save_state(k):
                act.wait_ge(scan_done, k + 1)
                act_copy(state[:, k % STATES, :], hs[k % 3][:, :, CH - 1]).then_inc(state_saved, 1)

            act.wait_ge(state_zero, 1)
            copy_b(0)
            decay(0)
            copy_b(1)
            copy_b(2)
            for k in range(STATES * NCH):
                if k:
                    save_state(k - 1)
                if k + 1 < STATES * NCH:
                    decay(k + 1)
                if k + 3 < STATES * NCH:
                    copy_b(k + 3)
            for q in range(4):
                root(4, q)

        def later_pe(pe):
            def xt_fill(r, q, bank, src):
                for b in range(4):
                    m = transpose_into(bank, b * P, src[:, 4 * q + b, :])
                m.then_inc(xt_mm, 1)

            def adjacency_product(weights, q, done):
                pe.wait_ge(diag_back, q + 1)
                for jt in range(4 * q, 4 * q + 4):
                    for c in range(NCH):
                        m = nc.tensor.matmul(PS[:, c, :], weights[:, jt, :], AT[:, jt, c * CH:(c + 1) * CH],
                                             start=(jt == 0), stop=(jt == NT - 1))
                        if jt == NT - 1:
                            m.then_inc(done, 1)

            def tiles_product(q, bank, left, right, done):
                for jt in range(4 * q, 4 * q + 4):
                    m = nc.tensor.matmul(PS[:, bank, jt % 4 * P:(jt % 4 + 1) * P], left[:, jt * P:(jt + 1) * P], right,
                                         start=True, stop=True)
                m.then_inc(done, 1)

            pe.wait_ge(x_in, 32)
            pe.wait_ge(es_out, 2 + NT // 2)
            for q in range(4):
                xt_fill(0, q, q, X)
            pe.wait_ge(xt_ev, 4)
            with pe.Fori(0, NCH) as c:
                for g in range(2):
                    pe.wait_ge(tanh_out, c * 2 + g + 1)
                    xs = (ns, es)[g][:, bass.ds(c * CH, CH)]
                    hx = XT[:, bass.ds(c * CH, CH)]
                    wi, wh = 6 * g, 6 * g + 3
                    for gate_no in range(2):
                        nc.tensor.matmul(PS[:, 4 * g + gate_no, :], wt[:, wi + gate_no, :], xs, start=True, stop=False)
                        nc.tensor.matmul(PS[:, 4 * g + gate_no, :], wt[:, wh + gate_no, :], hx, start=False, stop=True)
                    nc.tensor.matmul(PS[:, 4 * g + 2, :], wt[:, wi + 2, :], xs, start=True, stop=True)
                    nc.tensor.matmul(PS[:, 4 * g + 3, :], wt[:, wh + 2, :], hx, start=True, stop=True).then_inc(gru_mm, 1)
            pe.wait_ge(gru_out, 2 + 8)
            nst = ns[:].rearrange("p (t i) -> p t i", i=P)
            for q in range(4):
                for b in range(4):
                    m = transpose_into(4 + q, b * P, nst[:, 4 * q + b, :])
                m.then_inc(st_mm, 1)
            hj = H1.rearrange("p (t f) -> p t f", f=P)

            def x_transpose(q):
                pe.wait_ge(x_ready, q + 1)
                xt_fill(1, q, 4 + q, X)

            def features(q):
                pe.wait_ge(xt_ev, 4 + q + 1)
                tiles_product(q, 4 + q, XT, wt[:, 12, :], l1_h)

            x_transpose(0)
            features(0)
            pe.wait_ge(l1_hev, 1)
            adjacency_product(hj, 0, l1_mm)
            for q in range(1, 4):
                x_transpose(q)
            for q in range(1, 4):
                features(q)
            pe.wait_ge(l1_hev, 4)
            adjacency_product(hj, 1, l1_mm)
            for q in range(4):
                tiles_product(q, 4 + q, XT, wt[:, 13, :], l1_a)
            adjacency_product(hj, 2, l1_mm)
            adjacency_product(hj, 3, l1_mm)
            for q in range(4):
                pe.wait_ge(l1_aev, q + 1)
                tiles_product(q, q, AHT, wt[:, 14, :], l1_b)
            pe.wait_ge(w2_in, 16)
            pe.wait_ge(walb_ready, 1)
            pe.wait_ge(l1_add, 4)
            for q in range(4):
                pe.wait_ge(x_ready, 4 + q + 1)
                xt_fill(2, q, q, X)
                pe.wait_ge(xt_ev, 8 + q + 1)
                nc.tensor.matmul(PS[:, (5 + q) if q < 3 else 0, :], walb, XT[:, q * CH:(q + 1) * CH], start=True,
                                 stop=True).then_inc(l2_rb, 1)
                for jt in range(4 * q, 4 * q + 4):
                    m = nc.tensor.matmul(PS[:, 4, 2 * jt:2 * jt + 2], XT[:, jt * P:(jt + 1) * P], war[:], start=True,
                                         stop=True)
                if q == 3:
                    m.then_inc(l2_v, 1)

            def values(q):
                if q < 3:
                    pe.wait_ge(l2_rbev, q + 1)
                else:
                    pe.wait_ge(l2_xev, 1)
                tiles_product(q, 5 + q % 3, XT, dgt[:], l2_x)

            values(0)
            pe.wait_ge(l2_vec, 3)
            pe.wait_ge(l2_rbev, 4)
            pe.wait_ge(l2_xev, 1)
            x2 = ns[:].rearrange("p (t f) -> p t f", f=P)
            for jt in range(NT):
                pe.wait_ge(q2_ready, jt + 1)
                pe.wait_ge(l2_xev, jt // 4 + 1)
                for c in range(NCH):
                    m = nc.tensor.matmul(PS[:, c, :], x2[:, jt, :], q2[jt % 4][:, c * CH:(c + 1) * CH], start=(jt == 0),
                                         stop=(jt == NT - 1))
                    if jt == NT - 1:
                        m.then_inc(l2_mm, 1)
                if jt < NT - 1:
                    m.then_inc(q2_used, 1)
                if jt == 0:
                    for q in range(1, 4):
                        values(q)
            pe.wait_ge(q2_added, NT - 1)
            pe.wait_ge(rest_added, NT - 1)
            for it in range(NT):
                m = nc.tensor.matmul(PS[:, 4, it:it + 1], XT[:, it * P:(it + 1) * P], cst[:, 1:2], start=True, stop=True)
            m.then_inc(z_mm, 1)
            nt = q2[0].rearrange("p (t i) -> p t i", i=P)
            for q in range(4):
                pe.wait_ge(l2_aev, q + 1)
                if q == 3:
                    pe.wait_ge(sums_read, 1)
                for b in range(4):
                    m = transpose_into(4 + (q + 1) % 4, b * P, nt[:, 4 * q + b, :])
                m.then_inc(l2_b, 1)
            for q in range(4):
                pe.wait_ge(x_ready, 8 + q + 1)
                adjacency_product(X, q, l3_mm)
            pe.wait_ge(w3_in, 16 * 10)
            pe.wait_ge(ones_ready, 1)
            for q in range(4):
                pe.wait_ge(l3_aev, q + 1)
                for it in range(4 * q, 4 * q + 4):
                    o = PS[:, 4 + q, it % 4 * P:(it % 4 + 1) * P]
                    nc.tensor.matmul(o, AHT[:, it * P:(it + 1) * P], gcn_w, start=True, stop=False)
                    m = nc.tensor.matmul(o, ones_row, gcn_b, start=False, stop=True)
                m.then_inc(l3_g, 1)
            def h_fill(q):
                pe.wait_ge(h_ready, q + 1)
                xt_fill(3, q, q, hj)

            def in_product(c, half):
                for b in range(DI):
                    m = nc.tensor.matmul(banks(c)[:, b, :], w_in[:, 2 * half + b, :], es[:, c * CH:(c + 1) * CH],
                                         start=True, stop=True)
                m.then_inc(xz_mm, 1)

            def x_product(c):
                pe.wait_ge(ht_ev, c + 1 if c < 2 else 4)
                if c < 2:
                    pe.wait_ge(l3_gev, 2 * (c + 1))
                in_product(c, 0)

            def z_product(c):
                pe.wait_ge(xz_ev, c + 1)
                in_product(c, 1)

            def dbc_product(c):
                pe.wait_ge(u_ready, c + 1)
                pe.wait_ge(xz_ev, 4 + c + 1)
                for b in range(DI):
                    m = nc.tensor.matmul(banks(c)[0:104, 0, :], xps[:, b, :], u[:, b, c * CH:(c + 1) * CH],
                                         start=(b == 0), stop=(b == 1))
                m.then_inc(dbc_mm, 1)

            def dt_product(c):
                pe.wait_ge(dbc_ev, c + 1)
                for b in range(DI):
                    m = nc.tensor.matmul(banks(c)[:, b, :], w_dt[96:97 + DTR, b * P:(b + 1) * P],
                                         dbc[96:97 + DTR, c * CH:(c + 1) * CH], start=True, stop=True)
                m.then_inc(dt_mm, 1)

            h_fill(0)
            h_fill(1)
            for c in range(NCH):
                x_product(c)
                if c < 2:
                    h_fill(c + 2)
            pe.wait_ge(xps_ready, 1)
            z_product(0)
            z_product(1)
            dbc_product(0)
            z_product(2)
            dt_product(0)
            dbc_product(1)
            z_product(3)
            dt_product(1)
            dbc_product(2)
            dt_product(2)
            dbc_product(3)
            dt_product(3)
            pe.wait_ge(sp_relu, 4)
            pe.wait_ge(sp_neg, 4)
            pe.wait_ge(pieces_ready, NCH)
            pe.wait_ge(sel_ready, 4)

            def add_up(k):
                c, n = k // STATES, k % STATES
                pe.wait_ge(hc_ready, k + 1)
                if n == 0 and c:
                    pe.wait_ge(y_done, c)
                for b in range(DI):
                    m = nc.tensor.matmul(PS[:, 2 + b, :], ident[:], hc[k % 2][:, b, :], start=(n == 0),
                                         stop=(n == STATES - 1))
                m.then_inc(y_mm, 1)

            def spread(k, bank, row, done):
                c = k // STATES
                nc.tensor.matmul(PS[:, bank, :], sel[0:96, row + k % STATES, :], pieces[0:96, c * CH:(c + 1) * CH],
                                 start=True, stop=True).then_inc(done, 1)

            spread(0, 0, 0, b_mm)
            for k in range(1, 3):
                pe.wait_ge(bb_ready, k)
                spread(k, 0, 0, b_mm)
            for k in range(STATES * NCH):
                if k + 3 < STATES * NCH:
                    pe.wait_ge(bb_ready, k + 3)
                    spread(k + 3, 0, 0, b_mm)
                if k:
                    pe.wait_ge(hc_ready, k)
                spread(k, 1, STATES, c_mm)
                if k:
                    add_up(k - 1)

            def out_product(q):
                pe.wait_ge(yg_ready, q + 1)
                pe.wait_ge(scan_done, STATES * NCH - (1 if q < 2 else 0))
                for s in range(4):
                    it = 4 * q + s
                    for b in range(DI):
                        m = nc.tensor.matmul(PS[:, 4 + q, s * P:(s + 1) * P], yg[:, b, it * P:(it + 1) * P], w_out[:, b, :],
                                             start=(b == 0), stop=(b == 1))
                m.then_inc(o_mm, 1)

            out_product(0)
            add_up(STATES * NCH - 1)
            for q in range(1, 4):
                out_product(q)

        def later_dve(dve, link):
            def norm(k, v, ready, residual):
                def scale(q):
                    dve.wait_ge(std_ready, 4 * k + q + 1)
                    link(nc.vector.reciprocal(rstd[:, 4 * q:4 * q + 4], rstd[:, 4 * q:4 * q + 4]))
                    for i in range(4 * q, 4 * q + 4):
                        m = nc.vector.tensor_scalar(v[:, i, :], v[:, i, :], mv[:, i, 0:1], rstd[:, i:i + 1],
                                                    ALU.subtract, ALU.mult)
                    m.then_inc(ready, 1)

                for q in range(4):
                    if q == 1:
                        scale(0)
                    residual(q)
                    if q > 1:
                        scale(q - 1)
                    for i in range(4 * q, 4 * q + 4):
                        m = nc.vector.bn_stats(stats[:, i, :], v[:, i, :])
                    link(m)
                    for i in range(4 * q, 4 * q + 4):
                        m = nc.vector.bn_aggr(mv[:, i, :], stats[:, i, :])
                    m.then_inc(var_ready, 1)
                scale(3)

            def add_scaled(q, bank, factors):
                for i in range(4 * q, 4 * q + 4):
                    m = nc.vector.scalar_tensor_tensor(X[:, i, :], PS[:, bank, i % 4 * P:(i % 4 + 1) * P],
                                                       factors[:, i:i + 1], X[:, i, :], ALU.mult, ALU.add)
                link(m)

            def add_bank(q):
                return nc.vector.tensor_tensor(xtiles[:, q * CH:(q + 1) * CH], PS[:, 4 + q, :],
                                               xtiles[:, q * CH:(q + 1) * CH], ALU.add)

            for q in range(2, 4):
                dve.wait_ge(xt_mm, q + 1)
                nc.vector.tensor_copy(XT[:, q * CH:(q + 1) * CH], PS[:, q, :]).then_inc(xt_ev, 1)
            link(nc.vector.scalar_tensor_tensor(rdeg[:], deg[:], 1.0, dn[:], ALU.add, ALU.add))
            link(nc.vector.reciprocal(rdeg[:], rdeg[:]))
            dve.sem_inc(gru_out, 2)
            with dve.Fori(0, NCH) as c:
                steps = [0]

                def chain(ins):
                    steps[0] += 1
                    ins.then_inc(gru_step, 1)
                    dve.wait_ge(gru_step, c * 7 + steps[0])

                for g in range(2):
                    dve.wait_ge(gate, c * 2 + g + 1)
                    chain(nc.vector.scalar_tensor_tensor(gru_t[g], PS[:, 4 * g + 3, :], gb[:, 2 * g + 1, 2:3], gate_r[g],
                                                         ALU.add, ALU.mult))
                    nc.vector.tensor_tensor(gru_t[g], PS[:, 4 * g + 2, :], gru_t[g], ALU.add).then_inc(tanh_in, 1)
                    dve.wait_ge(tanh_out, c * 2 + g + 3)
                    chain(nc.vector.tensor_tensor(gru_t[g], XT[:, bass.ds(c * CH, CH)], gru_n[g], ALU.subtract))
                    chain(nc.vector.tensor_tensor(gru_t[g], gru_t[g], gate_z[g], ALU.mult))
                    if g == 0:
                        nc.vector.tensor_tensor(gru_s, gru_t[0], gru_n[0], ALU.add).then_inc(gru_out, 1)
                    else:
                        chain(nc.vector.tensor_tensor(gru_t[1], gru_t[1], gru_n[1], ALU.add))
                        nc.vector.tensor_tensor(ns[:, bass.ds(c * CH, CH)], gru_t[1], gru_s, ALU.add).then_inc(gru_out, 1)
                assert steps[0] == 7

            def diagonal_back(b):
                dve.wait_ge(at_in[b], 16)
                for jt in range(4 * b, 4 * b + 4):
                    blk = AT[:, jt, jt * P:(jt + 1) * P]
                    m = nc.vector.scalar_tensor_tensor(blk, ident[:], dn[:, jt:jt + 1], blk, ALU.mult, ALU.add)
                m.then_inc(diag_back, 1)

            def after_gru(q):
                if q == 2:
                    diagonal_back(0)
                dve.wait_ge(st_mm, q + 1)
                add_scaled(q, 4 + q, dn)

            norm(0, X, x_ready, after_gru)
            for b in range(1, 4):
                diagonal_back(b)
            nc.vector.tensor_copy(walb, war[:, 0:1].to_broadcast([P, P])).then_inc(walb_ready, 1)
            nc.vector.memset(ones_row, 1.0).then_inc(ones_ready, 1)
            for q in range(4):
                dve.wait_ge(l1_a, q + 1)
                m = add_bank(q)
                m.then_inc(l1_add, 1)
            dve.wait_ge(l1_add, 4)

            def after_layer1(q):
                dve.wait_ge(l1_b, q + 1)
                add_scaled(q, q, rdeg)

            norm(1, X, x_ready, after_layer1)
            def add_rest(jt):
                if jt == 1:
                    dve.wait_ge(l2_x, 4)
                    dve.wait_ge(l2_v, 1)
                else:
                    dve.wait_ge(rest_added, jt - 1)
                dve.wait_ge(q2_ready, jt + 1)
                nc.vector.tensor_tensor(XT[:, SPLIT:], (q2[0] if jt == 1 else XT)[:, SPLIT:], q2[jt % 4][:, SPLIT:],
                                        ALU.add).then_inc(rest_added, 1)

            dve.wait_ge(l2_vec, 3)
            dve.wait_ge(l2_rbev, 4)
            for jt in range(NT):
                if jt >= 4:
                    dve.wait_ge(q2_used, jt - 3)
                    dve.wait_ge(q2_added, max(jt - 4, 1))
                if jt % 2 == 0:
                    link(nc.vector.tensor_scalar(q2[jt % 4], es[:], bj[:, jt:jt + 1], dj[:, jt:jt + 1], ALU.mult, ALU.max))
                else:
                    dve.wait_ge(q2_act, jt + 1)
                nc.vector.scalar_tensor_tensor(q2[jt % 4], AT[:, jt, :], 0.0, q2[jt % 4], ALU.not_equal,
                                               ALU.mult).then_inc(q2_ready, 1)
                if jt >= 2:
                    add_rest(jt - 1)
            add_rest(NT - 1)
            dve.wait_ge(z_mm, 1)
            nc.vector.tensor_tensor(zi[:], PS[:, 4, 0:NT], ci[:], ALU.mult).then_inc(sums_read, 1)
            dve.wait_ge(sums_read, 1)
            link(nc.vector.tensor_scalar(zi[:], zi[:], 1e-12, None, ALU.max))
            link(nc.vector.reciprocal(zi[:], zi[:]))
            link(nc.vector.tensor_tensor(zi[:], zi[:], ci[:], ALU.mult))
            dve.wait_ge(x_plus_b, 1)

            def after_layer2(q):
                dve.wait_ge(l2_b, q + 1)
                add_scaled(q, 4 + (q + 1) % 4, zi)

            norm(2, X, x_ready, after_layer2)
            dve.wait_ge(l3_mm, 4)
            nc.vector.memset(dbc[96:97 + DTR], 1.0).then_inc(ones_in_dbc, 1)
            norm(3, H1.rearrange("p (t f) -> p t f", f=P), h_ready, lambda q: dve.wait_ge(l3_gev, q + 1))
            dve.wait_ge(w4_in, 16 * 3)
            for k in range(3):
                nc.vector.tensor_copy(xps[:, :, 32 * k:32 * (k + 1)], w_xp[:, :, DTR:DTR + 32])
            nc.vector.tensor_copy(xps[:, :, 96:104], w_xp[:, :, 0:DTR]).then_inc(xps_ready, 1)
            nc.vector.memset(state[:], 0.0).then_inc(state_zero, 1)
            dve.wait_ge(state_zero, 1)
            for c in range(NCH):
                dve.wait_ge(xz_ev, c + 1)
                for k in range(TAPS):
                    for b in range(DI):
                        src = xc[:, b, PAD - 3 + k + c * CH:PAD - 3 + k + (c + 1) * CH]
                        dst = u[:, b, c * CH:(c + 1) * CH]
                        if k == 0:
                            m = nc.vector.tensor_scalar(dst, src, conv_w[:, b, 0:1], None, ALU.mult)
                        else:
                            dve.wait_ge(conv_step, 6 * c + 2 * (k - 1) + b + 1)
                            m = nc.vector.scalar_tensor_tensor(dst, src, conv_w[:, b, k:k + 1], dst, ALU.mult, ALU.add)
                        if k < TAPS - 1:
                            m.then_inc(conv_step, 1)
                        else:
                            m.then_inc(conv_done, 1)
            def negative_abs(c):
                dve.wait_ge(sp_relu, c + 1)
                nc.vector.scalar_tensor_tensor(pair(tmp, c), pair(dt_, c), -2.0, banks(c), ALU.mult,
                                               ALU.add).then_inc(sp_neg, 1)

            def split_rows(c):
                cols = slice(c * CH, (c + 1) * CH)
                dve.wait_ge(dbc_ev, c + 1)
                link(nc.vector.tensor_copy(pieces[0:96, cols], dbc[0:96, cols]))
                link(nc.vector.tensor_tensor(rest[0:96, cols], dbc[0:96, cols], pieces[0:96, cols], ALU.subtract))
                link(nc.vector.tensor_copy(mid[0:96, cols], rest[0:96, cols]))
                nc.vector.tensor_copy(pieces[32:64, cols], mid[32:64, cols])
                link(nc.vector.tensor_tensor(rest[64:96, cols], rest[64:96, cols], mid[64:96, cols], ALU.subtract))
                nc.vector.tensor_copy(pieces[64:96, cols], rest[64:96, cols]).then_inc(pieces_ready, 1)

            negative_abs(0)
            negative_abs(1)
            split_rows(0)
            split_rows(1)
            negative_abs(2)
            split_rows(2)
            negative_abs(3)
            split_rows(3)
            dve.wait_ge(na_exp, 1)
            nc.vector.tensor_scalar(na[:], na[:], -1.0, None, ALU.mult).then_inc(na_ready, 1)
            dve.wait_ge(u_ready, NCH)
            for c in range(NCH):
                dve.wait_ge(sp_ln, c + 1)
                nc.vector.tensor_tensor(pair(dt_, c), pair(dt_, c), pair(tmp, c), ALU.add).then_inc(dt_ready, 1)
                if c == 0:
                    dve.wait_ge(dt_ready, 1)
                    nc.vector.tensor_tensor(pair(du, 0), pair(dt_, 0), pair(u, 0), ALU.mult).then_inc(du_ready, 1)

            def scan(k):
                n = k % STATES
                dve.wait_ge(da_ready, k + 1)
                dve.wait_ge(dbu_ready, k + 1)
                if k >= 3:
                    dve.wait_ge(state_saved, k - 2)
                    dve.wait_ge(hc_ready, k - 2)
                for b in range(DI):
                    m = nc.vector.tensor_tensor_scan(hs[k % 3][:, b, :], PS[:, 4 + 2 * (k % 2) + b, :], dbu[k % 3][:, b, :],
                                                     state[:, n, b:b + 1], ALU.mult, ALU.add)
                m.then_inc(scan_done, 1)

            dve.wait_ge(xz_ev, 8)
            def finish(c):
                cols = slice(c * CH, (c + 1) * CH)
                dve.wait_ge(y_mm, STATES * (c + 1))
                for b in range(DI):
                    m = nc.vector.scalar_tensor_tensor(yg[:, b, cols], u[:, b, cols], dskip[:, b:b + 1], PS[:, 2 + b, :],
                                                       ALU.mult, ALU.add)
                m.then_inc(y_done, 1)
                dve.wait_ge(y_done, c + 1)
                nc.vector.tensor_tensor(yg[:, :, cols], yg[:, :, cols], zg[:, :, cols], ALU.mult).then_inc(yg_ready, 1)

            scan(0)
            for c in range(NCH):
                for n in range(STATES):
                    k = STATES * c + n
                    if k + 1 < STATES * NCH:
                        scan(k + 1)
                    dve.wait_ge(scan_done, k + 1)
                    dve.wait_ge(c_mm, k + 1)
                    if k >= 2:
                        dve.wait_ge(y_mm, k - 1)
                    nc.vector.tensor_tensor(hc[k % 2], PS[:, 1, :].unsqueeze(1).to_broadcast([P, DI, CH]), hs[k % 3],
                                            ALU.mult).then_inc(hc_ready, 1)
                    if c and n == 0:
                        finish(c - 1)
            dve.wait_ge(o_mm, 1)
            add_bank(0).then_inc(res0_added, 1)
            finish(NCH - 1)

            def after_layer3(q):
                if q == 0:
                    dve.wait_ge(res0_added, 1)
                else:
                    dve.wait_ge(o_mm, q + 1)
                    link(add_bank(q))

            norm(4, X, x_ready, after_layer3)

        @block.sync
        def _(sp):
            sp.dma_start(X, x_tiles).then_inc(x_in, 16)
            for s in range(2):
                sp.dma_start(a1[s], adj_tiles[:, 2 * s:2 * s + 2, :]).then_inc(a1_in[s], 16)
            for g in range(NCH):
                for s in range(2):
                    k = 2 * g + s
                    if k + 2 < NT // 2:
                        sp.wait_ge(tr1, 8 * (k + 1))
                        sp.wait_ge(deg_done, 2 * (k + 1))
                        sp.dma_start(a1[s], adj_tiles[:, 2 * k + 4:2 * k + 6, :]).then_inc(a1_in[s], 16)
                sp.wait_ge(ev1a, 8 * (g + 1))
                sp.wait_ge(ev1v, 8 * (g + 1))
                sp.dma_start(at_tiles[:, :, g * CH:(g + 1) * CH], atg[g % 2]).then_inc(at_out[g % 2], 16)
            sp.wait_ge(ah_done, NCH)
            sp.wait_ge(deg_done, NT)
            sp.dma_start(aw[0], adj_tiles[:, 0:2, :]).then_inc(a2_in[0], 16)
            sp.wait_ge(er_ready, 4)
            sp.dma_start(e_dram, e_rows).then_inc(e_out, 16)
            sp.wait_ge(e_out, 16)
            sp.wait_ge(e1_done, NCH)
            for s in range(2):
                sp.wait_ge(at_out[s], 32)
            for h in range(HEADS):
                sp.dma_start(eb[:, 0, h, :], e_dram[h].partition_broadcast(P)).then_inc(ep_in[h], 16)
            sp.dma_start(aw[1], adj_tiles[:, 2:4, :]).then_inc(a2_in[1], 16)
            for h in range(HEADS):
                sp.dma_start(eb[:, 1, h, :], e_dram[HEADS + h].partition_broadcast(P)).then_inc(em_in, 16)
            with sp.Fori(0, NT // 4 - 1) as it:
                for s in range(2):
                    sp.wait_ge(q_done, it * 6 + 3 * (s + 1))
                    sp.dma_start(aw[s], adj_tiles[:, bass.ds(it * 4 + 4 + 2 * s, 2), :]).then_inc(a2_in[s], 16)
            sp.wait_ge(q_done, 3 * (NT // 2 - 1))
            sp.dma_start(X, x_tiles).then_inc(x_in, 16)
            sp.wait_ge(em_in, 16 * HEADS)
            sp.wait_ge(qt_used, 4 + 4 * 48)
            sp.wait_ge(q_done, 3 * NT // 2)
            for s in range(2):
                sp.wait_ge(at_out[s], 32)
            for b in range(NT // 4):
                sp.dma_start(AT[:, 4 * b:4 * b + 4, :], at_tiles[:, 4 * b:4 * b + 4, :]).then_inc(at_in[b], 16)
            later_loads(sp)

        @block.gpsimd
        def _(pool):
            nc.gpsimd.memset(ident[:], 0.0).then_inc(ident_ready, 1)
            nc.gpsimd.memset(cst[:, 0:1], 1e-5).then_inc(ident_ready, 1)
            nc.gpsimd.memset(cst[:, 1:2], 1.0).then_inc(ident_ready, 1)
            nc.gpsimd.memset(smask[:, 0], 0.0).then_inc(ident_ready, 1)
            nc.gpsimd.memset(smask[:, 1], 1.0).then_inc(ident_ready, 1)
            pool.wait_ge(ident_ready, 5)
            nc.gpsimd.affine_select(out=ident[:], in_=ident[:], compare_op=ALU.not_equal, fill=1.0, base=0,
                                    pattern=[[-1, P]], channel_multiplier=1).then_inc(ident_ready, 1)
            nc.gpsimd.memset(comb[0:ROWS], 0.0).then_inc(comb_ready, 1)
            for p in range(3):
                pool.wait_ge(comb_ready, p + 1)
                nc.gpsimd.affine_select(out=comb[0:ROWS], in_=comb[0:ROWS], compare_op=ALU.not_equal, fill=-1.0,
                                        base=-(1 + 3 * p), pattern=[[-9, 2], [-1, 3]],
                                        channel_multiplier=1).then_inc(comb_ready, 1)
            later_pool(pool)

        @block.scalar
        def _(act):
            act.dma_start(raw[:, 16:19, :], t["L0_gnn_gat_W"].rearrange("h k f -> k h f")).then_inc(gat_in, 16)
            act.dma_start(raw[:, 15, :], t["L2_gnn_weight"]).then_inc(gat_in, 16)
            for h in range(HEADS):
                act.dma_start(ga[:, h, :], t["L0_gnn_gat_a"][h].rearrange("(s f) o -> f (s o)", f=P)).then_inc(ga_in, 16)
            act.dma_start(a2[:, 0:1], t["L2_gnn_a_l"].rearrange("(f o) -> f o", o=1)).then_inc(ga_in, 16)
            act.dma_start(a2[:, 1:2], t["L2_gnn_a_r"].rearrange("(f o) -> f o", o=1)).then_inc(ga_in, 16)
            gru = ["edge_Wih", "edge_Whh", "node_Wih", "node_Whh"]
            for k, name in enumerate(gru):
                act.dma_start(raw[:, 3 * k:3 * k + 3, :],
                              t["L0_gnn_" + name].rearrange("(g p) k -> p g k", p=P)).then_inc(raw_in, 16)
            act.dma_start(raw[:, 12, :], t["L1_gnn_neigh_W"]).then_inc(raw_in, 16)
            act.dma_start(raw[:, 13:15, :], t["L1_gnn_lin_W"].rearrange("o (b c) -> o b c", c=P)).then_inc(raw_in, 16)
            for k, name in enumerate(["edge_bih", "edge_bhh", "node_bih", "node_bhh"]):
                act.dma_start(gb[:, k, :], t["L0_gnn_" + name].rearrange("(g p) -> p g", p=P)).then_inc(vec_in, 16)

            act.wait_ge(su_mm, 1)
            nc.scalar.activation(rawt[:], PS[:, 0, :].rearrange("p (b k) -> p b k", k=P), ACT.Copy).then_inc(su_act, 1)
            act.wait_ge(su_mm, 6)
            nc.scalar.activation(wa[:], PS[:, 5, 0:6], ACT.Copy).then_inc(su_act, 1)
            nc.scalar.activation(war[:], PS[:, 5, 6:8], ACT.Copy).then_inc(su_act, 1)

            for g in range(NCH):
                for k in range(4):
                    tile = 4 * g + k
                    act.wait_ge(diag_out, tile + 1)
                    if tile:
                        act.wait_ge(deg_done, tile)
                    if tile == 4:
                        act.wait_ge(su_mm, 23)
                    nc.scalar.activation(XT if g else es[:], a1[tile // 2 % 2][:, tile % 2, :], ACT.Copy,
                                         accum_out=deg[:, tile:tile + 1]).then_inc(deg_done, 1)
                    for b in range(2):
                        act.wait_ge(tr1, 4 * tile + b + 1)
                        if k == 0 and b == 0 and g >= 2:
                            act.wait_ge(at_out[g % 2], 16)
                            act.wait_ge(ah_done, g - 1)
                            act.wait_ge(masks_made, 4 * (g - 1))
                        nc.scalar.activation(atg[g % 2][:, 4 * b:4 * b + 4, k * P:(k + 1) * P],
                                             PS[:, b, :].rearrange("p (t i) -> p t i", i=P),
                                             ACT.Copy).then_inc(ev1a, 1)
                    if g == 0:
                        for jt in range(4 * k, 4 * k + 2):
                            act.wait_ge(su_mm, 7 + jt)
                            nc.scalar.activation(hw[:, jt].rearrange("p h f -> p (h f)"), PS[:, 4 + jt % 4, 0:HEADS * P],
                                                 ACT.Copy).then_inc(su_act, 1)
                if g == 0:
                    for q in range(4):
                        n = 4 if q < 3 else 3
                        act.wait_ge(su_mm, 24 + q)
                        nc.scalar.activation(wt[:, 4 * q:4 * q + n, :],
                                             PS[:, 5 + q % 3, 0:n * P].rearrange("p (b k) -> p b k", k=P),
                                             ACT.Copy).then_inc(su_act, 1)

            for q in range(NCH):
                act.wait_ge(eb_mm, q + 1)
                nc.scalar.activation(qt[q][0:6], PS[0:6, q, :], ACT.Copy, scale=0.2).then_inc(eb_act, 1)

            act.sem_inc(qt_ready, 4)
            act.sem_inc(es_out, 2)

            def softmax(it, k, tiles):
                for j in tiles:
                    s = 2 * (k % 3) + j
                    act.wait_ge(x_done, it * 12 + 2 * k + j + 1)
                    e = nc.scalar.activation(w[s], w[s], ACT.Exp, bias=ymin[:, s:s + 1], scale=-1.0,
                                             accum_out=zsum[:, s:s + 1])
                    if j == 1:
                        e.then_inc(exp_done, 1)

            def evacuate(it, k, parts):
                for v in parts:
                    act.wait_ge(tr2, it * 48 + 8 * k + v + 25)
                    act.wait_ge(qt_used, it * 48 + 8 * k + v + 1)
                    nc.scalar.activation(qt[v % 4], PS[:, v % 4, :], ACT.Copy).then_inc(qt_ready, 1)

            def support(it, pair):
                act.wait_ge(qt_used, it * 48 + 24 * pair + 28)
                act.wait_ge(er_ready, 4)
                nc.scalar.activation(es[:, bass.ds(it * CH + 256 * pair, 256)], PS[:, 4 + pair, 0:256], ACT.Copy,
                                     scale=1.0 / HEADS).then_inc(es_out, 1)

            def four_tiles(it, last):
                for k in range(6):
                    ahead = k < 4 or not last
                    evacuate(it, k, range(0, 3))
                    if k == 3:
                        support(it, 0)
                    if ahead:
                        softmax(it, k + 2, [0])
                    evacuate(it, k, range(3, 6))
                    if ahead:
                        softmax(it, k + 2, [1])
                    evacuate(it, k, range(6, 8))
                support(it, 1)

            for k in range(2):
                softmax(0, k, [0, 1])
            with act.Fori(0, NT // 4 - 1) as it:
                four_tiles(it, False)
            four_tiles(NT // 4 - 1, True)
            later_act(act)

        @block.tensor
        def _(pe):
            pe.wait_ge(ident_ready, 6)
            pe.wait_ge(gat_in, 16 * 2)
            for b in range(4):
                m = transpose_into(0, b * P, raw[:, 15 + b, :])
            m.then_inc(su_mm, 1)
            pe.wait_ge(x_in, 16)
            for q in range(4):
                for b in range(4):
                    m = transpose_into(1 + q, b * P, X[:, 4 * q + b, :])
                m.then_inc(su_mm, 1)
            pe.wait_ge(su_act, 1)
            pe.wait_ge(ga_in, 16 * 5)
            for h in range(HEADS):
                nc.tensor.matmul(PS[:, 5, 2 * h:2 * h + 2], rawt[:, 1 + h, :], ga[:, h, :], start=True, stop=True)
            nc.tensor.matmul(PS[:, 5, 6:8], rawt[:, 0, :], a2[:], start=True, stop=True).then_inc(su_mm, 1)

            def head_features(k):
                for jt in range(4 * k, 4 * k + 4):
                    b = jt % 4
                    if b < 2:
                        pe.wait_ge(su_act, 3 + (2 * k - 1 + b if k else 0))
                    elif k:
                        pe.wait_ge(su_dve, 4 + 2 * k - 3 + b)
                    nc.tensor.matmul(PS[:, 4 + b, 0:HEADS * P], XT[:, jt * P:(jt + 1) * P],
                                     raw[:, 16:19, :].rearrange("p h f -> p (h f)"), start=True,
                                     stop=True).then_inc(su_mm, 1)

            def rest_of_setup():
                pe.wait_ge(su_act, 3 + 7)
                for jt in range(NT):
                    m = nc.tensor.matmul(PS[:, 4, 6 * jt:6 * jt + 6], XT[:, jt * P:(jt + 1) * P], wa[:], start=True,
                                         stop=True)
                m.then_inc(su_mm, 1)
                pe.wait_ge(raw_in, 16 * 6)
                pe.wait_ge(su_act, 3 + 8)
                pe.wait_ge(su_dve, 4 + 8)
                for q in range(4):
                    if q == 3:
                        pe.wait_ge(su_act, 3 + 8 + 1)
                    for b in range(4 if q < 3 else 3):
                        m = transpose_into(5 + q % 3, b * P, raw[:, 4 * q + b, :])
                    m.then_inc(su_mm, 1)

            def products(g, q):
                pe.wait_ge(ev1a, 8 * (g + 1))
                pe.wait_ge(ev1v, 8 * (g + 1))
                if q == 0 and g >= 2:
                    pe.wait_ge(l1_ev, 2 * (g - 1))
                if q == 0 and g == 0:
                    pe.wait_ge(su_act, 15)
                    pe.wait_ge(su_dve, 13)
                for jt in range(4 * q, 4 * q + 4):
                    m = nc.tensor.matmul(PS[:, 4 + g % 2, :], X[:, jt, :], atg[g % 2][:, jt, :],
                                         start=(jt == 0), stop=(jt == NT - 1))
                if q == 3:
                    m.then_inc(ah_done, 1)
                pe.wait_ge(masks_made, 4 * g + q + 1)
                for jt in range(4 * q, 4 * q + 4):
                    for s in range(2):
                        m = nc.tensor.matmul(PS[0:ROWS, 6 + g % 2, :], smask[:, s, jt, 0:ROWS], pm[s][:, jt, :],
                                             start=(jt == 0 and s == 0), stop=(jt == NT - 1 and s == 1))
                if q == 3:
                    m.then_inc(e1_done, 1)

            pe.wait_ge(su_dve, 4)
            for g in range(NCH):
                for k in range(4):
                    tile = 4 * g + k
                    pe.wait_ge(diag_out, tile + 1)
                    for b in range(4):
                        if tile:
                            pe.wait_ge(ev1a if b < 2 else ev1v, 2 * (tile - 1) + b % 2 + 1)
                        for c in range(4):
                            m = transpose_into(b, c * P, a1[tile // 2 % 2][:, tile % 2, (4 * b + c) * P:(4 * b + c + 1) * P])
                        m.then_inc(tr1, 1)
                    if g == 0:
                        head_features(k)
                    else:
                        products(g - 1, k)
                if g == 0:
                    rest_of_setup()
            for k in range(4):
                products(NCH - 1, k)

            pe.wait_ge(comb_ready, 4)
            for q in range(NCH):
                pe.wait_ge(l1_ev, 2 * (q + 1))
                nc.tensor.matmul(PS[0:6, q, :], comb[0:ROWS].rearrange("p s h -> p (s h)"),
                                 es[0:ROWS, q * CH:(q + 1) * CH], start=True, stop=True).then_inc(eb_mm, 1)
            pe.wait_ge(er_ready, 4)

            pe.sem_inc(tr2, 24)
            pe.sem_inc(qt_used, 4)
            with pe.Fori(0, NT // 4) as it:
                for k in range(6):
                    h = k % 3
                    pe.wait_ge(q_done, it * 6 + k + 1)

                    def fill(v):
                        pe.wait_ge(qt_ready, it * 48 + 8 * k + v + 1)
                        for c in range(2):
                            for j in range(2):
                                m = transpose_into(v % 4, 256 * c + j * P, w[2 * (k % 3) + j][:, (2 * v + c) * P:(2 * v + c + 1) * P])
                        m.then_inc(tr2, 1)

                    def multiply(v):
                        pe.wait_ge(qt_ready, it * 48 + 8 * k + v + 5)
                        if h == 0 and v == 0:
                            pe.wait_ge(es_out, it * 2 + k // 3 + 1)
                        for c in range(2):
                            jt = 2 * v + c
                            m = nc.tensor.matmul(PS[:, 4 + k // 3, 0:256], hw[:, jt, h, :], qt[v % 4][:, 256 * c:256 * c + 256],
                                                 start=(h == 0 and jt == 0), stop=(h == 2 and jt == NT - 1))
                        m.then_inc(qt_used, 1)

                    fill(0)
                    fill(1)
                    for v in range(8):
                        if v + 2 < 8:
                            fill(v + 2)
                        multiply(v)
            later_pe(pe)

        @block.vector
        def _(dve):
            count = [0]

            def link(ins):
                count[0] += 1
                ins.then_inc(dch, 1)
                dve.wait_ge(dch, count[0])

            for q in range(4):
                dve.wait_ge(su_mm, 2 + q)
                nc.vector.tensor_copy(XT[:, q * CH:(q + 1) * CH], PS[:, 1 + q, :]).then_inc(su_dve, 1)
            nc.vector.memset(mk[:], 0.0).then_inc(marked, 1)

            def stationary_pieces():
                dve.wait_ge(su_mm, 23)
                link(nc.vector.tensor_copy(upc[:], PS[:, 4, 0:96].rearrange("p (t c) -> p t c", c=6)))
                dve.wait_ge(ident_ready, 6)
                for p in range(3):
                    link(nc.vector.tensor_copy(upb[:], upc[:]))
                    for s in range(2):
                        part = upb[:].rearrange("p t (h s) -> p t h s", s=2)[:, :, :, s]
                        nc.vector.tensor_copy(smask[:, 0, :, 1 + 9 * s + 3 * p:4 + 9 * s + 3 * p], part)
                        last = nc.vector.tensor_copy(smask[:, 1, :, 10 - 9 * s + 3 * p:13 - 9 * s + 3 * p], part)
                    if p < 2:
                        link(last)
                        link(nc.vector.tensor_tensor(upc[:], upc[:], upb[:], ALU.subtract))
                last.then_inc(su_dve, 1)
                dve.wait_ge(vec_in, 16 * 4)
                for g in range(2):
                    nc.vector.tensor_tensor(gbs[:, g, :], gb[:, 2 * g, 0:2], gb[:, 2 * g + 1, 0:2], ALU.add)

            def masks(g, q):
                if q == 0:
                    if g == 0:
                        dve.wait_ge(su_mm, 27)
                        dve.wait_ge(su_dve, 13)
                    dve.wait_ge(ev1a, 8 * (g + 1))
                    dve.wait_ge(ev1v, 8 * (g + 1))
                    if g:
                        dve.wait_ge(e1_done, g)
                src = atg[g % 2][:, 4 * q:4 * q + 4, :]
                nc.vector.tensor_scalar(pm[0][:, 4 * q:4 * q + 4, :], src, 0.0, None, ALU.is_gt)
                nc.vector.tensor_scalar(pm[1][:, 4 * q:4 * q + 4, :], src, 0.0, None, ALU.is_lt).then_inc(masks_made, 1)

            def rows_out(g):
                dve.wait_ge(ah_done, g + 1)
                nc.vector.tensor_copy(ns[:, g * CH:(g + 1) * CH], PS[:, 4 + g % 2, :]).then_inc(l1_ev, 1)
                dve.wait_ge(e1_done, g + 1)
                dve.wait_ge(deg_done, 4)
                nc.vector.tensor_copy(es[0:ROWS, g * CH:(g + 1) * CH], PS[0:ROWS, 6 + g % 2, :]).then_inc(l1_ev, 1)

            for g in range(NCH):
                for k in range(4):
                    tile = 4 * g + k
                    blk = a1[tile // 2 % 2][:, tile % 2, tile * P:(tile + 1) * P]
                    dve.wait_ge(a1_in[tile // 2 % 2], 16 * (tile // 4 + 1))
                    if tile:
                        dve.wait_ge(diag_out, tile)
                    link(nc.vector.tensor_tensor(dgt[:], blk, ident[:], ALU.mult))
                    nc.vector.reduce_sum(dn[:, tile:tile + 1], dgt[:], AXL.X)
                    nc.vector.tensor_tensor(blk, blk, dgt[:], ALU.subtract).then_inc(diag_out, 1)
                    if g >= 1:
                        masks(g - 1, k)
                    for b in range(2, 4):
                        dve.wait_ge(tr1, 4 * tile + b + 1)
                        if k == 0 and b == 2 and g >= 2:
                            dve.wait_ge(at_out[g % 2], 16)
                            dve.wait_ge(ah_done, g - 1)
                        nc.vector.tensor_copy(atg[g % 2][:, 4 * b:4 * b + 4, k * P:(k + 1) * P],
                                              PS[:, b, :].rearrange("p (t i) -> p t i", i=P)).then_inc(ev1v, 1)
                    if g == 0:
                        for jt in range(4 * k + 2, 4 * k + 4):
                            dve.wait_ge(su_mm, 7 + jt)
                            nc.vector.tensor_copy(hw[:, jt].rearrange("p h f -> p (h f)"),
                                                  PS[:, 4 + jt % 4, 0:HEADS * P]).then_inc(su_dve, 1)
                if g == 0:
                    stationary_pieces()
                if g >= 1:
                    rows_out(g - 1)
            for k in range(4):
                masks(NCH - 1, k)
            rows_out(NCH - 1)

            dve.wait_ge(deg_done, NT)
            for q in range(NCH):
                dve.wait_ge(eb_act, q + 1)
                nc.vector.tensor_tensor(e_rows[:, q * CH:(q + 1) * CH], PS[0:6, q, :], qt[q][0:6],
                                        ALU.min).then_inc(er_ready, 1)
            dve.wait_ge(l1_ev, 2 * NCH)
            link(nc.vector.tensor_reduce(flag[:], es[0:1, :], AXL.X, ALU.max))
            negative = dve.value_load(flag[:].bitcast(I32), min_val=0, max_val=0x7fffffff)

            def attention(signed):
                steps = [0]

                def chain(it, ins):
                    steps[0] += 1
                    ins.then_inc(signed_step, 1)
                    dve.wait_ge(signed_step, it * 84 + steps[0])

                def edge_mask(it, k, j):
                    pair = k // 3 % 2
                    tile = it * 4 + 2 * (k // 3) + j
                    if j == 0:
                        dve.wait_ge(a2_in[pair], it * 16 + 16 * (k // 6) + 16)
                    blk = aw[pair][:, j, bass.ds(tile * P, P)]
                    nc.vector.tensor_tensor(blk, blk, dgt[:], ALU.mult).then_inc(offd_done, 1)
                    dve.wait_ge(offd_done, tile + 1)
                    nc.vector.tensor_scalar(bm[2 * pair + j], aw[pair][:, j, :], 0.0, MASKED, ALU.is_le,
                                            ALU.mult).then_inc(bm_done, 1)
                    dve.wait_ge(bm_done, tile + 1)

                def logits(it, k, j):
                    pair, h = k // 3 % 2, k % 3
                    s = 2 * h + j
                    if h == 0 and k:
                        edge_mask(it, k, j)
                    dve.wait_ge(ep_in[h], 16)
                    if signed:
                        dve.wait_ge(em_in, 16 * HEADS)
                    dve.wait_ge(tr2, it * 48 + 8 * k + 8)
                    dve.wait_ge(marked, it * 12 + 2 * k + j + 1)
                    nc.vector.memset(mk[:], 0.0).then_inc(marked, 1)
                    if not signed:
                        m = nc.vector.tensor_tensor_reduce(
                            out=w[s], in0=bm[2 * pair + j], in1=eb[:, 0, h, :], scale=1.0, scalar=3.0e38,
                            op0=ALU.add, op1=ALU.min, accum_out=ymin[:, s:s + 1])
                    else:
                        a = aw[pair][:, j, :]
                        chain(it, nc.vector.tensor_tensor(w[s], bm[2 * pair + j], eb[:, 0, h, :], ALU.add))
                        for half in range(2):
                            cols = slice(half * N // 2, (half + 1) * N // 2)
                            spare = PS[:, 6:8, :].rearrange("p b c -> p (b c)")
                            chain(it, nc.vector.tensor_scalar(spare, a[:, cols], 0.0, MASKED, ALU.is_ge, ALU.mult))
                            chain(it, nc.vector.tensor_tensor(spare, spare, eb[:, 1, h, cols], ALU.add))
                            chain(it, nc.vector.tensor_tensor(w[s][:, cols], spare, w[s][:, cols], ALU.min))
                        m = nc.vector.tensor_reduce(ymin[:, s:s + 1], w[s], AXL.X, ALU.min)
                    m.then_inc(x_done, 1)

                def weights(it, k, j):
                    pair, h = k // 3, k % 3
                    if j == 0:
                        dve.wait_ge(exp_done, it * 6 + k + 1)
                        nc.vector.reciprocal(rz[:, 2 * h:2 * h + 2], zsum[:, 2 * h:2 * h + 2]).then_inc(rz_done, 1)
                        dve.wait_ge(rz_done, it * 6 + k + 1)
                    s = 2 * h + j
                    m = nc.vector.scalar_tensor_tensor(w[s], w[s], rz[:, s:s + 1], aw[pair][:, j, :], ALU.mult, ALU.mult)
                    if j == 1:
                        m.then_inc(q_done, 1)

                def four_tiles(it, last):
                    for k in range(6):
                        for j in range(2):
                            if k < 5 or not last:
                                logits(it, k + 1, j)
                            weights(it, k, j)

                for j in range(2):
                    edge_mask(0, 0, j)
                for j in range(2):
                    logits(0, 0, j)
                with dve.Fori(0, NT // 4 - 1) as it:
                    four_tiles(it, False)
                steps[0] -= 84
                four_tiles(NT // 4 - 1, True)

            link(nc.vector.tensor_scalar(dgt[:], ident[:], -1.0, 1.0, ALU.mult, ALU.add))
            with dve.If(negative != 0):
                attention(True)
            with dve.Else():
                attention(False)
            later_dve(dve, link)


_INS = ["x", "adj", "L0_gnn_gat_W", "L0_gnn_gat_a", "L0_gnn_edge_Wih", "L0_gnn_edge_Whh", "L0_gnn_edge_bih",
        "L0_gnn_edge_bhh", "L0_gnn_node_Wih", "L0_gnn_node_Whh", "L0_gnn_node_bih", "L0_gnn_node_bhh",
        "L1_gnn_neigh_W", "L1_gnn_lin_W", "L2_gnn_weight", "L2_gnn_a_l", "L2_gnn_a_r", "L2_gnn_b", "L3_gnn_gcn_w",
        "L3_gnn_gcn_b", "L3_gnn_ln_g", "L3_gnn_ln_b", "L3_gnn_w_in", "L3_gnn_conv_w", "L3_gnn_conv_b", "L3_gnn_w_xp",
        "L3_gnn_w_dt", "L3_gnn_b_dt", "L3_gnn_A_log", "L3_gnn_D_skip", "L3_gnn_w_out"]


def kernel(**inputs):
    import numpy as _np
    import concourse.bacc as _bacc
    from concourse import mybir as _mybir
    from concourse.bass_utils import run_bass_kernel_spmd as _run

    nc = _bacc.Bacc("TRN2", target_bir_lowering=False, num_devices=1)
    arrays, aps = {}, {}
    for name in _INS:
        a = _np.ascontiguousarray(inputs[name])
        arrays[f"in_{name}"] = a
        aps[name] = nc.dram_tensor(f"in_{name}", a.shape, _mybir.dt.from_np(a.dtype), kind="ExternalInput").ap()
    out = nc.dram_tensor("out_x", (N, P), F32, kind="ExternalOutput").ap()
    gnn_program(nc, aps, out)
    r = _run(nc, [arrays], core_ids=[0])
    return r.results[0]["out_x"]
```
